# Optimizing a Trainium2 kernel written in Bass

```python
import numpy as np
import jax
import jax.numpy as jnp

def _softmax(x, axis=-1):
    return jax.nn.softmax(x, axis=axis)

def _gelu(x):
    return jax.nn.gelu(x, approximate=True)

def _silu(x):
    return jax.nn.silu(x)

def _sigmoid(x):
    return jax.nn.sigmoid(x)

def _layernorm(x, axis=-1, eps=1e-05):
    m = jnp.mean(x, axis=axis, keepdims=True)
    v = jnp.var(x, axis=axis, keepdims=True)
    return (x - m) / jnp.sqrt(v + eps)

def _scatter_add(tgt, idx, src, axis=0):
    return tgt.at[idx].add(src)

def _segment_sum(src, seg, n):
    return jax.ops.segment_sum(src, seg, n)
kernel_name = 'mk_decoder_preln_d4_seqx_r8_9e10e4'

def setup_inputs(seed: int=0):
    np.random.seed(seed)
    _w = jnp.asarray

    def _rec_inputs():
        import jax
        import jax.numpy as jnp
        _rk = jax.random.key(seed)
        x = -0.000125 + 0.9999 * jax.random.normal(jax.random.fold_in(_rk, 1), (4, 256, 128), jnp.float32)
        _lenS = 256 - jax.random.randint(jax.random.fold_in(_rk, 7), (4,), 0, max(1, 256 // 4) + 1, jnp.int32)
        _lenS2 = 512 - jax.random.randint(jax.random.fold_in(_rk, 8), (4,), 0, max(1, 512 // 4) + 1, jnp.int32)
        _ctx_768P = jax.random.normal(jax.random.fold_in(_rk, 11), (4, 16, 96), jnp.float32)
        _ctx_768c = jax.random.dirichlet(jax.random.fold_in(_rk, 511), 0.3 * jnp.ones((16,), jnp.float32), (4, 512))
        _ctx_768t = jnp.einsum('bsk,bkd->bsd', _ctx_768c, _ctx_768P)
        _ctx_768t = _ctx_768t * jax.lax.rsqrt(jnp.mean(jnp.square(_ctx_768t)) + 1e-12) * 0.953939
        ctx_768 = 0.00243539 + 0.99952 * (_ctx_768t + 0.3 * jax.random.normal(jax.random.fold_in(_rk, 611), (4, 512, 96), jnp.float32))
        _validS = jnp.arange(256)[None, :] < _lenS[:, None]
        _validS2 = jnp.arange(512)[None, :] < _lenS2[:, None]
        _causal = jnp.tril(jnp.ones((256, 256), dtype=bool))
        mask_BxS2_bk0 = jnp.logical_not(jnp.broadcast_to(_validS2[:, :], (4, 512)))
        return (x, ctx_768, mask_BxS2_bk0)
    x, ctx_768, mask_BxS2_bk0 = _rec_inputs()

    def _L0_attn_setup():
        import jax, jax.numpy as jnp
        import numpy as np
        B, N, DIM, HID = (4, 256, 128, 128)
        key = jax.random.key(seed)
        k1, k2, k3 = jax.random.split(key, 3)
        x = jax.random.normal(k1, (B, N, DIM), dtype=jnp.float32)
        W = jax.random.normal(k2, (DIM, 3 * HID), dtype=jnp.float32) * (1.0 / np.sqrt(DIM))
        b = jax.random.normal(k3, (3 * HID,), dtype=jnp.float32) * 0.01
        return {'x': x, 'W': W, 'b': b}
    _L0_attn_all = _L0_attn_setup()
    _L0_attn_in = {k: v for k, v in _L0_attn_all.items() if k in ('W', 'b')}
    del _L0_attn_all

    def _L0_xattn_setup():
        import jax, jax.numpy as jnp
        import numpy as np
        HEADS = 16
        DIM_HEAD = 64
        RANK = 32
        LORA_W = 1.0
        IPA_SCALE = 1.0
        IPA_TOKENS = 4
        SCALE = DIM_HEAD ** (-0.5)

        def _split_heads(t):
            b, n, _ = t.shape
            return t.reshape(b, n, HEADS, DIM_HEAD).transpose(0, 2, 1, 3)

        def _merge_heads(t):
            b, h, n, d = t.shape
            return t.transpose(0, 2, 1, 3).reshape(b, n, h * d)

        def _attention(q_in, k_in, v_in):
            q = _split_heads(q_in)
            k = _split_heads(k_in)
            v = _split_heads(v_in)
            s = jnp.einsum('bhid,bhjd->bhij', q, k) * SCALE
            p = jax.nn.softmax(s, axis=-1)
            o = jnp.einsum('bhij,bhjd->bhid', p, v)
            return _merge_heads(o)

        def _lora(t, down, up, alpha):
            return t @ down @ up * (LORA_W * alpha[0] / RANK)
        key = jax.random.key(seed)
        ks = jax.random.split(key, 20)
        B, N, QD, CD, ID = (8, 512, 128, 96, HEADS * DIM_HEAD)
        CTX = 77 + IPA_TOKENS
        s = 0.02
        return {'x': jax.random.normal(ks[0], (B, N, QD), jnp.float32), 'context': jax.random.normal(ks[1], (B, CTX, CD), jnp.float32), 'Wq': jax.random.normal(ks[2], (QD, ID), jnp.float32) * s, 'Wk': jax.random.normal(ks[3], (CD, ID), jnp.float32) * s, 'Wv': jax.random.normal(ks[4], (CD, ID), jnp.float32) * s, 'Wo': jax.random.normal(ks[5], (ID, QD), jnp.float32) * s, 'bo': jnp.zeros((QD,), jnp.float32), 'q_down': jax.random.normal(ks[6], (QD, RANK), jnp.float32) * s, 'q_up': jax.random.normal(ks[7], (RANK, ID), jnp.float32) * s, 'q_alpha': jnp.ones((1,), jnp.float32) * RANK, 'k_down': jax.random.normal(ks[8], (CD, RANK), jnp.float32) * s, 'k_up': jax.random.normal(ks[9], (RANK, ID), jnp.float32) * s, 'k_alpha': jnp.ones((1,), jnp.float32) * RANK, 'v_down': jax.random.normal(ks[10], (CD, RANK), jnp.float32) * s, 'v_up': jax.random.normal(ks[11], (RANK, ID), jnp.float32) * s, 'v_alpha': jnp.ones((1,), jnp.float32) * RANK, 'o_down': jax.random.normal(ks[12], (ID, RANK), jnp.float32) * s, 'o_up': jax.random.normal(ks[13], (RANK, QD), jnp.float32) * s, 'o_alpha': jnp.ones((1,), jnp.float32) * RANK, 'Wk_ipa': jax.random.normal(ks[14], (CD, ID), jnp.float32) * s, 'Wv_ipa': jax.random.normal(ks[15], (CD, ID), jnp.float32) * s}
    _L0_xattn_all = _L0_xattn_setup()
    _L0_xattn_in = {k: v for k, v in _L0_xattn_all.items() if k in ('Wq', 'Wk', 'Wv', 'Wo', 'bo', 'q_down', 'q_up', 'q_alpha', 'k_down', 'k_up', 'k_alpha', 'v_down', 'v_up', 'v_alpha', 'o_down', 'o_up', 'o_alpha', 'Wk_ipa', 'Wv_ipa')}
    del _L0_xattn_all

    def _L0_ffn_setup():
        import jax, jax.numpy as jnp
        import numpy as np
        HID = 128
        NH = 16
        NKV = 4
        HD = HID // NH
        E = 8
        TOPK = 2
        FFN = 256
        EPS = 1e-05
        THETA = 10000.0

        def _rmsnorm(x, w):
            var = jnp.mean(x * x, axis=-1, keepdims=True)
            return x * jax.lax.rsqrt(var + EPS) * w

        def _rope_tables(S):
            inv_freq = 1.0 / THETA ** (jnp.arange(0, HD, 2, dtype=jnp.float32) / HD)
            freqs = jnp.arange(S, dtype=jnp.float32)[:, None] * inv_freq[None, :]
            emb = jnp.concatenate([freqs, freqs], axis=-1)
            return (jnp.cos(emb), jnp.sin(emb))

        def _apply_rope(t, cos, sin):
            t1, t2 = jnp.split(t, 2, axis=-1)
            rot = jnp.concatenate([-t2, t1], axis=-1)
            return t * cos[None, :, None, :] + rot * sin[None, :, None, :]
        key = jax.random.key(seed)
        ks = jax.random.split(key, 6)
        B, S = (1, 256)
        x = jax.random.normal(ks[0], (B, S, HID), dtype=jnp.float32)
        wqkv = jax.random.normal(ks[1], ((NH + 2 * NKV) * HD, HID), dtype=jnp.float32) * 0.02
        wo = jax.random.normal(ks[2], (HID, NH * HD), dtype=jnp.float32) * 0.02
        gate_w = jax.random.normal(ks[3], (E, HID), dtype=jnp.float32) * 0.02
        w13 = jax.random.normal(ks[4], (E, 2 * FFN, HID), dtype=jnp.float32) * 0.02
        w2 = jax.random.normal(ks[5], (E, HID, FFN), dtype=jnp.float32) * 0.02
        return {'x': x, 'ln1_w': jnp.ones((HID,), jnp.float32), 'ln2_w': jnp.ones((HID,), jnp.float32), 'wqkv': wqkv, 'wo': wo, 'gate_w': gate_w, 'w13': w13, 'w2': w2}
    _L0_ffn_all = _L0_ffn_setup()
    _L0_ffn_in = {k: v for k, v in _L0_ffn_all.items() if k in ('ln1_w', 'ln2_w', 'wqkv', 'wo', 'gate_w', 'w13', 'w2')}
    del _L0_ffn_all

    def _L1_attn_setup():
        import jax, jax.numpy as jnp
        import numpy as np
        D_MODEL = 128
        NHEAD = 16
        WIN = 128
        key = jax.random.key(seed)
        k0, k1, k2 = jax.random.split(key, 3)
        B, S = (4, 512)
        x = jax.random.normal(k0, (B, S, D_MODEL), dtype=jnp.float32)
        Wqkv = jax.random.normal(k1, (D_MODEL, 3 * D_MODEL), dtype=jnp.float32) * 0.02
        bqkv = jnp.zeros((3 * D_MODEL,), dtype=jnp.float32)
        Wout = jax.random.normal(k2, (D_MODEL, D_MODEL), dtype=jnp.float32) * 0.02
        bout = jnp.zeros((D_MODEL,), dtype=jnp.float32)
        return {'x': x, 'Wqkv': Wqkv, 'bqkv': bqkv, 'Wout': Wout, 'bout': bout}
    _L1_attn_all = _L1_attn_setup()
    _L1_attn_in = {k: v for k, v in _L1_attn_all.items() if k in ('Wqkv', 'bqkv', 'Wout', 'bout')}
    del _L1_attn_all

    def _L1_xattn_setup():
        import jax, jax.numpy as jnp
        import numpy as np
        N_HEADS = 16
        D_EMBED = 128
        D_CROSS = 96
        D_HEAD = D_EMBED // N_HEADS
        key = jax.random.key(seed)
        ks = jax.random.split(key, 10)
        B, SQ, SKV = (8, 512, 77)
        s_e = 1.0 / np.sqrt(D_EMBED)
        s_c = 1.0 / np.sqrt(D_CROSS)
        return {'x': jax.random.normal(ks[0], (B, SQ, D_EMBED), jnp.float32), 'y': jax.random.normal(ks[1], (B, SKV, D_CROSS), jnp.float32), 'wq': jax.random.normal(ks[2], (D_EMBED, D_EMBED), jnp.float32) * s_e, 'bq': jnp.zeros((D_EMBED,), jnp.float32), 'wk': jax.random.normal(ks[3], (D_CROSS, D_EMBED), jnp.float32) * s_c, 'bk': jnp.zeros((D_EMBED,), jnp.float32), 'wv': jax.random.normal(ks[4], (D_CROSS, D_EMBED), jnp.float32) * s_c, 'bv': jnp.zeros((D_EMBED,), jnp.float32), 'wo': jax.random.normal(ks[5], (D_EMBED, D_EMBED), jnp.float32) * s_e, 'bo': jnp.zeros((D_EMBED,), jnp.float32)}
    _L1_xattn_all = _L1_xattn_setup()
    _L1_xattn_in = {k: v for k, v in _L1_xattn_all.items() if k in ('wq', 'bq', 'wk', 'bk', 'wv', 'bv', 'wo', 'bo')}
    del _L1_xattn_all

    def _L1_ffn_setup():
        import jax, jax.numpy as jnp
        import numpy as np
        DIM = 128

        def _reference_tuple_inner(x, W_r, W_k, W_v, mu_r, mu_k):
            B, T, C = x.shape
            x_prev = jnp.concatenate([jnp.zeros((B, 1, C), x.dtype), x[:, :-1, :]], axis=1)
            xr = mu_r * x + (1.0 - mu_r) * x_prev
            xk = mu_k * x + (1.0 - mu_k) * x_prev
            r = jax.nn.sigmoid(jnp.einsum('btc,dc->btd', xr, W_r))
            k = jnp.einsum('btc,dc->btd', xk, W_k)
            k_act = jnp.square(jax.nn.relu(k))
            out = r * jnp.einsum('btc,dc->btd', k_act, W_v)
            new_state = x[:, -1, :]
            return (out, new_state)
        key = jax.random.key(seed)
        ks = jax.random.split(key, 6)
        B, T, C = (8, 256, DIM)
        x = jax.random.normal(ks[0], (B, T, C), dtype=jnp.float32)
        s = 1.0 / np.sqrt(C)
        W_r = jax.random.uniform(ks[1], (C, C), jnp.float32, -s, s)
        W_k = jax.random.uniform(ks[2], (C, C), jnp.float32, -s, s)
        W_v = jax.random.uniform(ks[3], (C, C), jnp.float32, -s, s)
        mu_r = jax.random.uniform(ks[4], (C,), jnp.float32)
        mu_k = jax.random.uniform(ks[5], (C,), jnp.float32)
        return {'x': x, 'W_r': W_r, 'W_k': W_k, 'W_v': W_v, 'mu_r': mu_r, 'mu_k': mu_k}
    _L1_ffn_all = _L1_ffn_setup()
    _L1_ffn_in = {k: v for k, v in _L1_ffn_all.items() if k in ('W_r', 'W_k', 'W_v', 'mu_r', 'mu_k')}
    del _L1_ffn_all

    def _L2_attn_setup():
        import jax, jax.numpy as jnp
        import numpy as np
        NUM_HEADS, D_HEAD, D_MODEL, N_CTX = (16, 64, 128, 256)
        BATCH, SEQ = (4, 256)
        key = jax.random.key(seed)
        kx, kq, kk, kv, ko = jax.random.split(key, 5)
        x = jax.random.normal(kx, (BATCH, SEQ, D_MODEL), dtype=jnp.float32)
        Q = jax.random.normal(kq, (NUM_HEADS, D_HEAD, D_MODEL), dtype=jnp.float32) / np.sqrt(D_MODEL)
        K = jax.random.normal(kk, (NUM_HEADS, D_HEAD, D_MODEL), dtype=jnp.float32) / np.sqrt(D_MODEL)
        V = jax.random.normal(kv, (NUM_HEADS, D_HEAD, D_MODEL), dtype=jnp.float32) / np.sqrt(D_MODEL)
        O = jax.random.normal(ko, (D_MODEL, NUM_HEADS * D_HEAD), dtype=jnp.float32) / np.sqrt(NUM_HEADS * D_HEAD)
        return {'x': x, 'Q': Q, 'K': K, 'V': V, 'O': O}
    _L2_attn_all = _L2_attn_setup()
    _L2_attn_in = {k: v for k, v in _L2_attn_all.items() if k in ('Q', 'K', 'V', 'O')}
    del _L2_attn_all

    def _L2_xattn_setup():
        import jax, jax.numpy as jnp
        import numpy as np
        DIM_IN, DIM_LAT, DIM_HEAD = (96, 128, 64)
        INNER = max(DIM_LAT, DIM_IN)
        HEADS = INNER // DIM_HEAD
        SCALE = DIM_HEAD ** (-0.5)
        RMS_EPS = 1e-08
        LN_EPS = 1e-05

        def layernorm(x, g, b):
            mu = jnp.mean(x, axis=-1, keepdims=True)
            var = jnp.mean((x - mu) ** 2, axis=-1, keepdims=True)
            return (x - mu) * jax.lax.rsqrt(var + LN_EPS) * g + b

        def rmsnorm(x, gamma):
            norm = jnp.sqrt(jnp.sum(x * x, axis=-1, keepdims=True)) * x.shape[-1] ** (-0.5)
            return x / jnp.maximum(norm, RMS_EPS) * gamma
        key = jax.random.key(seed)
        ks = jax.random.split(key, 12)
        b, n, m = (4, 512, 64)
        x = jax.random.normal(ks[0], (b, n, DIM_IN), jnp.float32)
        latents = jax.random.normal(ks[1], (b, m, DIM_LAT), jnp.float32)
        mask = jax.random.randint(ks[2], (b, n), 0, 2).astype(bool)
        s = lambda k, sh, fan: jax.random.normal(k, sh, jnp.float32) * fan ** (-0.5)
        return {'x': x, 'latents': latents, 'mask': mask, 'ln_x_g': jnp.ones((DIM_IN,), jnp.float32), 'ln_x_b': jnp.zeros((DIM_IN,), jnp.float32), 'ln_l_g': jnp.ones((DIM_LAT,), jnp.float32), 'ln_l_b': jnp.zeros((DIM_LAT,), jnp.float32), 'qn_g': jnp.ones((DIM_HEAD,), jnp.float32), 'kn_g': jnp.ones((DIM_HEAD,), jnp.float32), 'Wq': s(ks[3], (INNER, DIM_LAT), DIM_LAT), 'Wkv': s(ks[4], (2 * INNER, DIM_IN), DIM_IN), 'Wlkv': s(ks[5], (2 * INNER, DIM_LAT), DIM_LAT), 'Wo': s(ks[6], (DIM_LAT, INNER), INNER), 'bo': jnp.zeros((DIM_LAT,), jnp.float32)}
    _L2_xattn_all = _L2_xattn_setup()
    _L2_xattn_in = {k: v for k, v in _L2_xattn_all.items() if k in ('ln_x_g', 'ln_x_b', 'ln_l_g', 'ln_l_b', 'qn_g', 'kn_g', 'Wq', 'Wkv', 'Wlkv', 'Wo', 'bo')}
    del _L2_xattn_all

    def _L2_ffn_setup():
        import jax, jax.numpy as jnp
        import numpy as np
        BLOCK = 16
        _GRID = jnp.array([0.0, 0.5, 1.0, 1.5, 2.0, 3.0, 4.0, 6.0], dtype=jnp.float32)
        _MID = jnp.array([0.25, 0.75, 1.25, 1.75, 2.5, 3.5, 5.0], dtype=jnp.float32)

        def fp4_quant_dequant(x):
            shape = x.shape
            xb = x.reshape(shape[:-1] + (shape[-1] // BLOCK, BLOCK))
            scale = jnp.max(jnp.abs(xb), axis=-1, keepdims=True) / 6.0
            scale = jnp.maximum(scale, jnp.float32(1e-12))
            xn = xb / scale
            idx = jnp.searchsorted(_MID, jnp.abs(xn))
            q = _GRID[idx] * jnp.sign(xn) * scale
            return q.reshape(shape)

        def fp4_linear(x, w):
            xq = fp4_quant_dequant(x)
            wq = fp4_quant_dequant(w)
            return jnp.einsum('bsk,nk->bsn', xq, wq)
        key = jax.random.key(seed)
        k1, k2, k3, k4 = jax.random.split(key, 4)
        H, I = (128, 352)
        x = jax.random.normal(k1, (4, 512, H), dtype=jnp.float32)
        w_gate = jax.random.normal(k2, (I, H), dtype=jnp.float32) * 0.02
        w_up = jax.random.normal(k3, (I, H), dtype=jnp.float32) * 0.02
        w_down = jax.random.normal(k4, (H, I), dtype=jnp.float32) * 0.02
        return {'x': x, 'w_gate': w_gate, 'w_up': w_up, 'w_down': w_down}
    _L2_ffn_all = _L2_ffn_setup()
    _L2_ffn_in = {k: v for k, v in _L2_ffn_all.items() if k in ('w_gate', 'w_up', 'w_down')}
    del _L2_ffn_all

    def _L3_attn_setup():
        import jax, jax.numpy as jnp
        import numpy as np
        import math
        D_MODEL = 128
        D_QUERY = 64
        key = jax.random.key(seed)
        k1, k2, k3, k4 = jax.random.split(key, 4)
        X = jax.random.normal(k1, (4, 512, D_MODEL), dtype=jnp.float32)
        Wq = jax.random.normal(k2, (D_MODEL, D_QUERY), dtype=jnp.float32) * (1.0 / math.sqrt(D_MODEL))
        Wk = jax.random.normal(k3, (D_MODEL, D_QUERY), dtype=jnp.float32) * (1.0 / math.sqrt(D_MODEL))
        Wv = jax.random.normal(k4, (D_MODEL, D_MODEL), dtype=jnp.float32) * (1.0 / math.sqrt(D_MODEL))
        return {'X': X, 'Wq': Wq, 'Wk': Wk, 'Wv': Wv}
    _L3_attn_all = _L3_attn_setup()
    _L3_attn_in = {k: v for k, v in _L3_attn_all.items() if k in ('Wq', 'Wk', 'Wv')}
    del _L3_attn_all

    def _L3_xattn_setup():
        import jax, jax.numpy as jnp
        import numpy as np
        NUM_HEADS = 16
        HEAD_DIM = 64
        INNER = NUM_HEADS * HEAD_DIM
        QUERY_DIM = 128
        CONTEXT_DIM = 96
        SCALE = HEAD_DIM ** (-0.5)
        key = jax.random.key(seed)
        ks = jax.random.split(key, 6)
        B, NQ, NKV = (8, 128, 256)
        query = jax.random.normal(ks[0], (B, NQ, QUERY_DIM), dtype=jnp.float32)
        context = jax.random.normal(ks[1], (B, NKV, CONTEXT_DIM), dtype=jnp.float32)
        w_q = jax.random.normal(ks[2], (QUERY_DIM, INNER), dtype=jnp.float32) * QUERY_DIM ** (-0.5)
        w_kv = jax.random.normal(ks[3], (CONTEXT_DIM, 2 * INNER), dtype=jnp.float32) * CONTEXT_DIM ** (-0.5)
        w_out = jax.random.normal(ks[4], (INNER, QUERY_DIM), dtype=jnp.float32) * INNER ** (-0.5)
        b_out = jax.random.normal(ks[5], (QUERY_DIM,), dtype=jnp.float32) * 0.01
        return {'query': query, 'context': context, 'w_q': w_q, 'w_kv': w_kv, 'w_out': w_out, 'b_out': b_out}
    _L3_xattn_all = _L3_xattn_setup()
    _L3_xattn_in = {k: v for k, v in _L3_xattn_all.items() if k in ('w_q', 'w_kv', 'w_out', 'b_out')}
    del _L3_xattn_all

    def _L3_ffn_setup():
        import jax, jax.numpy as jnp
        import numpy as np
        DIM = 128
        DEPTH = 6
        HEADS = 16
        DIM_HEAD = 64
        WINDOW = 32
        INNER = HEADS * DIM_HEAD
        DIM_INNER = int(DIM * 4 * 2 / 3)
        QK_SCALE = 8.0

        def shift_tokens(t):
            a, s = jnp.split(t, 2, -1)
            s = jnp.pad(s, ((0, 0), (1, 0), (0, 0)))[:, :-1]
            return jnp.concatenate([a, s], -1)

        def l2norm(t):
            return t / jnp.maximum(jnp.linalg.norm(t, axis=-1, keepdims=True), 1e-12)

        def rotate_half(x):
            x1, x2 = jnp.split(x, 2, -1)
            return jnp.concatenate([-x2, x1], -1)

        def rotary_tables(n):
            half = jnp.arange(0, DIM_HEAD, 2, dtype=jnp.float32)
            inv_freq = 1.0 / 10000.0 ** (half / DIM_HEAD)
            t = jnp.arange(n, dtype=jnp.float32)
            freqs = t[:, None] * inv_freq[None, :]
            freqs = jnp.concatenate([freqs, freqs], -1)
            base_scale = (half + 0.4 * DIM_HEAD) / (1.4 * DIM_HEAD)
            power = (t - n // 2) / (WINDOW // 2)
            scale = base_scale[None, :] ** power[:, None]
            scale = jnp.concatenate([scale, scale], -1)
            return (freqs, scale)

        def local_attention(q, k, v):
            b, h, n, d = q.shape
            w = WINDOW
            nw = n // w
            bq = q.reshape(b, h, nw, w, d)
            bk = k.reshape(b, h, nw, w, d)
            bv = v.reshape(b, h, nw, w, d)

            def look(t):
                p = jnp.pad(t, ((0, 0), (0, 0), (1, 0), (0, 0), (0, 0)))
                return jnp.concatenate([p[:, :, :nw], p[:, :, 1:]], axis=3)
            bk2, bv2 = (look(bk), look(bv))
            seq = jnp.arange(n).reshape(nw, w)
            seq_p = jnp.pad(seq, ((1, 0), (0, 0)), constant_values=-1)
            jt = jnp.concatenate([seq_p[:nw], seq_p[1:]], axis=1)
            it = seq[:, :, None]
            jb = jt[:, None, :]
            mask = (it < jb) | (it > jb + w) | (jb == -1)
            sim = jnp.einsum('bhwie,bhwje->bhwij', bq, bk2) * QK_SCALE
            sim = jnp.where(mask, -jnp.finfo(sim.dtype).max, sim)
            attn = jax.nn.softmax(sim, -1)
            out = jnp.einsum('bhwij,bhwje->bhwie', attn, bv2)
            return out.reshape(b, h, n, d)

        def attn_layer(x, Wqkv, qs, ksc, Wo):
            b, n, _ = x.shape
            qkv = x @ Wqkv
            q, k, v = jnp.split(qkv, 3, -1)
            sh = lambda t: t.reshape(b, n, HEADS, DIM_HEAD).transpose(0, 2, 1, 3)
            q, k, v = (sh(q), sh(k), sh(v))
            q = l2norm(q) * qs
            k = l2norm(k) * ksc
            freqs, scale = rotary_tables(n)
            cos, sin = (jnp.cos(freqs), jnp.sin(freqs))
            q = q * cos * scale + rotate_half(q) * sin * scale
            inv = 1.0 / scale
            k = k * cos * inv + rotate_half(k) * sin * inv
            out = local_attention(q, k, v)
            out = out.transpose(0, 2, 1, 3).reshape(b, n, INNER)
            return out @ Wo

        def ffn_layer(x, g, bln, W1, b1, W2, b2):
            mu = x.mean(-1, keepdims=True)
            var = ((x - mu) ** 2).mean(-1, keepdims=True)
            xn = (x - mu) / jnp.sqrt(var + 1e-05) * g + bln
            hg = xn @ W1 + b1
            a, gate = jnp.split(hg, 2, -1)
            return a * jax.nn.gelu(gate, approximate=False) @ W2 + b2
        key = jax.random.key(seed)
        ks = jax.random.split(key, 8)
        B, N = (2, 256)
        init = lambda k, shape: jax.random.normal(k, shape, jnp.float32) * 0.02
        return {'x': jax.random.normal(ks[0], (B, N, DIM), jnp.float32), 'Wqkv': init(ks[1], (DEPTH, DIM, 3 * INNER)), 'q_scale': jnp.ones((DEPTH, DIM_HEAD), jnp.float32), 'k_scale': jnp.ones((DEPTH, DIM_HEAD), jnp.float32), 'Wo': init(ks[2], (DEPTH, INNER, DIM)), 'ln_g': jnp.ones((DEPTH, DIM), jnp.float32), 'ln_b': jnp.zeros((DEPTH, DIM), jnp.float32), 'W1': init(ks[3], (DEPTH, DIM, 2 * DIM_INNER)), 'b1': jnp.zeros((DEPTH, 2 * DIM_INNER), jnp.float32), 'W2': init(ks[4], (DEPTH, DIM_INNER, DIM)), 'b2': jnp.zeros((DEPTH, DIM), jnp.float32)}
    _L3_ffn_all = _L3_ffn_setup()
    _L3_ffn_in = {k: v for k, v in _L3_ffn_all.items() if k in ('Wqkv', 'q_scale', 'k_scale', 'Wo', 'ln_g', 'ln_b', 'W1', 'b1', 'W2', 'b2')}
    del _L3_ffn_all
    return {'x': x, 'ctx_768': ctx_768, 'mask_BxS2_bk0': mask_BxS2_bk0, 'L0_attn_W': _L0_attn_in['W'], 'L0_attn_b': _L0_attn_in['b'], 'L0_xattn_Wq': _L0_xattn_in['Wq'], 'L0_xattn_Wk': _L0_xattn_in['Wk'], 'L0_xattn_Wv': _L0_xattn_in['Wv'], 'L0_xattn_Wo': _L0_xattn_in['Wo'], 'L0_xattn_bo': _L0_xattn_in['bo'], 'L0_xattn_q_down': _L0_xattn_in['q_down'], 'L0_xattn_q_up': _L0_xattn_in['q_up'], 'L0_xattn_q_alpha': _L0_xattn_in['q_alpha'], 'L0_xattn_k_down': _L0_xattn_in['k_down'], 'L0_xattn_k_up': _L0_xattn_in['k_up'], 'L0_xattn_k_alpha': _L0_xattn_in['k_alpha'], 'L0_xattn_v_down': _L0_xattn_in['v_down'], 'L0_xattn_v_up': _L0_xattn_in['v_up'], 'L0_xattn_v_alpha': _L0_xattn_in['v_alpha'], 'L0_xattn_o_down': _L0_xattn_in['o_down'], 'L0_xattn_o_up': _L0_xattn_in['o_up'], 'L0_xattn_o_alpha': _L0_xattn_in['o_alpha'], 'L0_xattn_Wk_ipa': _L0_xattn_in['Wk_ipa'], 'L0_xattn_Wv_ipa': _L0_xattn_in['Wv_ipa'], 'L0_ffn_ln1_w': _L0_ffn_in['ln1_w'], 'L0_ffn_ln2_w': _L0_ffn_in['ln2_w'], 'L0_ffn_wqkv': _L0_ffn_in['wqkv'], 'L0_ffn_wo': _L0_ffn_in['wo'], 'L0_ffn_gate_w': _L0_ffn_in['gate_w'], 'L0_ffn_w13': _L0_ffn_in['w13'], 'L0_ffn_w2': _L0_ffn_in['w2'], 'L1_attn_Wqkv': _L1_attn_in['Wqkv'], 'L1_attn_bqkv': _L1_attn_in['bqkv'], 'L1_attn_Wout': _L1_attn_in['Wout'], 'L1_attn_bout': _L1_attn_in['bout'], 'L1_xattn_wq': _L1_xattn_in['wq'], 'L1_xattn_bq': _L1_xattn_in['bq'], 'L1_xattn_wk': _L1_xattn_in['wk'], 'L1_xattn_bk': _L1_xattn_in['bk'], 'L1_xattn_wv': _L1_xattn_in['wv'], 'L1_xattn_bv': _L1_xattn_in['bv'], 'L1_xattn_wo': _L1_xattn_in['wo'], 'L1_xattn_bo': _L1_xattn_in['bo'], 'L1_ffn_W_r': _L1_ffn_in['W_r'], 'L1_ffn_W_k': _L1_ffn_in['W_k'], 'L1_ffn_W_v': _L1_ffn_in['W_v'], 'L1_ffn_mu_r': _L1_ffn_in['mu_r'], 'L1_ffn_mu_k': _L1_ffn_in['mu_k'], 'L2_attn_Q': _L2_attn_in['Q'], 'L2_attn_K': _L2_attn_in['K'], 'L2_attn_V': _L2_attn_in['V'], 'L2_attn_O': _L2_attn_in['O'], 'L2_xattn_ln_x_g': _L2_xattn_in['ln_x_g'], 'L2_xattn_ln_x_b': _L2_xattn_in['ln_x_b'], 'L2_xattn_ln_l_g': _L2_xattn_in['ln_l_g'], 'L2_xattn_ln_l_b': _L2_xattn_in['ln_l_b'], 'L2_xattn_qn_g': _L2_xattn_in['qn_g'], 'L2_xattn_kn_g': _L2_xattn_in['kn_g'], 'L2_xattn_Wq': _L2_xattn_in['Wq'], 'L2_xattn_Wkv': _L2_xattn_in['Wkv'], 'L2_xattn_Wlkv': _L2_xattn_in['Wlkv'], 'L2_xattn_Wo': _L2_xattn_in['Wo'], 'L2_xattn_bo': _L2_xattn_in['bo'], 'L2_ffn_w_gate': _L2_ffn_in['w_gate'], 'L2_ffn_w_up': _L2_ffn_in['w_up'], 'L2_ffn_w_down': _L2_ffn_in['w_down'], 'L3_attn_Wq': _L3_attn_in['Wq'], 'L3_attn_Wk': _L3_attn_in['Wk'], 'L3_attn_Wv': _L3_attn_in['Wv'], 'L3_xattn_w_q': _L3_xattn_in['w_q'], 'L3_xattn_w_kv': _L3_xattn_in['w_kv'], 'L3_xattn_w_out': _L3_xattn_in['w_out'], 'L3_xattn_b_out': _L3_xattn_in['b_out'], 'L3_ffn_Wqkv': _L3_ffn_in['Wqkv'], 'L3_ffn_q_scale': _L3_ffn_in['q_scale'], 'L3_ffn_k_scale': _L3_ffn_in['k_scale'], 'L3_ffn_Wo': _L3_ffn_in['Wo'], 'L3_ffn_ln_g': _L3_ffn_in['ln_g'], 'L3_ffn_ln_b': _L3_ffn_in['ln_b'], 'L3_ffn_W1': _L3_ffn_in['W1'], 'L3_ffn_b1': _L3_ffn_in['b1'], 'L3_ffn_W2': _L3_ffn_in['W2'], 'L3_ffn_b2': _L3_ffn_in['b2']}

def reference(x, ctx_768, mask_BxS2_bk0, L0_attn_W, L0_attn_b, L0_xattn_Wq, L0_xattn_Wk, L0_xattn_Wv, L0_xattn_Wo, L0_xattn_bo, L0_xattn_q_down, L0_xattn_q_up, L0_xattn_q_alpha, L0_xattn_k_down, L0_xattn_k_up, L0_xattn_k_alpha, L0_xattn_v_down, L0_xattn_v_up, L0_xattn_v_alpha, L0_xattn_o_down, L0_xattn_o_up, L0_xattn_o_alpha, L0_xattn_Wk_ipa, L0_xattn_Wv_ipa, L0_ffn_ln1_w, L0_ffn_ln2_w, L0_ffn_wqkv, L0_ffn_wo, L0_ffn_gate_w, L0_ffn_w13, L0_ffn_w2, L1_attn_Wqkv, L1_attn_bqkv, L1_attn_Wout, L1_attn_bout, L1_xattn_wq, L1_xattn_bq, L1_xattn_wk, L1_xattn_bk, L1_xattn_wv, L1_xattn_bv, L1_xattn_wo, L1_xattn_bo, L1_ffn_W_r, L1_ffn_W_k, L1_ffn_W_v, L1_ffn_mu_r, L1_ffn_mu_k, L2_attn_Q, L2_attn_K, L2_attn_V, L2_attn_O, L2_xattn_ln_x_g, L2_xattn_ln_x_b, L2_xattn_ln_l_g, L2_xattn_ln_l_b, L2_xattn_qn_g, L2_xattn_kn_g, L2_xattn_Wq, L2_xattn_Wkv, L2_xattn_Wlkv, L2_xattn_Wo, L2_xattn_bo, L2_ffn_w_gate, L2_ffn_w_up, L2_ffn_w_down, L3_attn_Wq, L3_attn_Wk, L3_attn_Wv, L3_xattn_w_q, L3_xattn_w_kv, L3_xattn_w_out, L3_xattn_b_out, L3_ffn_Wqkv, L3_ffn_q_scale, L3_ffn_k_scale, L3_ffn_Wo, L3_ffn_ln_g, L3_ffn_ln_b, L3_ffn_W1, L3_ffn_b1, L3_ffn_W2, L3_ffn_b2):
    import jax
    import jax.numpy as jnp

    def _L0_attn_ref(x, W, b):
        import jax, jax.numpy as jnp
        import numpy as np
        B, N, DIM, HID = (4, 256, 128, 128)
        qkv = jnp.einsum('bnd,dh->bnh', x, W) + b
        Q, K, V = jnp.split(qkv, 3, axis=-1)
        scale = 1.0 / jnp.sqrt(jnp.asarray(HID, dtype=x.dtype))
        scores = jnp.einsum('bqh,bkh->bqk', Q, K) * scale
        attn = jax.nn.softmax(scores, axis=-1)
        out = jnp.einsum('bqk,bkh->bqh', attn, V)
        return out

    def _L0_xattn_ref(x, context, Wq, Wk, Wv, Wo, bo, q_down, q_up, q_alpha, k_down, k_up, k_alpha, v_down, v_up, v_alpha, o_down, o_up, o_alpha, Wk_ipa, Wv_ipa):
        import jax, jax.numpy as jnp
        import numpy as np
        HEADS = 16
        DIM_HEAD = 64
        RANK = 32
        LORA_W = 1.0
        IPA_SCALE = 1.0
        IPA_TOKENS = 4
        SCALE = DIM_HEAD ** (-0.5)

        def _split_heads(t):
            b, n, _ = t.shape
            return t.reshape(b, n, HEADS, DIM_HEAD).transpose(0, 2, 1, 3)

        def _merge_heads(t):
            b, h, n, d = t.shape
            return t.transpose(0, 2, 1, 3).reshape(b, n, h * d)

        def _attention(q_in, k_in, v_in):
            q = _split_heads(q_in)
            k = _split_heads(k_in)
            v = _split_heads(v_in)
            s = jnp.einsum('bhid,bhjd->bhij', q, k) * SCALE
            p = jax.nn.softmax(s, axis=-1)
            o = jnp.einsum('bhij,bhjd->bhid', p, v)
            return _merge_heads(o)

        def _lora(t, down, up, alpha):
            return t @ down @ up * (LORA_W * alpha[0] / RANK)
        q_in = x @ Wq + _lora(x, q_down, q_up, q_alpha)
        end = context.shape[1] - IPA_TOKENS
        org_ctx = context[:, :end, :]
        ipa_ctx = context[:, end:, :]
        k_in = org_ctx @ Wk + _lora(org_ctx, k_down, k_up, k_alpha)
        v_in = org_ctx @ Wv + _lora(org_ctx, v_down, v_up, v_alpha)
        out = _attention(q_in, k_in, v_in)
        ipa_k = ipa_ctx @ Wk_ipa
        ipa_v = ipa_ctx @ Wv_ipa
        out_ipa = _attention(q_in, ipa_k, ipa_v)
        out = out + IPA_SCALE * out_ipa
        return out @ Wo + bo + _lora(out, o_down, o_up, o_alpha)

    def _L0_ffn_ref(x, ln1_w, ln2_w, wqkv, wo, gate_w, w13, w2):
        import jax, jax.numpy as jnp
        import numpy as np
        HID = 128
        NH = 16
        NKV = 4
        HD = HID // NH
        E = 8
        TOPK = 2
        FFN = 256
        EPS = 1e-05
        THETA = 10000.0

        def _rmsnorm(x, w):
            var = jnp.mean(x * x, axis=-1, keepdims=True)
            return x * jax.lax.rsqrt(var + EPS) * w

        def _rope_tables(S):
            inv_freq = 1.0 / THETA ** (jnp.arange(0, HD, 2, dtype=jnp.float32) / HD)
            freqs = jnp.arange(S, dtype=jnp.float32)[:, None] * inv_freq[None, :]
            emb = jnp.concatenate([freqs, freqs], axis=-1)
            return (jnp.cos(emb), jnp.sin(emb))

        def _apply_rope(t, cos, sin):
            t1, t2 = jnp.split(t, 2, axis=-1)
            rot = jnp.concatenate([-t2, t1], axis=-1)
            return t * cos[None, :, None, :] + rot * sin[None, :, None, :]
        B, S, _ = x.shape
        h = _rmsnorm(x, ln1_w)
        qkv = jnp.einsum('bsh,oh->bso', h, wqkv)
        q = qkv[..., :NH * HD].reshape(B, S, NH, HD)
        k = qkv[..., NH * HD:(NH + NKV) * HD].reshape(B, S, NKV, HD)
        v = qkv[..., (NH + NKV) * HD:].reshape(B, S, NKV, HD)
        cos, sin = _rope_tables(S)
        q = _apply_rope(q, cos, sin)
        k = _apply_rope(k, cos, sin)
        groups = NH // NKV
        k = jnp.repeat(k, groups, axis=2)
        v = jnp.repeat(v, groups, axis=2)
        scale = HD ** (-0.5)
        scores = jnp.einsum('bqhd,bkhd->bhqk', q, k) * scale
        causal = jnp.tril(jnp.ones((S, S), dtype=bool))
        scores = jnp.where(causal[None, None], scores, jnp.finfo(scores.dtype).min)
        probs = jax.nn.softmax(scores, axis=-1)
        attn = jnp.einsum('bhqk,bkhd->bqhd', probs, v).reshape(B, S, NH * HD)
        x = x + jnp.einsum('bso,ho->bsh', attn, wo)
        h = _rmsnorm(x, ln2_w).reshape(-1, HID)
        T = h.shape[0]
        logits = jnp.einsum('th,eh->te', h, gate_w)
        rprobs = jax.nn.softmax(logits.astype(jnp.float32), axis=-1)
        topw, topi = jax.lax.top_k(rprobs, TOPK)
        topw = topw / jnp.sum(topw, axis=-1, keepdims=True)
        wfull = jnp.zeros((T, E), jnp.float32).at[jnp.arange(T)[:, None], topi].set(topw)
        wfull = wfull.astype(h.dtype)
        out = jnp.zeros((T, HID), h.dtype)
        for e in range(E):
            w1 = w13[e, :FFN]
            w3 = w13[e, FFN:]
            g = jax.nn.silu(h @ w1.T) * (h @ w3.T)
            out = out + jnp.einsum('tf,hf->th', g, w2[e]) * wfull[:, e:e + 1]
        return x + out.reshape(B, S, HID)

    def _L1_attn_ref(x, Wqkv, bqkv, Wout, bout):
        import jax, jax.numpy as jnp
        import numpy as np
        D_MODEL = 128
        NHEAD = 16
        WIN = 128
        B, S, dm = x.shape
        H, W = (NHEAD, WIN)
        Dh = dm // H
        nb = S // W
        qkv = (x @ Wqkv + bqkv).reshape(B, S, 3, H, Dh)
        q = qkv[:, :, 0].transpose(0, 2, 1, 3)
        k = qkv[:, :, 1].transpose(0, 2, 1, 3)
        v = qkv[:, :, 2].transpose(0, 2, 1, 3)
        qb = q.reshape(B, H, nb, W, Dh)
        kb = k.reshape(B, H, nb, W, Dh)
        vb = v.reshape(B, H, nb, W, Dh)
        kp = jnp.pad(kb, ((0, 0), (0, 0), (1, 1), (0, 0), (0, 0)))
        vp = jnp.pad(vb, ((0, 0), (0, 0), (1, 1), (0, 0), (0, 0)))
        kwin = jnp.concatenate([kp[:, :, :-2], kp[:, :, 1:-1], kp[:, :, 2:]], axis=3)
        vwin = jnp.concatenate([vp[:, :, :-2], vp[:, :, 1:-1], vp[:, :, 2:]], axis=3)
        scale = jnp.float32(1.0 / np.sqrt(dm))
        scores = jnp.einsum('bhnqd,bhnkd->bhnqk', qb, kwin) * scale
        n = jnp.arange(nb)[:, None, None]
        i = jnp.arange(W)[None, :, None]
        j = jnp.arange(3 * W)[None, None, :]
        qpos = n * W + i
        kpos = n * W - W + j
        mask = (jnp.abs(kpos - qpos) <= W) & (kpos >= 0) & (kpos < S)
        scores = jnp.where(mask[None, None], scores, jnp.float32(-1e+30))
        attn = jax.nn.softmax(scores, axis=-1)
        out = jnp.einsum('bhnqk,bhnkd->bhnqd', attn, vwin)
        out = out.reshape(B, H, S, Dh).transpose(0, 2, 1, 3).reshape(B, S, dm)
        return out @ Wout + bout

    def _L1_xattn_ref(x, y, wq, bq, wk, bk, wv, bv, wo, bo):
        import jax, jax.numpy as jnp
        import numpy as np
        N_HEADS = 16
        D_EMBED = 128
        D_CROSS = 96
        D_HEAD = D_EMBED // N_HEADS
        B, SQ, _ = x.shape
        SKV = y.shape[1]
        q = (x @ wq + bq).reshape(B, SQ, N_HEADS, D_HEAD)
        k = (y @ wk + bk).reshape(B, SKV, N_HEADS, D_HEAD)
        v = (y @ wv + bv).reshape(B, SKV, N_HEADS, D_HEAD)
        scores = jnp.einsum('bqhd,bkhd->bhqk', q, k) / jnp.sqrt(jnp.asarray(D_HEAD, x.dtype))
        attn = jax.nn.softmax(scores, axis=-1)
        out = jnp.einsum('bhqk,bkhd->bqhd', attn, v).reshape(B, SQ, D_EMBED)
        return out @ wo + bo

    def _L1_ffn_ref(x, W_r, W_k, W_v, mu_r, mu_k):
        import jax, jax.numpy as jnp
        import numpy as np
        DIM = 128

        def _reference_tuple_inner(x, W_r, W_k, W_v, mu_r, mu_k):
            B, T, C = x.shape
            x_prev = jnp.concatenate([jnp.zeros((B, 1, C), x.dtype), x[:, :-1, :]], axis=1)
            xr = mu_r * x + (1.0 - mu_r) * x_prev
            xk = mu_k * x + (1.0 - mu_k) * x_prev
            r = jax.nn.sigmoid(jnp.einsum('btc,dc->btd', xr, W_r))
            k = jnp.einsum('btc,dc->btd', xk, W_k)
            k_act = jnp.square(jax.nn.relu(k))
            out = r * jnp.einsum('btc,dc->btd', k_act, W_v)
            new_state = x[:, -1, :]
            return (out, new_state)
        return _reference_tuple_inner(x, W_r, W_k, W_v, mu_r, mu_k)[0]

    def _L2_attn_ref(x, Q, K, V, O):
        import jax, jax.numpy as jnp
        import numpy as np
        NUM_HEADS, D_HEAD, D_MODEL, N_CTX = (16, 64, 128, 256)
        BATCH, SEQ = (4, 256)
        q = jnp.einsum('nhm,btm->bnth', Q, x)
        k = jnp.einsum('nhm,btm->bnth', K, x)
        v = jnp.einsum('nhm,btm->bnth', V, x)
        scores = jnp.einsum('bnqh,bnkh->bnqk', q, k)
        s = x.shape[1]
        causal = jnp.tril(jnp.ones((s, s), dtype=bool))
        masked = jnp.where(causal, scores, jnp.float32(-10000000000.0))
        attn = jax.nn.softmax(masked, axis=-1)
        z = jnp.einsum('bnqk,bnkh->bnqh', attn, v)
        z = jnp.transpose(z, (0, 2, 1, 3)).reshape(x.shape[0], s, -1)
        return jnp.einsum('ma,bqa->bqm', O, z)

    def _L2_xattn_ref(x, latents, mask, ln_x_g, ln_x_b, ln_l_g, ln_l_b, qn_g, kn_g, Wq, Wkv, Wlkv, Wo, bo):
        import jax, jax.numpy as jnp
        import numpy as np
        DIM_IN, DIM_LAT, DIM_HEAD = (96, 128, 64)
        INNER = max(DIM_LAT, DIM_IN)
        HEADS = INNER // DIM_HEAD
        SCALE = DIM_HEAD ** (-0.5)
        RMS_EPS = 1e-08
        LN_EPS = 1e-05

        def layernorm(x, g, b):
            mu = jnp.mean(x, axis=-1, keepdims=True)
            var = jnp.mean((x - mu) ** 2, axis=-1, keepdims=True)
            return (x - mu) * jax.lax.rsqrt(var + LN_EPS) * g + b

        def rmsnorm(x, gamma):
            norm = jnp.sqrt(jnp.sum(x * x, axis=-1, keepdims=True)) * x.shape[-1] ** (-0.5)
            return x / jnp.maximum(norm, RMS_EPS) * gamma
        b, n, _ = x.shape
        m = latents.shape[1]
        xn = layernorm(x, ln_x_g, ln_x_b)
        ln = layernorm(latents, ln_l_g, ln_l_b)
        q = ln @ Wq.T
        kv = jnp.concatenate([xn @ Wkv.T, ln @ Wlkv.T], axis=1)
        k, v = (kv[..., :INNER], kv[..., INNER:])
        split_heads = lambda t: t.reshape(t.shape[0], t.shape[1], HEADS, DIM_HEAD).transpose(0, 2, 1, 3)
        q, k, v = (split_heads(q), split_heads(k), split_heads(v))
        qn = rmsnorm(q, qn_g) * SCALE
        kn = rmsnorm(k, kn_g)
        attn = jnp.einsum('bhid,bhjd->bhij', qn, kn)
        full_mask = jnp.pad(mask, ((0, 0), (0, m)), constant_values=True)
        attn = jnp.where(full_mask[:, None, None, :], attn, -jnp.finfo(attn.dtype).max)
        attn = jax.nn.softmax(attn, axis=-1)
        out = jnp.einsum('bhij,bhjd->bhid', attn, v)
        out = out.transpose(0, 2, 1, 3).reshape(b, m, INNER)
        return out @ Wo.T + bo

    def _L2_ffn_ref(x, w_gate, w_up, w_down):
        import jax, jax.numpy as jnp
        import numpy as np
        BLOCK = 16
        _GRID = jnp.array([0.0, 0.5, 1.0, 1.5, 2.0, 3.0, 4.0, 6.0], dtype=jnp.float32)
        _MID = jnp.array([0.25, 0.75, 1.25, 1.75, 2.5, 3.5, 5.0], dtype=jnp.float32)

        def fp4_quant_dequant(x):
            shape = x.shape
            xb = x.reshape(shape[:-1] + (shape[-1] // BLOCK, BLOCK))
            scale = jnp.max(jnp.abs(xb), axis=-1, keepdims=True) / 6.0
            scale = jnp.maximum(scale, jnp.float32(1e-12))
            xn = xb / scale
            idx = jnp.searchsorted(_MID, jnp.abs(xn))
            q = _GRID[idx] * jnp.sign(xn) * scale
            return q.reshape(shape)

        def fp4_linear(x, w):
            xq = fp4_quant_dequant(x)
            wq = fp4_quant_dequant(w)
            return jnp.einsum('bsk,nk->bsn', xq, wq)
        gate = fp4_linear(x, w_gate)
        y = fp4_linear(x, w_up)
        h = jax.nn.silu(gate) * y
        return fp4_linear(h, w_down)

    def _L3_attn_ref(X, Wq, Wk, Wv):
        import jax, jax.numpy as jnp
        import numpy as np
        import math
        D_MODEL = 128
        D_QUERY = 64
        B, T, _ = X.shape
        Q = X @ Wq
        K = X @ Wk
        V = X @ Wv
        scores = jnp.einsum('btd,bsd->bts', Q, K)
        causal = jnp.tril(jnp.ones((T, T), dtype=bool))
        scores = jnp.where(causal[None, :, :], scores, -jnp.inf)
        attn = jax.nn.softmax(scores / math.sqrt(D_QUERY), axis=2)
        return attn @ V

    def _L3_xattn_ref(query, context, w_q, w_kv, w_out, b_out):
        import jax, jax.numpy as jnp
        import numpy as np
        NUM_HEADS = 16
        HEAD_DIM = 64
        INNER = NUM_HEADS * HEAD_DIM
        QUERY_DIM = 128
        CONTEXT_DIM = 96
        SCALE = HEAD_DIM ** (-0.5)
        B, NQ, _ = query.shape
        NKV = context.shape[1]
        q = query @ w_q
        kv = context @ w_kv
        k, v = jnp.split(kv, 2, axis=-1)
        q = q.reshape(B, NQ, NUM_HEADS, HEAD_DIM).transpose(0, 2, 1, 3)
        k = k.reshape(B, NKV, NUM_HEADS, HEAD_DIM).transpose(0, 2, 1, 3)
        v = v.reshape(B, NKV, NUM_HEADS, HEAD_DIM).transpose(0, 2, 1, 3)
        scores = jnp.einsum('bhqd,bhkd->bhqk', q, k) * SCALE
        attn = jax.nn.softmax(scores, axis=-1)
        out = jnp.einsum('bhqk,bhkd->bhqd', attn, v)
        out = out.transpose(0, 2, 1, 3).reshape(B, NQ, INNER)
        return out @ w_out + b_out

    def _L3_ffn_ref(x, Wqkv, q_scale, k_scale, Wo, ln_g, ln_b, W1, b1, W2, b2):
        import jax, jax.numpy as jnp
        import numpy as np
        DIM = 128
        DEPTH = 6
        HEADS = 16
        DIM_HEAD = 64
        WINDOW = 32
        INNER = HEADS * DIM_HEAD
        DIM_INNER = int(DIM * 4 * 2 / 3)
        QK_SCALE = 8.0

        def shift_tokens(t):
            a, s = jnp.split(t, 2, -1)
            s = jnp.pad(s, ((0, 0), (1, 0), (0, 0)))[:, :-1]
            return jnp.concatenate([a, s], -1)

        def l2norm(t):
            return t / jnp.maximum(jnp.linalg.norm(t, axis=-1, keepdims=True), 1e-12)

        def rotate_half(x):
            x1, x2 = jnp.split(x, 2, -1)
            return jnp.concatenate([-x2, x1], -1)

        def rotary_tables(n):
            half = jnp.arange(0, DIM_HEAD, 2, dtype=jnp.float32)
            inv_freq = 1.0 / 10000.0 ** (half / DIM_HEAD)
            t = jnp.arange(n, dtype=jnp.float32)
            freqs = t[:, None] * inv_freq[None, :]
            freqs = jnp.concatenate([freqs, freqs], -1)
            base_scale = (half + 0.4 * DIM_HEAD) / (1.4 * DIM_HEAD)
            power = (t - n // 2) / (WINDOW // 2)
            scale = base_scale[None, :] ** power[:, None]
            scale = jnp.concatenate([scale, scale], -1)
            return (freqs, scale)

        def local_attention(q, k, v):
            b, h, n, d = q.shape
            w = WINDOW
            nw = n // w
            bq = q.reshape(b, h, nw, w, d)
            bk = k.reshape(b, h, nw, w, d)
            bv = v.reshape(b, h, nw, w, d)

            def look(t):
                p = jnp.pad(t, ((0, 0), (0, 0), (1, 0), (0, 0), (0, 0)))
                return jnp.concatenate([p[:, :, :nw], p[:, :, 1:]], axis=3)
            bk2, bv2 = (look(bk), look(bv))
            seq = jnp.arange(n).reshape(nw, w)
            seq_p = jnp.pad(seq, ((1, 0), (0, 0)), constant_values=-1)
            jt = jnp.concatenate([seq_p[:nw], seq_p[1:]], axis=1)
            it = seq[:, :, None]
            jb = jt[:, None, :]
            mask = (it < jb) | (it > jb + w) | (jb == -1)
            sim = jnp.einsum('bhwie,bhwje->bhwij', bq, bk2) * QK_SCALE
            sim = jnp.where(mask, -jnp.finfo(sim.dtype).max, sim)
            attn = jax.nn.softmax(sim, -1)
            out = jnp.einsum('bhwij,bhwje->bhwie', attn, bv2)
            return out.reshape(b, h, n, d)

        def attn_layer(x, Wqkv, qs, ksc, Wo):
            b, n, _ = x.shape
            qkv = x @ Wqkv
            q, k, v = jnp.split(qkv, 3, -1)
            sh = lambda t: t.reshape(b, n, HEADS, DIM_HEAD).transpose(0, 2, 1, 3)
            q, k, v = (sh(q), sh(k), sh(v))
            q = l2norm(q) * qs
            k = l2norm(k) * ksc
            freqs, scale = rotary_tables(n)
            cos, sin = (jnp.cos(freqs), jnp.sin(freqs))
            q = q * cos * scale + rotate_half(q) * sin * scale
            inv = 1.0 / scale
            k = k * cos * inv + rotate_half(k) * sin * inv
            out = local_attention(q, k, v)
            out = out.transpose(0, 2, 1, 3).reshape(b, n, INNER)
            return out @ Wo

        def ffn_layer(x, g, bln, W1, b1, W2, b2):
            mu = x.mean(-1, keepdims=True)
            var = ((x - mu) ** 2).mean(-1, keepdims=True)
            xn = (x - mu) / jnp.sqrt(var + 1e-05) * g + bln
            hg = xn @ W1 + b1
            a, gate = jnp.split(hg, 2, -1)
            return a * jax.nn.gelu(gate, approximate=False) @ W2 + b2
        for i in range(DEPTH):
            x = attn_layer(shift_tokens(x), Wqkv[i], q_scale[i], k_scale[i], Wo[i]) + x
            x = ffn_layer(shift_tokens(x), ln_g[i], ln_b[i], W1[i], b1[i], W2[i], b2[i]) + x
        return x
    x = x + _L0_attn_ref(_layernorm(x, axis=-1), L0_attn_W, L0_attn_b)
    x = x + _L0_xattn_ref(_layernorm(x, axis=-1), ctx_768, L0_xattn_Wq, L0_xattn_Wk, L0_xattn_Wv, L0_xattn_Wo, L0_xattn_bo, L0_xattn_q_down, L0_xattn_q_up, L0_xattn_q_alpha, L0_xattn_k_down, L0_xattn_k_up, L0_xattn_k_alpha, L0_xattn_v_down, L0_xattn_v_up, L0_xattn_v_alpha, L0_xattn_o_down, L0_xattn_o_up, L0_xattn_o_alpha, L0_xattn_Wk_ipa, L0_xattn_Wv_ipa)
    x = x + _L0_ffn_ref(_layernorm(x, axis=-1), L0_ffn_ln1_w, L0_ffn_ln2_w, L0_ffn_wqkv, L0_ffn_wo, L0_ffn_gate_w, L0_ffn_w13, L0_ffn_w2)
    x = x + _L1_attn_ref(_layernorm(x, axis=-1), L1_attn_Wqkv, L1_attn_bqkv, L1_attn_Wout, L1_attn_bout)
    x = x + _L1_xattn_ref(_layernorm(x, axis=-1), ctx_768, L1_xattn_wq, L1_xattn_bq, L1_xattn_wk, L1_xattn_bk, L1_xattn_wv, L1_xattn_bv, L1_xattn_wo, L1_xattn_bo)
    x = x + _L1_ffn_ref(_layernorm(x, axis=-1), L1_ffn_W_r, L1_ffn_W_k, L1_ffn_W_v, L1_ffn_mu_r, L1_ffn_mu_k)
    x = x + _L2_attn_ref(_layernorm(x, axis=-1), L2_attn_Q, L2_attn_K, L2_attn_V, L2_attn_O)
    x = x + _L2_xattn_ref(ctx_768, _layernorm(x, axis=-1), mask_BxS2_bk0, L2_xattn_ln_x_g, L2_xattn_ln_x_b, L2_xattn_ln_l_g, L2_xattn_ln_l_b, L2_xattn_qn_g, L2_xattn_kn_g, L2_xattn_Wq, L2_xattn_Wkv, L2_xattn_Wlkv, L2_xattn_Wo, L2_xattn_bo)
    x = x + _L2_ffn_ref(_layernorm(x, axis=-1), L2_ffn_w_gate, L2_ffn_w_up, L2_ffn_w_down)
    x = x + _L3_attn_ref(_layernorm(x, axis=-1), L3_attn_Wq, L3_attn_Wk, L3_attn_Wv)
    x = x + _L3_xattn_ref(_layernorm(x, axis=-1), ctx_768, L3_xattn_w_q, L3_xattn_w_kv, L3_xattn_w_out, L3_xattn_b_out)
    x = x + _L3_ffn_ref(_layernorm(x, axis=-1), L3_ffn_Wqkv, L3_ffn_q_scale, L3_ffn_k_scale, L3_ffn_Wo, L3_ffn_ln_g, L3_ffn_ln_b, L3_ffn_W1, L3_ffn_b1, L3_ffn_W2, L3_ffn_b2)
    return x

_drawn_inputs = setup_inputs


def setup_inputs(seed=0):
    import zlib

    import numpy as np

    out = dict(_drawn_inputs(seed))
    spreads = {'L0_xattn_bo': (0.0, 0.1),
     'L0_ffn_ln1_w': (1.0, 0.6),
     'L0_ffn_ln2_w': (1.0, 0.6),
     'L1_attn_bqkv': (0.0, 0.511),
     'L1_attn_bout': (0.0, 0.1),
     'L1_xattn_bq': (0.0, 0.563),
     'L1_xattn_bk': (0.0, 2.0),
     'L1_xattn_bv': (0.0, 0.1),
     'L1_xattn_bo': (0.0, 0.1),
     'L2_xattn_ln_x_g': (1.0, 0.6),
     'L2_xattn_ln_x_b': (0.0, 0.567),
     'L2_xattn_ln_l_g': (1.0, 0.2),
     'L2_xattn_ln_l_b': (0.0, 0.1),
     'L2_xattn_qn_g': (1.0, 0.6),
     'L2_xattn_kn_g': (1.0, 0.6),
     'L2_xattn_bo': (0.0, 0.1),
     'L3_ffn_q_scale': (1.0, 0.6),
     'L3_ffn_k_scale': (1.0, 0.6),
     'L3_ffn_ln_g': (1.0, 0.6),
     'L3_ffn_ln_b': (0.0, 0.8),
     'L3_ffn_b1': (0.0, 0.8),
     'L3_ffn_b2': (0.0, 0.433)}
    factors = {'L0_attn_b': 3.819,
     'L0_xattn_Wq': 8.0,
     'L0_xattn_Wk': 8.0,
     'L0_xattn_q_down': 8.0,
     'L0_xattn_q_up': 8.0,
     'L0_xattn_k_down': 8.0,
     'L0_xattn_k_up': 8.0,
     'L0_xattn_v_down': 5.595,
     'L0_xattn_v_up': 5.779,
     'L0_xattn_o_down': 3.626,
     'L0_xattn_o_up': 3.624,
     'L0_xattn_Wk_ipa': 8.0,
     'L0_ffn_wqkv': 5.924,
     'L0_ffn_wo': 5.998,
     'L0_ffn_gate_w': 8.0,
     'L0_ffn_w13': 8.0,
     'L0_ffn_w2': 8.0,
     'L1_attn_Wqkv': 8.0,
     'L1_attn_Wout': 3.47,
     'L1_ffn_W_r': 4.004,
     'L1_ffn_mu_r': 8.0,
     'L2_ffn_w_gate': 8.0,
     'L2_ffn_w_up': 8.0,
     'L2_ffn_w_down': 8.0,
     'L3_xattn_b_out': 41.835,
     'L3_ffn_W1': 6.1,
     'L3_ffn_W2': 6.078,
     'L3_attn_Wq': 2.862,
     'L3_attn_Wk': 2.903}
    for name, (base, spread) in spreads.items():
        noise = np.random.default_rng([zlib.crc32(name.encode()), seed]).standard_normal(out[name].shape)
        drawn = base * np.exp(spread * noise) if base else spread * noise
        out[name] = jnp.asarray(drawn.astype(out[name].dtype))
    for name, factor in factors.items():
        out[name] = (out[name] * factor).astype(out[name].dtype)
    return out
```

```python
from contextlib import ExitStack, contextmanager

import numpy as np
import concourse.bass as bass
from concourse import mybir

F32 = mybir.dt.float32
BF16 = mybir.dt.bfloat16
U8 = mybir.dt.uint8
ALU = mybir.AluOpType
ACT = mybir.ActivationFunctionType
AX = mybir.AxisListType

P = 128
B, N, D = 4, 256, 128
T = B * N
NT = T // P
QT = N // P
M, C = 512, 96
MT = B * M // P
KT = M // P
BANK = 512
H, DH = 16, 64
HS = D // H
PAIRS = H // 2
RANK = 32
IPA = 4
EXPERTS, FFN = 8, 256
FP4_FFN, FP4_BLOCK = 352, 16
DEPTH, GLU, WINDOW = 6, int(D * 4 * 2 / 3), 32
NEG = -1.0e30
LN_EPS = 1e-5


class Count:

    def __init__(self, sem, base, per, step):
        self.sem, self.base, self.per, self.step = sem, base, per, step

    def at(self, i, k):
        return i * (self.per * self.step) + (self.base + k * self.step)


class Signals:

    def __init__(self, nc, ctx, ahead):
        self.nc, self.ctx, self.sems, self.base = nc, ctx, {}, {}
        for name in ahead:
            self(name, 1)
            nc.sync.sem_inc(self.sems[name], 1)
        nc.all_engine_barrier()

    def __call__(self, name, per, iters=1, step=1):
        if name not in self.sems:
            self.sems[name] = self.ctx.enter_context(self.nc.semaphore(name))
            self.base[name] = 0
        out = Count(self.sems[name], self.base[name], per, step)
        self.base[name] += per * iters * step
        return out


@contextmanager
def rounds(eng, iters):
    if iters == 1:
        yield 0
    else:
        with eng.Fori(0, iters) as i:
            yield i


class Chunk:

    def __init__(self, engine, mm, out, after=()):
        self.engine, self.mm, self.out, self.after = engine, mm, out, after


def emptied_before(chunks, j, banks):
    need = {}
    for d in ([j - banks] if j >= banks else []) + list(chunks[j].after):
        e = chunks[d].engine
        need[e] = max(need.get(e, 0), sum(c.engine == e for c in chunks[:d + 1]))
    return sorted(need.items())


class Unit:

    def __init__(self, nk, scores, values, store, width, base=None):
        self.nk, self.scores, self.values, self.store, self.width = nk, scores, values, store, width


def decoder(nc, a, out):
    ctx = ExitStack()
    with ctx:
        signal = Signals(nc, ctx, AHEAD)

        def sb(name, shape, dt=F32):
            return ctx.enter_context(nc.sbuf_tensor(name, shape, dt))

        def ps(name, shape):
            psum_names[0] += 1
            return nc.psum_tensor(f"{name}_{psum_names[0]}", shape, F32)
        psum_names = [0]

        def copy(engine, dst, src, scale=1.0):
            if engine == "act":
                return nc.scalar.activation(dst, src, ACT.Copy, scale=scale)
            if isinstance(scale, float) and scale == 1.0:
                return nc.vector.tensor_copy(dst, src)
            return nc.vector.tensor_scalar(dst, src, scale, None, ALU.mult)

        def affine(engine, dst, src, scale, bias):
            if engine == "act":
                return nc.scalar.activation(dst, src, ACT.Identity, bias=bias, scale=scale)
            return nc.vector.tensor_scalar(dst, src, scale, bias, ALU.mult, ALU.add)

        x = sb("x", [P, NT, D])
        xin = sb("xin", [P, NT, D])
        z = sb("z", [P, NT, D])
        xnT = sb("xnT", [P, T])
        ctx_tok = sb("ctx_tok", [P, MT, C])
        ctxT = sb("ctxT", [P, B * M])
        stats = sb("stats", [P, MT, 6])
        meanvar = sb("meanvar", [P, MT, 2])
        spread = sb("spread", [P, MT])
        rstd = sb("rstd", [P, MT])
        ident = sb("ident", [P, P])
        ident16 = sb("ident16", [P, P], BF16)
        masks = sb("masks", [P, 4, P])
        masks16 = sb("masks16", [P, 4, P], BF16)
        ones = sb("ones", [P, P])
        ones16 = sb("ones16", [P, P], BF16)
        head_mask = sb("head_mask", [P, H])
        rot8 = sb("rot8", [P, P])
        rot64 = sb("rot64", [P, P])
        block64 = sb("block64", [P, P])
        cols = sb("cols", [P, 32])
        brow = sb("brow", [1, 512])
        qT = sb("qT", [P, 2, T])
        qM = sb("qM", [P, 2, T])
        kT = sb("kT", [P, B * (M + N)])
        V = sb("V", [P, MT + NT, D])
        probs = sb("probs", [P, 3, M + N])
        turned = sb("turned", [P, 4, BANK])
        negmax = sb("negmax", [P, 32])
        rowsum = sb("rowsum", [P, 32])
        rowinv = sb("rowinv", [P, 32])
        heads_out = sb("heads_out", [P, NT, D])
        outT = sb("outT", [P, T])
        wq = sb("wq", [P, D])
        wk = sb("wk", [P, D])
        wv = sb("wv", [P, D])
        wo = sb("wo", [P, D])

        def columns(c0, c1=None):
            return cols[:, c0:(c0 + 1 if c1 is None else c1)]

        def load(pairs):
            arrived = signal("small_loads", len(pairs), step=16)
            with nc.Block() as block:
                @block.sync
                def _(sp):
                    for dst, src in pairs:
                        sp.dma_start(dst, src).then_inc(arrived.sem, 16)
                    sp.wait_ge(arrived.sem, arrived.at(0, len(pairs)))

        def col_of(vec):
            return vec.rearrange("(d o) -> d o", o=1)

        def row_of(vec):
            return vec.rearrange("(o d) -> o d", o=1)

        def chunk_block(chunks, n=0, iters=1, tag=""):
            filled = signal(tag + "bank_filled", len(chunks), iters)
            count = {e: sum(c.engine == e for c in chunks) for e in ("act", "dve")}
            emptied = {e: signal(f"{tag}bank_emptied_{e}", count[e], iters) for e in ("act", "dve")}
            slots = 4
            with ps("bank", [P, slots, BANK]) as bank, nc.Block() as block:
                @block.tensor
                def _(pe):
                    for j, c in enumerate(chunks):
                        for e, k in emptied_before(chunks, j, slots):
                            pe.wait_ge(emptied[e].sem, emptied[e].at(n, k))
                        c.mm(bank[:, j % slots, :]).then_inc(filled.sem, 1)

                def empty(eng, e):
                    for j, c in enumerate(chunks):
                        if c.engine == e:
                            eng.wait_ge(filled.sem, filled.at(n, j + 1))
                            c.out(bank[:, j % slots, :]).then_inc(emptied[e].sem, 1)

                @block.scalar
                def _(act):
                    empty(act, "act")

                @block.vector
                def _(dve):
                    empty(dve, "dve")

        def norm(src, tiles, width, dst, dstT=None, rms=False, gain=None, bias=None, eps=LN_EPS):
            measured = signal("measured", tiles)
            gathered = signal("gathered", tiles)
            eps_added = signal("eps_added", 2)
            rooted = signal("rooted", 1)
            inverted = signal("inverted", 1)
            normed = signal("normed", tiles)
            nbank = (tiles + 3) // 4 if dstT is not None else 0
            turned_in = signal("norm_turned", nbank)
            moved_act = signal("norm_moved_act", (nbank + 1) // 2)
            moved_dve = signal("norm_moved_dve", nbank // 2)
            with ps("bank", [P, 4, BANK]) as bank, nc.Block() as block:
                def move(e, j):
                    s, d = bank[0:width, j % 4, :], dstT[0:width, j * BANK:(j + 1) * BANK]
                    if bias is not None:
                        return affine(e, d, s, gain[0:width], bias[0:width])
                    return copy(e, d, s, 1.0 if gain is None else gain[0:width])

                @block.vector
                def _(dve):
                    for t in range(tiles):
                        nc.vector.bn_stats(stats[:, t, :], src[:, t, 0:width]).then_inc(measured.sem, 1)
                    for t in range(tiles):
                        dve.wait_ge(measured.sem, measured.at(0, t + 1))
                        nc.vector.bn_aggr(meanvar[:, t, :], stats[:, t, :]).then_inc(gathered.sem, 1)
                    dve.wait_ge(gathered.sem, gathered.at(0, tiles))
                    if rms:
                        nc.vector.tensor_tensor(spread[:, 0:tiles], meanvar[:, 0:tiles, 0], meanvar[:, 0:tiles, 0],
                                                ALU.mult).then_inc(eps_added.sem, 1)
                        dve.wait_ge(eps_added.sem, eps_added.at(0, 1))
                        nc.vector.scalar_tensor_tensor(spread[:, 0:tiles], meanvar[:, 0:tiles, 1], eps,
                                                       spread[:, 0:tiles], ALU.add, ALU.add).then_inc(eps_added.sem, 1)
                    else:
                        nc.vector.tensor_scalar(spread[:, 0:tiles], meanvar[:, 0:tiles, 1], eps, None,
                                                ALU.add).then_inc(eps_added.sem, 2)
                    dve.wait_ge(rooted.sem, rooted.at(0, 1))
                    nc.vector.reciprocal(rstd[:, 0:tiles], spread[:, 0:tiles]).then_inc(inverted.sem, 1)
                    dve.wait_ge(inverted.sem, inverted.at(0, 1))
                    for t in range(tiles):
                        if rms:
                            last = nc.vector.tensor_scalar(dst[:, t, 0:width], src[:, t, 0:width], rstd[:, t:t + 1],
                                                           None, ALU.mult)
                        else:
                            last = nc.vector.tensor_scalar(dst[:, t, 0:width], src[:, t, 0:width],
                                                           meanvar[:, t, 0:1], rstd[:, t:t + 1],
                                                           ALU.subtract, ALU.mult)
                        last.then_inc(normed.sem, 1)
                    for j in range(1, nbank, 2):
                        dve.wait_ge(turned_in.sem, turned_in.at(0, j + 1))
                        move("dve", j).then_inc(moved_dve.sem, 1)

                @block.scalar
                def _(act):
                    act.wait_ge(eps_added.sem, eps_added.at(0, 2))
                    nc.scalar.activation(spread[:, 0:tiles], spread[:, 0:tiles], ACT.Sqrt).then_inc(rooted.sem, 1)
                    for j in range(0, nbank, 2):
                        act.wait_ge(turned_in.sem, turned_in.at(0, j + 1))
                        move("act", j).then_inc(moved_act.sem, 1)

                @block.tensor
                def _(pe):
                    for j in range(nbank):
                        pe.wait_ge(normed.sem, normed.at(0, 4 * j + 4))
                        for q in range(4):
                            last = nc.tensor.transpose(bank[0:width, j % 4, q * P:(q + 1) * P],
                                                       dst[:, 4 * j + q, 0:width], ident[:, :])
                        last.then_inc(turned_in.sem, 1)

        def attention(units, iters=1, n_of=lambda i: i, total=None, head=(), tail=(), head_loads=None, tail_loads=None,
                      loads=(0, 0), mask_heads=False, ipa=False, finish=None, wide=1):
            total = iters if total is None else total
            chunks = list(head) + list(tail)
            nh, U = len(head), len(units)
            turns = [[(g, min(g + 4, u.nk // P)) for g in range(0, u.nk // P, 4)] if wide == 1 else
                     [(0, 3), (3, 6)] for u in units]
            G = len(turns[0])
            slots = {1: 4, 2: 2}[wide]
            banks = 2
            lag_v = 3
            ow = units[0].width

            weights_in = signal("weights_in", loads[0], total, 16)
            out_weights_in = signal("out_weights_in", loads[1], total, 16)
            filled = signal("bank_filled", len(chunks), total)
            count = {e: sum(c.engine == e for c in chunks) for e in ("act", "dve")}
            emptied = {e: signal(f"bank_emptied_{e}", count[e], total) for e in ("act", "dve")}
            nhead = {e: sum(c.engine == e for c in head) for e in ("act", "dve")}
            masked = signal("masked_q", 2 if mask_heads else 0, total)
            scored = signal("scores_ready", U, total)
            maxed = signal("max_ready", U, total)
            exped = signal("probs_ready", U, total)
            rescaled = signal("ipa_rescaled", 2 * U if ipa else 0, total)
            flipped = signal("probs_turned", U * G, total)
            moved = [signal(f"turned_moved_{e}", U * G // 2, total) for e in ("act", "dve")]
            summed = signal("values_ready", U, total)
            inverse = signal("rowinv_ready", U, total)
            stored = signal("head_stored", U, total)

            with ExitStack() as inner:
                proj = inner.enter_context(ps("proj", [P, banks, BANK]))
                scores = inner.enter_context(ps("scores", [P, slots, wide * BANK]))
                flip = inner.enter_context(ps("flip", [P, 2, BANK]))
                block = inner.enter_context(nc.Block())

                def weighted(u):
                    return proj[:, u % banks, 0:ow]

                @block.sync
                def _(sp):
                    if loads[0]:
                        head_loads(sp, n_of(0) if iters == 1 else 0, weights_in.sem)
                    if loads[1]:
                        tail_loads(sp, n_of(0) if iters == 1 else 0, out_weights_in.sem)
                    if iters > 1 and loads[0]:
                        with sp.Fori(0, iters - 1) as i:
                            n = n_of(i)
                            sp.wait_ge(filled.sem, filled.at(n, nh))
                            head_loads(sp, i + 1, weights_in.sem)
                            if loads[1]:
                                sp.wait_ge(filled.sem, filled.at(n, len(chunks)))
                                tail_loads(sp, i + 1, out_weights_in.sem)

                @block.gpsimd
                def _(pool):
                    def mask(i, s):
                        nc.gpsimd.tensor_tensor(qM[:, s, :], qT[:, 0, :],
                                                head_mask[:, bass.ds(2 * i + s, 1)].to_broadcast([P, T]),
                                                ALU.mult).then_inc(masked.sem, 1)
                    if mask_heads:
                        mask(0, 0)
                        mask(0, 1)
                        with pool.Fori(0, iters - 1) as i:
                            for s in range(2):
                                pool.wait_ge(scored.sem, scored.at(i, (s + 1) * U // 2))
                                mask(i + 1, s)
                    if finish:
                        with rounds(pool, iters) as i:
                            finish.pool(pool, n_of(i), emptied)

                @block.tensor
                def _(pe):
                    def fill(n, j):
                        c = chunks[j]
                        if j < banks:
                            for e in ("act", "dve"):
                                pe.wait_ge(emptied[e].sem, emptied[e].at(n, 0))
                        for e, k in emptied_before(chunks, j, banks):
                            pe.wait_ge(emptied[e].sem, emptied[e].at(n, k))
                        c.mm(proj[:, j % banks, :]).then_inc(filled.sem, 1)

                    with rounds(pe, iters) as i:
                        n = n_of(i)
                        if loads[0]:
                            pe.wait_ge(weights_in.sem, weights_in.at(n, loads[0]))
                        for j in range(nh):
                            fill(n, j)
                        for e in ("act", "dve"):
                            pe.wait_ge(emptied[e].sem, emptied[e].at(n, nhead[e]))
                        if finish:
                            pe.wait_ge(finish.done.sem, finish.done.at(n, finish.done.per))
                        for s in range(U + lag_v):
                            if s < U:
                                if mask_heads and s % (U // 2) == 0:
                                    pe.wait_ge(masked.sem, masked.at(n, s // (U // 2) + 1))
                                pe.wait_ge(exped.sem, exped.at(n, max(0, s - slots + 1)))
                                units[s].scores(scores[:, s % slots, :]).then_inc(scored.sem, 1)
                            t = s - 2
                            if 0 <= t < U:
                                if ipa:
                                    pe.wait_ge(rescaled.sem, rescaled.at(n, 2 * t + 2))
                                else:
                                    pe.wait_ge(exped.sem, exped.at(n, t + 1))
                                for g, (b0, b1) in enumerate(turns[t]):
                                    q = t * G + g
                                    pe.wait_ge(moved[q % 2].sem, moved[q % 2].at(n, q // 2))
                                    for j in range(b0, b1):
                                        last = nc.tensor.transpose(flip[:, q % 2, (j - b0) * P:(j - b0 + 1) * P],
                                                                   probs[:, t % 3, j * P:(j + 1) * P], ident[:, :])
                                    last.then_inc(flipped.sem, 1)
                            t = s - lag_v
                            if 0 <= t < U:
                                pe.wait_ge(stored.sem, stored.at(n, max(0, t - banks + 1)))
                                for g, (b0, b1) in enumerate(turns[t]):
                                    q = t * G + g
                                    pe.wait_ge(moved[q % 2].sem, moved[q % 2].at(n, q // 2 + 1))
                                    for j in range(b0, b1):
                                        last = nc.tensor.matmul(weighted(t),
                                                                turned[:, q % 4, (j - b0) * P:(j - b0 + 1) * P],
                                                                units[t].values(j, i),
                                                                start=(j == 0), stop=(j == units[t].nk // P - 1))
                                last.then_inc(summed.sem, 1)
                        if tail:
                            pe.wait_ge(stored.sem, stored.at(n, U))
                            if loads[1]:
                                pe.wait_ge(out_weights_in.sem, out_weights_in.at(n, loads[1]))
                            for j in range(nh, len(chunks)):
                                fill(n, j)

                def empty(eng, e, n, js):
                    for j in js:
                        if chunks[j].engine == e:
                            eng.wait_ge(filled.sem, filled.at(n, j + 1))
                            chunks[j].out(proj[:, j % banks, :]).then_inc(emptied[e].sem, 1)

                def move_turned(eng, k, n, t):
                    for g, (b0, b1) in enumerate(turns[t]):
                        q = t * G + g
                        if q % 2 == k:
                            w = (b1 - b0) * P
                            eng.wait_ge(flipped.sem, flipped.at(n, q + 1))
                            if q >= 4:
                                eng.wait_ge(summed.sem, summed.at(n, (q - 4) // G + 1))
                            else:
                                eng.wait_ge(summed.sem, summed.at(n, 0))
                            copy(("act", "dve")[k], turned[:, q % 4, 0:w],
                                 flip[:, q % 2, 0:w]).then_inc(moved[k].sem, 1)

                @block.scalar
                def _(act):
                    with rounds(act, iters) as i:
                        n = n_of(i)
                        empty(act, "act", n, range(nh))
                        if finish:
                            finish.act(act, n, emptied)
                        act.wait_ge(stored.sem, stored.at(n, 0))
                        for s in range(U + 2):
                            if s < U:
                                nk = units[s].nk
                                act.wait_ge(maxed.sem, maxed.at(n, s + 1))
                                act.wait_ge(flipped.sem, flipped.at(n, max(0, s - 2) * G))
                                if ipa:
                                    nc.scalar.activation(probs[:, s % 3, 0:nk - IPA], scores[:, s % slots, 0:nk - IPA],
                                                         ACT.Exp, bias=negmax[:, s:s + 1],
                                                         accum_out=rowsum[:, s:s + 1])
                                    nc.scalar.activation(probs[:, s % 3, nk - IPA:nk], scores[:, s % slots, nk - IPA:nk],
                                                         ACT.Exp, bias=negmax[:, U + s:U + s + 1],
                                                         accum_out=rowsum[:, U + s:U + s + 1]).then_inc(exped.sem, 1)
                                else:
                                    nc.scalar.activation(probs[:, s % 3, 0:nk], scores[:, s % slots, 0:nk], ACT.Exp,
                                                         bias=negmax[:, s:s + 1],
                                                         accum_out=rowsum[:, s:s + 1]).then_inc(exped.sem, 1)
                            if 0 <= s - 2 < U:
                                move_turned(act, 0, n, s - 2)
                        empty(act, "act", n, range(nh, len(chunks)))

                @block.vector
                def _(dve):
                    with rounds(dve, iters) as i:
                        n = n_of(i)
                        empty(dve, "dve", n, range(nh))
                        if finish:
                            finish.dve(dve, n, emptied)
                        for s in range(U + lag_v):
                            if s < U:
                                nk = units[s].nk
                                dve.wait_ge(scored.sem, scored.at(n, s + 1))
                                if ipa:
                                    nc.vector.tensor_reduce(negmax[:, U + s:U + s + 1],
                                                            scores[:, s % slots, nk - IPA:nk], AX.X, ALU.max,
                                                            negate=True)
                                    nc.vector.tensor_reduce(negmax[:, s:s + 1], scores[:, s % slots, 0:nk - IPA],
                                                            AX.X, ALU.max, negate=True).then_inc(maxed.sem, 1)
                                else:
                                    nc.vector.tensor_reduce(negmax[:, s:s + 1], scores[:, s % slots, 0:nk], AX.X,
                                                            ALU.max, negate=True).then_inc(maxed.sem, 1)
                            t = s - 1
                            if ipa and 0 <= t < U:
                                nk = units[t].nk
                                dve.wait_ge(exped.sem, exped.at(n, t + 1))
                                nc.vector.reciprocal(rowinv[:, U + t:U + t + 1],
                                                     rowsum[:, U + t:U + t + 1]).then_inc(rescaled.sem, 1)
                                dve.wait_ge(rescaled.sem, rescaled.at(n, 2 * t + 1))
                                tail_p = probs[:, t % 3, nk - IPA:nk]
                                nc.vector.tensor_scalar(tail_p, tail_p, rowsum[:, t:t + 1],
                                                        rowinv[:, U + t:U + t + 1], ALU.mult,
                                                        ALU.mult).then_inc(rescaled.sem, 1)
                            t = s - 2
                            if 0 <= t < U:
                                dve.wait_ge(exped.sem, exped.at(n, t + 1))
                                nc.vector.reciprocal(rowinv[:, t:t + 1], rowsum[:, t:t + 1]).then_inc(inverse.sem, 1)
                                move_turned(dve, 1, n, t)
                            t = s - lag_v
                            if 0 <= t < U:
                                dve.wait_ge(inverse.sem, inverse.at(n, t + 1))
                                dve.wait_ge(summed.sem, summed.at(n, t + 1))
                                units[t].store(weighted(t), rowinv[:, t:t + 1], i).then_inc(stored.sem, 1)
                        empty(dve, "dve", n, range(nh, len(chunks)))

        HALF = BANK

        def mm_T(w, srcT, c0, k=P, m=P, cols_n=HALF):
            return lambda o: nc.tensor.matmul(o[0:m, 0:cols_n], w, srcT[0:k, c0:c0 + cols_n], start=True, stop=True)

        def mm_tok(srcT, w, t0, k=P, m=D, bias=None, tiles=4):
            def f(o):
                for q in range(tiles):
                    last = nc.tensor.matmul(o[:, q * m:(q + 1) * m], srcT[0:k, (t0 + q) * P:(t0 + q + 1) * P], w,
                                            start=True, stop=bias is None)
                    if bias is not None:
                        last = nc.tensor.matmul(o[:, q * m:(q + 1) * m], ones[0:1, :], bias, start=False, stop=True)
                return last
            return f

        def tiles_of(o, m=D, n=4):
            return o[:, 0:n * m].rearrange("p (t d) -> p t d", t=n)

        def turn_chunk(engine, src, t0, dstT):
            def f(o):
                for q in range(4):
                    last = nc.tensor.transpose(o[:, q * P:(q + 1) * P], src[:, t0 + q, :], ident[:, :])
                return last
            return Chunk(engine, f, lambda o: copy(engine, dstT[:, t0 * P:(t0 + 4) * P], o))

        def add_to(acc, t0):
            return lambda o: nc.vector.tensor_tensor(acc[:, t0:t0 + 4, :], acc[:, t0:t0 + 4, :], tiles_of(o), ALU.add)

        def out_chunks(first, acc, w, bias=None):
            return [turn_chunk("act", heads_out, 0, outT), turn_chunk("dve", heads_out, 4, outT),
                    Chunk("dve", mm_tok(outT, w, 0, bias=bias), add_to(acc, 0), after=(first,)),
                    Chunk("dve", mm_tok(outT, w, 4, bias=bias), add_to(acc, 4), after=(first + 1,))]

        ENG = ("act", "dve")

        def self_chunks(qs=1.0, srcT=xnT, first=0, vbias=None, qbias=None, kbias=None, m=D, mv=D):
            out_list = []
            for w, dst, s, bcol in ((wq, qT[:, 0, :], qs, qbias), (wk, kT, 1.0, kbias)):
                for c in range(T // HALF):
                    e = ENG[c % 2]
                    d = dst[0:m, c * HALF:(c + 1) * HALF]
                    if bcol is None:
                        f = lambda o, e=e, d=d, s=s: copy(e, d, o[0:m, :], s)
                    else:
                        f = lambda o, d=d, s=s, bcol=bcol: nc.vector.tensor_scalar(d, o[0:m, :], bcol, s, ALU.add, ALU.mult)
                        e = "dve"
                    out_list.append(Chunk(e, mm_T(w[:, 0:m], srcT, c * HALF, m=m), f))
            for t in range(0, NT, 4):
                e = ENG[t // 4 % 2]
                out_list.append(Chunk(e, mm_tok(srcT, wv[:, 0:mv], t, bias=vbias),
                                      lambda o, e=e, t=t: copy(e, V[:, t:t + 4, :], tiles_of(o))))
            return out_list

        def score_mm(segments):
            def f(o):
                for c0, w, q, k, mk in segments:
                    last = nc.tensor.matmul(o[:, c0:c0 + w], q, k, start=True, stop=not mk)
                    for j, (ml, mr, m0, mw) in enumerate(mk):
                        last = nc.tensor.matmul(o[:, m0:m0 + mw], ml, mr, start=False, stop=(j == len(mk) - 1))
                return last
            return f

        CAUSAL, NOT_BEFORE, BAND, BAND_PREV = range(4)

        def block_mask(kind, c0):
            return (ident16[:, :], masks16[:, kind, :], c0, P)

        def self_units(q_of, k_of, v_of, store_of, kind, heads, width):
            us = []
            for h in range(heads):
                for b in range(B):
                    for qt in range(QT):
                        t = b * QT + qt
                        nk, mk = N, []
                        if kind == "causal":
                            nk, mk = (qt + 1) * P, [block_mask(CAUSAL, qt * P)]
                        elif kind == "near":
                            mk = [block_mask(CAUSAL, P)] if qt == 0 else [block_mask(NOT_BEFORE, 0)]
                        elif kind == "window":
                            nk = (qt + 1) * P
                            mk = [block_mask(BAND, 0)] if qt == 0 else [block_mask(BAND_PREV, 0), block_mask(BAND, P)]
                        us.append(Unit(nk, score_mm([(0, nk, q_of(h, t), k_of(h, b * N, nk), mk)]),
                                       lambda j, i, h=h, b=b: v_of(h, b * QT + j, i), store_of(h, t), width))
            return us

        def cross_units(q_of, k_of, v_of, store_of, heads, width):
            us = []
            for h in range(heads):
                for b in range(B):
                    for qt in range(QT):
                        t = b * QT + qt
                        us.append(Unit(M, score_mm([(0, M, q_of(h, t), k_of(h, b * M, M), [])]),
                                       lambda j, i, h=h, b=b: v_of(h, b * KT + j, i), store_of(h, t), width))
            return us

        def pair_rows(h):
            return slice(h * DH, (h + 1) * DH)

        pair_q = lambda h, t: qT[pair_rows(h), 0, t * P:(t + 1) * P]
        pair_k = lambda h, k0, w: kT[pair_rows(h), k0:k0 + w]
        pair_v = lambda h, t, i: V[:, t, pair_rows(h)]

        def pair_store(h, t):
            return lambda o, r, i: nc.vector.tensor_scalar(heads_out[:, t, pair_rows(h)], o, r, None, ALU.mult)

        slot_q = lambda h, t: qM[:, h, t * P:(t + 1) * P]
        all_k = lambda h, k0, w: kT[:, k0:k0 + w]
        slot_v = lambda h, t, i: V[:, t, bass.ds(i * (2 * HS) + h * HS, HS)]

        def slot_store(h, t):
            return lambda o, r, i: nc.vector.tensor_scalar(heads_out[:, t, bass.ds(i * (2 * HS) + h * HS, HS)], o, r,
                                                           None, ALU.mult)

        def add_store(h, t):
            return lambda o, r, i: nc.vector.scalar_tensor_tensor(x[:, t, :], o, r, x[:, t, :], ALU.mult, ALU.add)

        def pair_of(w, i):
            return w[:, bass.ds(i * D, D)]

        def pair_rows_of(w, i):
            return w[bass.ds(i * D, D), :]

        def setup():
            load([(x[:, :, :], a["x"].rearrange("b (t p) d -> p (b t) d", p=P)),
                  (ctx_tok[:, :, :], a["ctx_768"].rearrange("b (t p) d -> p (b t) d", p=P)),
                  (ident[:, :], a["c_ident"]), (masks[:, :, :], a["c_masks"]), (head_mask[:, :], a["c_head_mask"]),
                  (rot8[:, :], a["c_rot8"]), (rot64[:, :], a["c_rot64"]), (block64[:, :], a["c_block64"])])
            made = signal("consts_made", 4)
            with nc.Block() as block:
                @block.vector
                def _(dve):
                    nc.vector.tensor_copy(ident16[:, :], ident[:, :]).then_inc(made.sem, 1)
                    nc.vector.tensor_copy(masks16[:, :, :], masks[:, :, :]).then_inc(made.sem, 1)
                    nc.vector.memset(ones[:, :], 1.0).then_inc(made.sem, 1)
                    nc.vector.memset(ones16[:, :], 1.0).then_inc(made.sem, 1)
                    dve.wait_ge(made.sem, made.at(0, 4))

            def turn(t):
                def f(o):
                    for q in range(4):
                        last = nc.tensor.transpose(o[0:C, q * P:(q + 1) * P], ctx_tok[:, t + q, :], ident[:, :])
                    return last
                e = ENG[t // 4 % 2]
                return Chunk(e, f, lambda o: copy(e, ctxT[0:C, t * P:(t + 4) * P], o[0:C, :]))
            chunk_block([turn(t) for t in range(0, MT, 4)])

        def l0_attn():
            load([(wq[:, :], a["L0_attn_W"][:, 0:D]), (wk[:, :], a["L0_attn_W"][:, D:2 * D]),
                  (wv[:, :], a["L0_attn_W"][:, 2 * D:3 * D]),
                  (columns(0), col_of(a["L0_attn_b"][0:D])), (columns(1), col_of(a["L0_attn_b"][D:2 * D])),
                  (brow[0:1, 0:D], row_of(a["L0_attn_b"][2 * D:3 * D]))])
            norm(x, NT, D, z, xnT)
            attention(self_units(lambda h, t: qT[:, 0, t * P:(t + 1) * P], all_k, lambda h, t, i: V[:, t, :],
                                 add_store, "all", 1, D),
                      head=self_chunks(qs=float(D) ** -0.5, qbias=columns(0), kbias=columns(1), vbias=brow[0:1, 0:D]))

        def l0_xattn():
            sub = ExitStack()
            with sub:
                def sbl(name, shape):
                    return sub.enter_context(nc.sbuf_tensor("lora_" + name, shape, F32))
                low = {}
                for nm, k in (("q", D), ("k", C), ("v", C)):
                    low[nm] = (sbl(f"{nm}_downT", [RANK, k]), sbl(f"{nm}_up", [RANK, D]), k)
                o_downT, o_up = sbl("o_downT", [RANK, D]), sbl("o_up", [RANK, D])
                raw = {nm: sbl(f"{nm}_raw", [P, D]) for nm in "qkvo"}
                wki, wvi = sbl("wk_ipa", [C, D]), sbl("wv_ipa", [C, D])
                org, img = sbl("org_ctxT", [C, B, P]), sbl("img_ctxT", [C, B, P])
                load([(columns(j), a[f"L0_xattn_{nm}_alpha"].rearrange("(p o) -> p o", o=1).to_broadcast([P, 1]))
                      for j, nm in enumerate("qkvo")]
                     + [(low[nm][0][:, :], a[f"L0_xattn_{nm}_downT"]) for nm in "qkv"]
                     + [(o_up[:, :], a["L0_xattn_o_up"]), (brow[0:1, 0:D], row_of(a["L0_xattn_bo"]))])
                made = signal("ipa_made", 5)
                last_tiles = ctxT[0:C, :].rearrange("c (b t k) -> c b t k", b=B, t=KT)[:, :, KT - 1, :]
                with nc.Block() as block:
                    @block.vector
                    def _(dve):
                        nc.vector.memset(org[:, :, :], 0.0).then_inc(made.sem, 1)
                        nc.vector.memset(img[:, :, :], 0.0).then_inc(made.sem, 1)
                        dve.wait_ge(made.sem, made.at(0, 2))
                        nc.vector.tensor_copy(org[:, :, 0:P - IPA], last_tiles[:, :, 0:P - IPA]).then_inc(made.sem, 1)
                        nc.vector.tensor_copy(img[:, :, P - IPA:P], last_tiles[:, :, P - IPA:P]).then_inc(made.sem, 1)
                        nc.vector.tensor_scalar(columns(4, 8), columns(0, 4), 1.0 / RANK, None,
                                                ALU.mult).then_inc(made.sem, 1)
                        dve.wait_ge(made.sem, made.at(0, 5))
                norm(x, NT, D, z, xnT)

                def head_loads(sp, i, s):
                    for nm in "qkv":
                        sp.dma_start(raw[nm][0:low[nm][2], :], pair_of(a[f"L0_xattn_W{nm}"], i)).then_inc(s, 16)
                        sp.dma_start(low[nm][1][:, :], pair_of(a[f"L0_xattn_{nm}_up"], i)).then_inc(s, 16)
                    sp.dma_start(wki[:, :], pair_of(a["L0_xattn_Wk_ipa"], i)).then_inc(s, 16)
                    sp.dma_start(wvi[:, :], pair_of(a["L0_xattn_Wv_ipa"], i)).then_inc(s, 16)

                def tail_loads(sp, i, s):
                    sp.dma_start(raw["o"][:, :], pair_rows_of(a["L0_xattn_Wo"], i)).then_inc(s, 16)
                    sp.dma_start(o_downT[:, :], pair_of(a["L0_xattn_o_downT"], i)).then_inc(s, 16)

                def fold(nm, j, dst):
                    k = P if nm in "qo" else C
                    down, up = (o_downT, o_up) if nm == "o" else low[nm][:2]
                    return Chunk("dve", lambda o: nc.tensor.matmul(o[0:k, 0:D], down[:, 0:k], up[:, :], start=True, stop=True),
                                 lambda o: nc.vector.scalar_tensor_tensor(dst[0:k, :], o[0:k, 0:D], cols[0:k, 4 + j:5 + j],
                                                                          raw[nm][0:k, :], ALU.mult, ALU.add))

                head = [fold("q", 0, wq), fold("k", 1, wk), fold("v", 2, wv)]
                for c in range(2):
                    e = ENG[c % 2]
                    head.append(Chunk(e, mm_T(wq[:, :], xnT, c * HALF),
                                      lambda o, e=e, c=c: copy(e, qT[:, 0, c * HALF:(c + 1) * HALF], o, DH ** -0.5),
                                      after=(0,)))
                for b in range(B):
                    e = ENG[b % 2]

                    def keys(o, b=b):
                        nc.tensor.matmul(o[:, 0:M - IPA], wk[0:C, :], ctxT[0:C, b * M:(b + 1) * M - IPA],
                                         start=True, stop=True)
                        return nc.tensor.matmul(o[:, M - IPA:M], wki[:, :], ctxT[0:C, (b + 1) * M - IPA:(b + 1) * M],
                                                start=True, stop=True)
                    head.append(Chunk(e, keys, lambda o, e=e, b=b: copy(e, kT[:, b * M:(b + 1) * M], o), after=(1,)))
                for b in range(B):
                    e = ENG[b % 2]

                    def vals(o, b=b):
                        for q in range(KT - 1):
                            nc.tensor.matmul(o[:, q * D:(q + 1) * D], ctxT[0:C, b * M + q * P:b * M + (q + 1) * P],
                                             wv[0:C, :], start=True, stop=True)
                        nc.tensor.matmul(o[:, (KT - 1) * D:KT * D], org[:, b, :], wv[0:C, :], start=True, stop=False)
                        return nc.tensor.matmul(o[:, (KT - 1) * D:KT * D], img[:, b, :], wvi[:, :], start=False, stop=True)
                    head.append(Chunk(e, vals, lambda o, e=e, b=b: copy(e, V[:, b * KT:(b + 1) * KT, :], tiles_of(o)),
                                      after=(2,)))
                nh = len(head)
                tail = [fold("o", 3, wo)] + out_chunks(nh + 1, x, wo[:, :])
                for c in tail[3:]:
                    c.after = tuple(c.after) + (nh,)
                attention(cross_units(pair_q, pair_k, pair_v, pair_store, 2, DH), iters=PAIRS, head=head, tail=tail,
                          head_loads=head_loads, tail_loads=tail_loads, loads=(8, 2), ipa=True)
                add_row(x, brow[0:1, 0:D])

        def add_row(acc, row):
            chunk_block([Chunk("dve", (lambda o: [nc.tensor.matmul(o[:, q * D:(q + 1) * D], ones[0:1, :], row, start=True,
                                                                   stop=True) for q in range(4)][-1]), add_to(acc, t))
                         for t in range(0, NT, 4)])

        def l0_ffn():
            sub = ExitStack()
            with sub:
                def sbl(name, shape):
                    return sub.enter_context(nc.sbuf_tensor("gqa_" + name, shape, F32))
                cos, sin = sbl("cos8", [P, N]), sbl("sin8", [P, N])
                gate = sbl("gate_w", [P, EXPERTS])
                sums = sbl("rope_sum", [P, 2, T])
                load([(wq[:, :], a["L0_ffn_wqT"]), (wk[:, :], a["L0_ffn_wkT"]), (wv[:, :], a["L0_ffn_wvT"]),
                      (wo[:, :], a["L0_ffn_woT"]), (columns(0), col_of(a["L0_ffn_ln1_w"])),
                      (columns(1), col_of(a["L0_ffn_ln2_w"])), (cos[:, :], a["c_cos8"]), (sin[:, :], a["c_sin8"]),
                      (gate[:, :], a["L0_ffn_gate_wT"])])
                norm(x, NT, D, xin)
                norm(xin, NT, D, z, xnT, rms=True, gain=columns(0))
                chunks = []
                for s, w in ((0, wq), (1, wk)):
                    for c in range(2):
                        chunks.append(Chunk("act", mm_T(w[:, :], xnT, c * HALF),
                                            lambda o, s=s, c=c: copy("act", sums[:, s, c * HALF:(c + 1) * HALF], o,
                                                                     (HS ** -0.5, 1.0)[s])))
                for t in (0, 4):
                    chunks.append(Chunk("dve", mm_tok(xnT, wv[:, :], t), lambda o, t=t: copy("dve", V[:, t:t + 4, :], tiles_of(o))))
                wave = lambda tab: tab[:, :].rearrange("p (o n) -> p o n", o=1).to_broadcast([P, HALF // N, N])
                dsts = (qT[:, 0, :], kT)
                for s in range(2):
                    for c in range(2):
                        chunks.append(Chunk("dve", mm_T(rot8[:, :], sums[:, s, :], c * HALF),
                                            lambda o, s=s, c=c: nc.vector.tensor_tensor(
                                                dsts[s][:, c * HALF:(c + 1) * HALF].rearrange("p (b n) -> p b n", n=N),
                                                o.rearrange("p (b n) -> p b n", n=N), wave(sin), ALU.mult),
                                            after=(2 * s + c,)))
                chunk_block(chunks)
                turned_q = signal("rope_done", 4)
                with nc.Block() as block:
                    @block.vector
                    def _(dve):
                        for s in range(2):
                            v4 = sums[:, s, :].rearrange("p (b n) -> p b n", n=N)
                            nc.vector.tensor_tensor(v4, v4, cos[:, :].rearrange("p (o n) -> p o n", o=1).to_broadcast([P, B, N]),
                                                    ALU.mult).then_inc(turned_q.sem, 1)
                        for s in range(2):
                            dve.wait_ge(turned_q.sem, turned_q.at(0, s + 1))
                            nc.vector.tensor_tensor(dsts[s][:, 0:T], dsts[s][:, 0:T], sums[:, s, :],
                                                    ALU.add).then_inc(turned_q.sem, 1)
                attention(self_units(slot_q, all_k, slot_v, slot_store, "causal", 2, HS), iters=PAIRS, mask_heads=True)
                chunk_block(out_chunks(0, xin, wo[:, :]))
                norm(xin, NT, D, z, xnT, rms=True, gain=columns(1))
                experts(gate)
                add_all(x, xin)

        def add_all(acc, src):
            added = signal("added_all", 1)
            with nc.Block() as block:
                @block.vector
                def _(dve):
                    nc.vector.tensor_tensor(acc[:, :, :], acc[:, :, :], src[:, :, :], ALU.add).then_inc(added.sem, 1)
                    dve.wait_ge(added.sem, added.at(0, 1))

        def experts(gate):
            sub = ExitStack()
            with sub:
                def sbl(name, shape):
                    return sub.enter_context(nc.sbuf_tensor("moe_" + name, shape, F32))
                logit = sbl("logit", [P, NT, EXPERTS])
                prob = sbl("gate_prob", [P, NT, EXPERTS])
                best = sbl("gate_best", [P, NT, 8])
                above = sbl("gate_above", [P, NT, EXPERTS])
                equal = sbl("gate_equal", [P, NT, EXPERTS])
                before = sbl("gate_before", [P, NT, EXPERTS])
                room = sbl("gate_room", [P, NT, 1])
                total = sbl("gate_total", [P, NT, 1])
                share = sbl("gate_share", [P, NT, EXPERTS])
                w13 = sbl("w13", [P, 2 * FFN])
                w2 = sbl("w2", [P, 2, D])
                gated = sbl("gated", [P, 2, T])
                silu = sbl("silu", [P, 2, BANK])
                hT = xnT

                def logits(o):
                    for t in range(NT):
                        last = nc.tensor.matmul(o[:, t * EXPERTS:(t + 1) * EXPERTS], hT[:, t * P:(t + 1) * P], gate[:, :],
                                                start=True, stop=True)
                    return last
                chunk_block([Chunk("dve", logits, lambda o: nc.vector.tensor_copy(
                    logit[:, :, :], o[:, 0:NT * EXPERTS].rearrange("p (t e) -> p t e", e=EXPERTS)))])

                step = signal("gate_step", 64)
                exped = signal("gate_exp", 1)
                with nc.Block() as block:
                    @block.vector
                    def _(dve):
                        done = [0]

                        def then(ins):
                            done[0] += 1
                            ins.then_inc(step.sem, 1)
                            dve.wait_ge(step.sem, step.at(0, done[0]))
                        wide = lambda v: v[:, :, 0:1].to_broadcast([P, NT, EXPERTS])
                        then(nc.vector.tensor_reduce(room[:, :, :], logit[:, :, :], AX.X, ALU.max))
                        then(nc.vector.tensor_tensor(logit[:, :, :], logit[:, :, :], wide(room), ALU.subtract))
                        dve.wait_ge(exped.sem, exped.at(0, 1))
                        then(nc.vector.tensor_reduce(total[:, :, :], prob[:, :, :], AX.X, ALU.add))
                        then(nc.vector.reciprocal(room[:, :, :], total[:, :, :]))
                        then(nc.vector.tensor_tensor(prob[:, :, :], prob[:, :, :], wide(room), ALU.mult))
                        for t in range(NT):
                            then(nc.vector.max(best[:, t, :], prob[:, t, :]))
                        second = best[:, :, 1:2].to_broadcast([P, NT, EXPERTS])
                        then(nc.vector.tensor_tensor(above[:, :, :], prob[:, :, :], second, ALU.is_gt))
                        then(nc.vector.tensor_tensor(equal[:, :, :], prob[:, :, :], second, ALU.is_equal))
                        then(nc.vector.tensor_reduce(room[:, :, :], above[:, :, :], AX.X, ALU.add))
                        then(nc.vector.tensor_scalar(room[:, :, :], room[:, :, :], -1.0, 2.0, ALU.mult, ALU.add))
                        then(nc.vector.memset(before[:, :, 0:1], 0.0))
                        for e in range(1, EXPERTS):
                            then(nc.vector.tensor_tensor(before[:, :, e:e + 1], before[:, :, e - 1:e],
                                                         equal[:, :, e - 1:e], ALU.add))
                        then(nc.vector.tensor_tensor(before[:, :, :], before[:, :, :], wide(room), ALU.is_lt))
                        then(nc.vector.tensor_tensor(equal[:, :, :], equal[:, :, :], before[:, :, :], ALU.mult))
                        then(nc.vector.tensor_tensor(above[:, :, :], above[:, :, :], equal[:, :, :], ALU.add))
                        then(nc.vector.tensor_tensor(share[:, :, :], prob[:, :, :], above[:, :, :], ALU.mult))
                        then(nc.vector.tensor_tensor(total[:, :, :], best[:, :, 0:1], best[:, :, 1:2], ALU.add))
                        then(nc.vector.reciprocal(room[:, :, :], total[:, :, :]))
                        then(nc.vector.tensor_tensor(share[:, :, :], share[:, :, :], wide(room), ALU.mult))

                    @block.scalar
                    def _(act):
                        act.wait_ge(step.sem, step.at(0, 2))
                        nc.scalar.activation(prob[:, :, :], logit[:, :, :], ACT.Exp).then_inc(exped.sem, 1)

                w_in = signal("expert_up_in", 1, EXPERTS, 16)
                w2_in = signal("expert_down_in", 1, EXPERTS, 16)
                up = signal("expert_up", 4, EXPERTS)
                silued = signal("expert_silu", 4, EXPERTS)
                gated_up = signal("expert_gated", 4, EXPERTS)
                down = signal("expert_down", 2, EXPERTS)
                added = signal("expert_added", NT, EXPERTS)
                w13_d, w2_d = a["L0_ffn_w13T"], a["L0_ffn_w2T"]
                with ps("gu", [P, 2, 2, BANK]) as gu, ps("eo", [P, 2, BANK]) as eo, \
                        nc.Block() as block:
                    @block.sync
                    def _(sp):
                        def fetch_up(e):
                            sp.dma_start(w13[:, :], w13_d[:, bass.ds(e * 2 * FFN, 2 * FFN)]).then_inc(w_in.sem, 16)

                        def fetch_down(e):
                            sp.dma_start(w2[:, :, :], w2_d[:, bass.ds(e * 2 * D, 2 * D)].rearrange("p (f d) -> p f d", f=2)).then_inc(w2_in.sem, 16)
                        fetch_up(0)
                        fetch_down(0)
                        with sp.Fori(0, EXPERTS - 1) as e:
                            sp.wait_ge(up.sem, up.at(e, 4))
                            fetch_up(e + 1)
                            sp.wait_ge(down.sem, down.at(e, 2))
                            fetch_down(e + 1)

                    @block.tensor
                    def _(pe):
                        with pe.Fori(0, EXPERTS) as e:
                            pe.wait_ge(w_in.sem, w_in.at(e, 1))
                            for c in range(4):
                                f, th = c // 2, c % 2
                                pe.wait_ge(gated_up.sem, gated_up.at(e, max(0, c - 1)))
                                for g in range(2):
                                    last = nc.tensor.matmul(gu[:, c % 2, g, :], w13[:, g * FFN + f * P:g * FFN + (f + 1) * P],
                                                            hT[:, th * HALF:(th + 1) * HALF], start=True, stop=True)
                                last.then_inc(up.sem, 1)
                            pe.wait_ge(gated_up.sem, gated_up.at(e, 4))
                            pe.wait_ge(w2_in.sem, w2_in.at(e, 1))
                            pe.wait_ge(added.sem, added.at(e, 0))
                            for g in range(2):
                                for q in range(4):
                                    t = 4 * g + q
                                    for f in range(2):
                                        last = nc.tensor.matmul(eo[:, g, q * D:(q + 1) * D], gated[:, f, t * P:(t + 1) * P],
                                                                w2[:, f, :], start=(f == 0), stop=(f == 1))
                                last.then_inc(down.sem, 1)

                    @block.scalar
                    def _(act):
                        with act.Fori(0, EXPERTS) as e:
                            for c in range(4):
                                act.wait_ge(up.sem, up.at(e, c + 1))
                                act.wait_ge(gated_up.sem, gated_up.at(e, max(0, c - 1)))
                                nc.scalar.activation(silu[:, c % 2, :], gu[:, c % 2, 0, :], ACT.Silu).then_inc(silued.sem, 1)

                    @block.vector
                    def _(dve):
                        with dve.Fori(0, EXPERTS) as e:
                            dve.wait_ge(down.sem, down.at(e, 0))
                            for c in range(4):
                                f, th = c // 2, c % 2
                                dve.wait_ge(silued.sem, silued.at(e, c + 1))
                                nc.vector.tensor_tensor(gated[:, f, th * HALF:(th + 1) * HALF], silu[:, c % 2, :],
                                                        gu[:, c % 2, 1, :], ALU.mult).then_inc(gated_up.sem, 1)
                            for t in range(NT):
                                dve.wait_ge(down.sem, down.at(e, t // 4 + 1))
                                nc.vector.scalar_tensor_tensor(xin[:, t, :], eo[:, t // 4, (t % 4) * D:(t % 4 + 1) * D],
                                                               share[:, t, bass.ds(e, 1)], xin[:, t, :], ALU.mult,
                                                               ALU.add).then_inc(added.sem, 1)

        def l1_attn():
            w = a["L1_attn_Wqkv"]
            load([(wq[:, :], w[:, 0:D]), (wk[:, :], w[:, D:2 * D]), (wv[:, :], w[:, 2 * D:3 * D]),
                  (columns(0), col_of(a["L1_attn_bqkv"][0:D])), (columns(1), col_of(a["L1_attn_bqkv"][D:2 * D])),
                  (brow[0:1, 0:D], row_of(a["L1_attn_bqkv"][2 * D:3 * D])),
                  (brow[0:1, D:2 * D], row_of(a["L1_attn_bout"])), (wo[:, :], a["L1_attn_Wout"])])
            norm(x, NT, D, z, xnT)
            chunk_block(self_chunks(qs=float(D) ** -0.5, qbias=columns(0), kbias=columns(1), vbias=brow[0:1, 0:D]))
            attention(self_units(slot_q, all_k, slot_v, slot_store, "near", 2, HS), iters=PAIRS, mask_heads=True)
            chunk_block(out_chunks(0, x, wo[:, :], bias=brow[0:1, D:2 * D]))

        def context_chunks(qs, qbias=None, kbias=None, vbias=None):
            cs = []
            for c in range(2):
                d = qT[:, 0, c * HALF:(c + 1) * HALF]
                if qbias is None:
                    cs.append(Chunk(ENG[c], mm_T(wq[:, :], xnT, c * HALF), lambda o, c=c, d=d: copy(ENG[c], d, o, qs)))
                else:
                    cs.append(Chunk("dve", mm_T(wq[:, :], xnT, c * HALF),
                                    lambda o, d=d: nc.vector.tensor_scalar(d, o, qbias, qs, ALU.add, ALU.mult)))
            for b in range(B):
                e, d = ENG[b % 2], kT[:, b * M:(b + 1) * M]
                cs.append(Chunk(e, mm_T(wk[0:C, :], ctxT, b * M, k=C),
                                (lambda o, e=e, d=d: copy(e, d, o)) if kbias is None else
                                (lambda o, e=e, d=d: affine(e, d, o, 1.0, kbias))))
            for b in range(B):
                e = ENG[b % 2]
                cs.append(Chunk(e, mm_tok(ctxT, wv[0:C, :], b * KT, k=C, bias=vbias),
                                lambda o, e=e, b=b: copy(e, V[:, b * KT:(b + 1) * KT, :], tiles_of(o))))
            return cs

        def l1_xattn():
            p = lambda s: a["L1_xattn_" + s]
            load([(wq[:, :], p("wq")), (wk[0:C, :], p("wk")), (wv[0:C, :], p("wv")), (wo[:, :], p("wo")),
                  (columns(0), col_of(p("bq"))), (columns(1), col_of(p("bk"))), (brow[0:1, 0:D], row_of(p("bv"))),
                  (brow[0:1, D:2 * D], row_of(p("bo")))])
            norm(x, NT, D, z, xnT)
            chunk_block(context_chunks(HS ** -0.5, columns(0), columns(1), brow[0:1, 0:D]))
            attention(cross_units(slot_q, all_k, slot_v, slot_store, 2, HS), iters=PAIRS, mask_heads=True)
            chunk_block(out_chunks(0, x, wo[:, :], bias=brow[0:1, D:2 * D]))

        def l1_ffn():
            load([(wq[:, :], a["L1_ffn_W_rT"]), (wk[:, :], a["L1_ffn_W_kT"]), (wv[:, :], a["L1_ffn_W_vT"]),
                  (columns(0), col_of(a["L1_ffn_mu_r"])), (columns(1), col_of(a["L1_ffn_mu_k"]))])
            norm(x, NT, D, z, xnT)
            mixed = signal("mixed", 9)
            prev = V[:, 0:NT, :].rearrange("p t d -> p (t d)").rearrange("p (b n) -> p b n", b=B)
            now = xnT[:, :].rearrange("p (b n) -> p b n", b=B)
            r, k, act_k = qT[:, 0, :], qT[:, 1, :], kT[:, 0:T]
            with nc.Block() as block:
                @block.vector
                def _(dve):
                    nc.vector.memset(prev[:, :, 0:1], 0.0).then_inc(mixed.sem, 1)
                    nc.vector.tensor_copy(prev[:, :, 1:N], now[:, :, 0:N - 1]).then_inc(mixed.sem, 1)
                    nc.vector.tensor_scalar(columns(2, 4), columns(0, 2), -1.0, 1.0, ALU.mult, ALU.add).then_inc(mixed.sem, 1)
                    dve.wait_ge(mixed.sem, mixed.at(0, 3))
                    flat = V[:, 0:NT, :].rearrange("p t d -> p (t d)")
                    nc.vector.tensor_scalar(r, flat, columns(2), None, ALU.mult).then_inc(mixed.sem, 1)
                    nc.vector.tensor_scalar(k, flat, columns(3), None, ALU.mult).then_inc(mixed.sem, 1)
                    dve.wait_ge(mixed.sem, mixed.at(0, 5))
                    nc.vector.scalar_tensor_tensor(r, xnT[:, :], columns(0), r, ALU.mult, ALU.add).then_inc(mixed.sem, 2)
                    nc.vector.scalar_tensor_tensor(k, xnT[:, :], columns(1), k, ALU.mult, ALU.add).then_inc(mixed.sem, 2)
            sig = heads_out
            chunks = []
            for t in (0, 4):
                chunks.append(Chunk("act", mm_tok(r, wq[:, :], t),
                                    lambda o, t=t: nc.scalar.activation(sig[:, t:t + 4, :], tiles_of(o), ACT.Sigmoid)))
            for c in range(2):
                chunks.append(Chunk("dve", mm_T(wk[:, :], k, c * HALF),
                                    lambda o, c=c: nc.vector.tensor_scalar(outT[:, c * HALF:(c + 1) * HALF], o, 0.0, None, ALU.max)))
            chunk_block(chunks)
            squared = signal("squared", 1)
            with nc.Block() as block:
                @block.scalar
                def _(act):
                    nc.scalar.activation(act_k, outT[:, :], ACT.Square).then_inc(squared.sem, 1)
            chunk_block([Chunk("dve", mm_tok(kT, wv[:, :], t),
                               lambda o, t=t: nc.vector.tensor_tensor(z[:, t:t + 4, :], sig[:, t:t + 4, :], tiles_of(o), ALU.mult))
                         for t in (0, 4)])
            add_all(x, z)

        def wide_loads(pre, wo_name):
            def head_loads(sp, i, s):
                for nm, buf, k in pre:
                    sp.dma_start(buf[0:k, :], pair_of(a[nm], i)).then_inc(s, 16)

            def tail_loads(sp, i, s):
                sp.dma_start(wo[:, :], pair_rows_of(a[wo_name], i)).then_inc(s, 16)
            return dict(head_loads=head_loads, tail_loads=tail_loads, loads=(len(pre), 1))

        def l2_attn():
            norm(x, NT, D, z, xnT)
            head = self_chunks()
            attention(self_units(pair_q, pair_k, pair_v, pair_store, "causal", 2, DH), iters=PAIRS, head=head,
                      tail=out_chunks(len(head), x, wo[:, :]),
                      **wide_loads((("L2_attn_QT", wq, D), ("L2_attn_KT", wk, D), ("L2_attn_VT", wv, D)), "L2_attn_OT"))

        def l3_xattn():
            load([(brow[0:1, 0:D], row_of(a["L3_xattn_b_out"]))])
            norm(x, NT, D, z, xnT)
            head = context_chunks(DH ** -0.5)
            attention(cross_units(pair_q, pair_k, pair_v, pair_store, 2, DH), iters=PAIRS, head=head,
                      tail=out_chunks(len(head), x, wo[:, :]),
                      **wide_loads((("L3_xattn_w_q", wq, D), ("L3_xattn_w_k", wk, C), ("L3_xattn_w_v", wv, C)), "L3_xattn_w_out"))
            add_row(x, brow[0:1, 0:D])

        def l2_xattn():
            sub = ExitStack()
            with sub:
                def sbl(name, shape, dt=F32):
                    return sub.enter_context(nc.sbuf_tensor("latent_" + name, shape, dt))
                p = lambda s: a["L2_xattn_" + s]
                wlk, wlv = sbl("wlk", [P, D]), sbl("wlv", [P, D])
                ctx_z, ctx_nT = sbl("ctx_z", [P, MT, C]), sbl("ctx_nT", [P, B * M])
                keep8, keep = sbl("keep8", [1, B * M], U8), sbl("keep", [1, B * M], BF16)
                squares, root = sbl("squares", [P, 4 * T]), sbl("root", [P, 4 * T])
                two = lambda v: v.rearrange("(o d) -> o d", o=1)
                load([(wq[:, :], p("WqT")), (wk[0:C, :], p("WkT")), (wv[0:C, :], p("WvT")), (wlk[:, :], p("WlkT")),
                      (wlv[:, :], p("WlvT")), (wo[:, :], p("WoT")), (cols[0:C, 0:1], col_of(p("ln_x_g"))),
                      (cols[0:C, 1:2], col_of(p("ln_x_b"))), (columns(2), col_of(p("ln_l_g"))),
                      (columns(3), col_of(p("ln_l_b"))), (cols[0:DH, 4:5], col_of(p("qn_g"))),
                      (cols[DH:2 * DH, 4:5], col_of(p("qn_g"))), (cols[0:DH, 5:6], col_of(p("kn_g"))),
                      (cols[DH:2 * DH, 5:6], col_of(p("kn_g"))), (brow[0:1, 0:D], row_of(p("bo"))),
                      (keep8[:, :], a["mask_BxS2_bk0"])])
                kept = signal("mask_made", 2)
                with nc.Block() as block:
                    @block.vector
                    def _(dve):
                        nc.vector.tensor_scalar(keep[:, :], keep8[:, :], -1.0, -NEG, ALU.add, ALU.mult).then_inc(kept.sem, 1)
                        nc.vector.tensor_scalar(columns(4), columns(4), DH ** -0.5, None, ALU.mult).then_inc(kept.sem, 1)
                norm(ctx_tok, MT, C, ctx_z, ctx_nT, gain=columns(0), bias=columns(1))
                norm(x, NT, D, z)
                norm(z, NT, D, heads_out, xnT, gain=columns(2), bias=columns(3))

                k4 = kT[:, :].rearrange("p (b m) -> p b m", b=B)
                chunks = []
                q0 = [(qT[:, 0, c * HALF:(c + 1) * HALF], squares[:, c * HALF:(c + 1) * HALF],
                       mm_T(wq[:, :], xnT, c * HALF), None) for c in range(2)]
                sq4 = squares[:, T:4 * T].rearrange("p (b m) -> p b m", b=B)
                kc = [(k4[:, b, 0:M], sq4[:, b, 0:M], mm_T(wk[0:C, :], ctx_nT, b * M, k=C), None) for b in range(B)]
                kl = [(k4[:, 2 * c:2 * c + 2, M:M + N], sq4[:, 2 * c:2 * c + 2, M:M + N], mm_T(wlk[:, :], xnT, c * HALF), 2)
                      for c in range(2)]
                for dst, sq, mm, split in q0 + kc + kl:
                    def both(o, dst=dst, sq=sq, split=split):
                        o = o if split is None else o.rearrange("p (b n) -> p b n", b=split)
                        nc.scalar.activation(dst, o, ACT.Copy)
                        return nc.scalar.activation(sq, o, ACT.Square)
                    chunks.append(Chunk("act", mm, both))
                for b in range(B):
                    chunks.append(Chunk("dve", mm_tok(ctx_nT, wv[0:C, :], b * KT, k=C),
                                        lambda o, b=b: copy("dve", V[:, b * KT:(b + 1) * KT, :], tiles_of(o))))
                for t in (0, 4):
                    chunks.append(Chunk("dve", mm_tok(xnT, wlv[:, :], t),
                                        lambda o, t=t: copy("dve", V[:, MT + t:MT + t + 4, :], tiles_of(o))))
                chunk_block(chunks)
                chunk_block([Chunk("dve", mm_T(block64[:, :], squares, c * HALF),
                                   lambda o, c=c: nc.vector.tensor_scalar(root[:, c * HALF:(c + 1) * HALF], o, 1.0 / DH, 1e-16,
                                                                          ALU.mult, ALU.max))
                             for c in range(4 * T // HALF)])
                rooted, inverted, scaled = signal("qk_rooted", 4), signal("qk_inverted", 4), signal("qk_scaled", 4)
                with nc.Block() as block:
                    @block.scalar
                    def _(act):
                        for c in range(4):
                            v = root[:, c * T:(c + 1) * T]
                            nc.scalar.activation(v, v, ACT.Sqrt).then_inc(rooted.sem, 1)

                    @block.vector
                    def _(dve):
                        for c in range(4):
                            v = root[:, c * T:(c + 1) * T]
                            dve.wait_ge(rooted.sem, rooted.at(0, c + 1))
                            nc.vector.reciprocal(v, v).then_inc(inverted.sem, 1)
                            dve.wait_ge(inverted.sem, inverted.at(0, c + 1))
                            d = qT[:, 0, :] if c == 0 else kT[:, (c - 1) * T:c * T]
                            nc.vector.scalar_tensor_tensor(d, d, columns(4 if c == 0 else 5), v, ALU.mult,
                                                           ALU.mult).then_inc(scaled.sem, 1)
                us = []
                for h in range(2):
                    for b in range(B):
                        for qt in range(QT):
                            t = b * QT + qt
                            q = pair_q(h, t)
                            seg = [(0, M, q, k4[pair_rows(h), b, 0:M], [(ones16[0:1, :], keep[0:1, b * M:(b + 1) * M], 0, M)]),
                                   (M, N, q, k4[pair_rows(h), b, M:M + N], [])]
                            us.append(Unit(M + N, score_mm(seg),
                                           lambda j, i, h=h, b=b: V[:, b * KT + j if j < KT else MT + b * QT + j - KT, pair_rows(h)],
                                           pair_store(h, t), DH))
                attention(us, wide=2)
                chunk_block(out_chunks(0, x, wo[:, :], bias=brow[0:1, 0:D]))

        def l2_ffn():
            sub = ExitStack()
            with sub:
                def sbl(name, shape):
                    return sub.enter_context(nc.sbuf_tensor("fp4_" + name, shape, F32))
                FT = 3
                FP = [P, P, FP4_FFN - 2 * P]
                w_up = sbl("w_up", [P, 2 * FT, D])
                w_down = sbl("w_down", [P, FP4_FFN])
                wT = sbl("w_upT", [P, 2, FP4_FFN])
                wdT = sbl("w_downT", [P, FT, D])
                hid = sbl("hid", [P, NT, FP4_FFN])
                hidT = sbl("hidT", [P, FT, T])
                silu = sbl("silu", [P, NT, FP4_FFN])
                big = NT * FP4_FFN
                mag, sgn = sbl("mag", [P, big]), sbl("sgn", [P, big])
                amax, inv = sbl("amax", [P, big // FP4_BLOCK]), sbl("amax_inv", [P, big // FP4_BLOCK])
                cleared = signal("fp4_cleared", 1)
                with nc.Block() as block:
                    @block.vector
                    def _(dve):
                        nc.vector.memset(w_up[:, :, :], 0.0).then_inc(cleared.sem, 1)
                        dve.wait_ge(cleared.sem, cleared.at(0, 1))
                pairs = [(w_down[:, :], a["L2_ffn_w_down"])]
                for g, nm in enumerate(("L2_ffn_w_gate", "L2_ffn_w_up")):
                    for f in range(FT):
                        pairs.append((w_up[0:FP[f], g * FT + f, :], a[nm][f * P:f * P + FP[f], :]))
                load(pairs)

                def quantize(v, width):
                    nb = width // FP4_BLOCK
                    blocks = lambda t: t[:, 0:width].rearrange("p (n k) -> p n k", k=FP4_BLOCK)
                    of_block = lambda t: t[:, 0:nb].rearrange("p (n o) -> p n o", o=1).to_broadcast([P, nb, FP4_BLOCK])
                    step, side = signal("fp4_step", 32), signal("fp4_sign", 2)
                    with nc.Block() as block:
                        @block.scalar
                        def _(act):
                            nc.scalar.activation(sgn[:, 0:width], v, ACT.Sign).then_inc(side.sem, 1)
                            nc.scalar.activation(mag[:, 0:width], v, ACT.Abs).then_inc(side.sem, 1)

                        @block.vector
                        def _(dve):
                            done = [0]

                            def then(ins):
                                done[0] += 1
                                ins.then_inc(step.sem, 1)
                                dve.wait_ge(step.sem, step.at(0, done[0]))
                            m = mag[:, 0:width]
                            dve.wait_ge(side.sem, side.at(0, 2))
                            then(nc.vector.tensor_reduce(amax[:, 0:nb], blocks(mag), AX.X, ALU.max))
                            then(nc.vector.tensor_scalar(amax[:, 0:nb], amax[:, 0:nb], 1.0 / 6.0, 1e-12, ALU.mult, ALU.max))
                            then(nc.vector.reciprocal(inv[:, 0:nb], amax[:, 0:nb]))
                            then(nc.vector.tensor_tensor(blocks(mag), blocks(mag), of_block(inv), ALU.mult))
                            then(nc.vector.tensor_scalar(v, m, 5.0, 2.0, ALU.is_gt, ALU.mult))
                            then(nc.vector.scalar_tensor_tensor(v, m, 3.5, v, ALU.is_gt, ALU.add))
                            then(nc.vector.scalar_tensor_tensor(v, m, 2.5, v, ALU.is_gt, ALU.add))
                            then(nc.vector.tensor_scalar(v, v, 2.0, None, ALU.mult))
                            for mid in (1.75, 1.25, 0.75, 0.25):
                                then(nc.vector.scalar_tensor_tensor(v, m, mid, v, ALU.is_gt, ALU.add))
                            then(nc.vector.scalar_tensor_tensor(v, v, 0.5, sgn[:, 0:width], ALU.mult, ALU.mult))
                            v3 = v.rearrange("p (n k) -> p n k", k=FP4_BLOCK)
                            then(nc.vector.tensor_tensor(v3, v3, of_block(amax), ALU.mult))
                            while done[0] < 32:
                                then(nc.vector.memset(inv[:, 0:1], 0.0))

                flat = lambda t: t.rearrange("p t d -> p (t d)")
                quantize(flat(w_up[:, :, :]), 2 * FT * D)
                quantize(w_down[:, :], FP4_FFN)
                norm(x, NT, D, z)
                quantize(flat(z[:, :, :]), T)

                chunks = [turn_chunk("act", z, 0, xnT), turn_chunk("dve", z, 4, xnT)]

                def turn_rows(g):
                    def f(o):
                        for j in range(FT):
                            last = nc.tensor.transpose(o[:, j * P:j * P + FP[j]], w_up[0:FP[j], g * FT + j, :],
                                                       ident[0:FP[j], 0:FP[j]])
                        return last
                    return Chunk(ENG[g], f, lambda o: copy(ENG[g], wT[:, g, :], o[:, 0:FP4_FFN]))
                chunks += [turn_rows(0), turn_rows(1)]

                def turn_down(j):
                    return Chunk("dve", lambda o: nc.tensor.transpose(o[0:FP[j], 0:D], w_down[:, j * P:j * P + FP[j]], ident[:, :]),
                                 lambda o: copy("dve", wdT[0:FP[j], j, :], o[0:FP[j], 0:D]))
                chunks += [turn_down(j) for j in range(FT)]
                chunk_block(chunks)
                chunks = []
                for t in range(NT):
                    for g in range(2):
                        mm = lambda o, t=t, g=g: nc.tensor.matmul(o[:, 0:FP4_FFN], xnT[:, t * P:(t + 1) * P], wT[:, g, :],
                                                                  start=True, stop=True)
                        if g == 0:
                            chunks.append(Chunk("act", mm, lambda o, t=t: nc.scalar.activation(silu[:, t, :], o[:, 0:FP4_FFN], ACT.Silu)))
                        else:
                            chunks.append(Chunk("dve", mm, lambda o, t=t: nc.vector.tensor_tensor(hid[:, t, :], o[:, 0:FP4_FFN], silu[:, t, :], ALU.mult),
                                                after=(2 * t,)))
                chunk_block(chunks)
                quantize(flat(hid[:, :, :]), big)
                chunks = []
                for j in range(FT):
                    for t in (0, 4):
                        def turn(o, j=j, t=t):
                            for q in range(4):
                                last = nc.tensor.transpose(o[0:FP[j], q * P:(q + 1) * P], hid[:, t + q, j * P:j * P + FP[j]], ident[:, :])
                            return last
                        e = ENG[t // 4]
                        chunks.append(Chunk(e, turn, lambda o, e=e, j=j, t=t: copy(e, hidT[0:FP[j], j, t * P:(t + 4) * P], o[0:FP[j], :])))
                for t in (0, 4):
                    def downs(o, t=t):
                        for q in range(4):
                            for j in range(FT):
                                last = nc.tensor.matmul(o[:, q * D:(q + 1) * D], hidT[0:FP[j], j, (t + q) * P:(t + q + 1) * P],
                                                        wdT[0:FP[j], j, :], start=(j == 0), stop=(j == FT - 1))
                        return last
                    chunks.append(Chunk("dve", downs, add_to(x, t), after=tuple(range(2 * FT))))
                chunk_block(chunks)

        def l3_attn():
            DQ = 64
            load([(wq[:, 0:DQ], a["L3_attn_Wq"]), (wk[:, 0:DQ], a["L3_attn_Wk"]), (wv[:, :], a["L3_attn_Wv"])])
            norm(x, NT, D, z, xnT)
            attention(self_units(lambda h, t: qT[0:DQ, 0, t * P:(t + 1) * P], lambda h, k0, w: kT[0:DQ, k0:k0 + w],
                                 lambda h, t, i: V[:, t, :], add_store, "causal", 1, D),
                      head=self_chunks(qs=float(DQ) ** -0.5, m=DQ))

        def l3_ffn():
            sub = ExitStack()
            with sub:
                def sbl(name, shape):
                    return sub.enter_context(nc.sbuf_tensor("net_" + name, shape, F32))
                p = lambda s: a["L3_ffn_" + s]
                waves = sbl("waves", [P, 2, 2, N])
                scaled = sbl("qk_scaled", [P, 2, T])
                squares = sbl("squares", [P, 2, T])
                root = sbl("root", [P, 2, T])
                vec = sbl("layer_cols", [P, 16])
                w1 = sbl("w1", [P, 2 * GLU])
                w2 = sbl("w2", [P, 3, D])
                acts = sbl("acts", [P, 3, T])
                gelu = sbl("gelu", [P, 2, BANK])
                centred = outT
                load([(waves[:, :, :, :], a["c_waves"])])
                norm(x, NT, D, xin)
                GT = [P, P, GLU - 2 * P]
                by_batch = lambda v: v.rearrange("p (b n) -> p b n", b=B)

                def shift(l, dst, tag, loads=None, nloads=0):
                    cleared = signal(tag + "shift_cleared", 1, DEPTH)
                    turned_in = signal(tag + "shift_turned", 2, DEPTH)
                    lower = signal(tag + "shift_lower", 2, DEPTH)
                    upper = signal(tag + "shift_upper", 2, DEPTH)
                    loaded = signal("layer_loads", nloads, DEPTH, 16)
                    with ps("bank", [P, 2, BANK]) as bank, nc.Block() as block:
                        if loads:
                            @block.sync
                            def _(sp):
                                loads(sp, loaded)

                        @block.tensor
                        def _(pe):
                            for j in range(2):
                                for q in range(4):
                                    last = nc.tensor.transpose(bank[:, j, q * P:(q + 1) * P], xin[:, 4 * j + q, :], ident[:, :])
                                last.then_inc(turned_in.sem, 1)

                        @block.scalar
                        def _(act):
                            for j in range(2):
                                act.wait_ge(turned_in.sem, turned_in.at(l, j + 1))
                                copy("act", dst[0:D // 2, j * BANK:(j + 1) * BANK], bank[0:D // 2, j, :]).then_inc(lower.sem, 1)

                        @block.vector
                        def _(dve):
                            up = slice(D // 2, D)
                            nc.vector.memset(by_batch(dst[up, :])[:, :, 0:1], 0.0).then_inc(cleared.sem, 1)
                            for j in range(2):
                                dve.wait_ge(turned_in.sem, turned_in.at(l, j + 1))
                                if loads and j == 1:
                                    dve.wait_ge(loaded.sem, loaded.at(l, nloads))
                                copy("dve", by_batch(dst[up, :])[:, 2 * j:2 * j + 2, 1:N],
                                     bank[up, j, :].rearrange("p (b n) -> p b n", b=2)[:, :, 0:N - 1]).then_inc(upper.sem, 1)

                class Finish:
                    done = None

                with nc.Fori(0, DEPTH) as l:
                    def layer_loads(sp, lv):
                        one = lambda w: w[bass.ds(l, 1), :]
                        for r in range(2):
                            for j, nm in enumerate(("q_scale", "k_scale")):
                                sp.dma_start(vec[r * DH:(r + 1) * DH, j:j + 1], one(p(nm)).rearrange("o d -> d o")).then_inc(lv.sem, 16)
                        sp.dma_start(vec[:, 2:3], one(p("ln_g")).rearrange("o d -> d o")).then_inc(lv.sem, 16)
                        sp.dma_start(vec[:, 3:4], one(p("ln_b")).rearrange("o d -> d o")).then_inc(lv.sem, 16)
                        sp.dma_start(vec[:, 4:10], p("b1c")[bass.ds(l, 1), :, :].rearrange("o p c -> p (o c)")).then_inc(lv.sem, 16)
                        sp.dma_start(brow[0:1, 0:D], one(p("b2"))).then_inc(lv.sem, 16)
                        sp.dma_start(w1[:, :], p("W1")[bass.ds(l, 1), :, :].rearrange("o p c -> p (o c)")).then_inc(lv.sem, 16)
                        for j in range(3):
                            sp.dma_start(w2[0:GT[j], j, :], p("W2")[bass.ds(l, 1), j * P:j * P + GT[j], :].rearrange("o p c -> (o p) c")).then_inc(lv.sem, 16)
                    shift(l, xnT, "attn_", layer_loads, 12)

                    head = []
                    for s, w in ((0, wq), (1, wk)):
                        for c in range(2):
                            def both(o, s=s, c=c):
                                nc.scalar.activation(squares[:, s, c * HALF:(c + 1) * HALF], o, ACT.Square)
                                return nc.scalar.activation(scaled[:, s, c * HALF:(c + 1) * HALF], o, ACT.Copy, scale=vec[:, s:s + 1])
                            head.append(Chunk("act", mm_T(w[:, :], xnT, c * HALF), both))
                    for t in (0, 4):
                        head.append(Chunk("dve", mm_tok(xnT, wv[:, :], t), lambda o, t=t: copy("dve", V[:, t:t + 4, :], tiles_of(o))))
                    two = lambda v: v.rearrange("p (b n) -> p b n", n=N)
                    wave = lambda s, w, nb: waves[:, s, w:w + 1, :].to_broadcast([P, nb, N])
                    dsts = (qT[:, 0, :], kT[:, 0:T])
                    for s in range(2):
                        for c in range(2):
                            head.append(Chunk("dve", mm_T(block64[:, :], squares[:, s, :], c * HALF),
                                              lambda o, s=s, c=c: nc.vector.tensor_scalar(root[:, s, c * HALF:(c + 1) * HALF], o, 1e-24, None, ALU.max),
                                              after=(2 * s + c,)))
                    for s in range(2):
                        for c in range(2):
                            head.append(Chunk("dve", mm_T(rot64[:, :], scaled[:, s, :], c * HALF),
                                              lambda o, s=s, c=c: nc.vector.tensor_tensor(two(dsts[s][:, c * HALF:(c + 1) * HALF]), two(o), wave(s, 1, 2), ALU.mult),
                                              after=(2 * s + c,)))
                    ndve_ss = 2 + 4
                    total = DEPTH * PAIRS
                    fin = Finish()
                    turned_cos = signal("cos_done", 2, total)
                    rotated = signal("rotated", 2, total)
                    rooted = signal("root_done", 1, total)
                    rinv = signal("root_inverted", 1, total)
                    fin.done = signal("qk_done", 2, total)

                    def fin_pool(pool, n, emptied):
                        for s in range(2):
                            pool.wait_ge(emptied["dve"].sem, emptied["dve"].at(n, ndve_ss + 2 * s + 2))
                            v = two(scaled[:, s, :])
                            nc.gpsimd.tensor_tensor(v, v, wave(s, 0, B), ALU.mult).then_inc(turned_cos.sem, 1)
                            pool.wait_ge(turned_cos.sem, turned_cos.at(n, s + 1))
                            nc.gpsimd.tensor_tensor(dsts[s], dsts[s], scaled[:, s, :], ALU.add).then_inc(rotated.sem, 1)

                    def fin_act(act, n, emptied):
                        act.wait_ge(emptied["dve"].sem, emptied["dve"].at(n, ndve_ss))
                        nc.scalar.activation(root[:, :, :], root[:, :, :], ACT.Sqrt).then_inc(rooted.sem, 1)

                    def fin_dve(dve, n, emptied):
                        dve.wait_ge(rooted.sem, rooted.at(n, 1))
                        nc.vector.reciprocal(root[:, :, :], root[:, :, :]).then_inc(rinv.sem, 1)
                        dve.wait_ge(rinv.sem, rinv.at(n, 1))
                        for s in range(2):
                            dve.wait_ge(rotated.sem, rotated.at(n, s + 1))
                            nc.vector.scalar_tensor_tensor(dsts[s], dsts[s], (8.0, 1.0)[s], root[:, s, :], ALU.mult,
                                                           ALU.mult).then_inc(fin.done.sem, 1)
                    fin.pool, fin.act, fin.dve = fin_pool, fin_act, fin_dve

                    def head_loads(sp, i, s):
                        for j, buf in enumerate((wq, wk, wv)):
                            sp.dma_start(buf[:, :], p("Wqkv")[bass.ds(l, 1), :, bass.ds(i * D + j * H * DH, D)].rearrange("o p c -> (o p) c")).then_inc(s, 16)

                    def tail_loads(sp, i, s):
                        sp.dma_start(wo[:, :], p("Wo")[bass.ds(l, 1), bass.ds(i * D, D), :].rearrange("o p c -> (o p) c")).then_inc(s, 16)
                    attention(self_units(pair_q, pair_k, pair_v, pair_store, "window", 2, DH), iters=PAIRS,
                              n_of=lambda i: l * PAIRS + i, total=total, head=head, tail=out_chunks(len(head), xin, wo[:, :]),
                              head_loads=head_loads, tail_loads=tail_loads, loads=(3, 1), finish=fin)

                    shift(l, xnT, "ff_")
                    chunk_block([Chunk("dve", mm_T(ones[:, :], xnT, c * HALF),
                                       lambda o, c=c: nc.vector.scalar_tensor_tensor(
                                           centred[:, c * HALF:(c + 1) * HALF], o, -1.0 / D, xnT[:, c * HALF:(c + 1) * HALF], ALU.mult, ALU.add))
                                 for c in range(2)], n=l, iters=DEPTH, tag="mean_")
                    sq, rt = squares[:, 0, :], root[:, 0, :]
                    fsq = signal("ff_squared", 1, DEPTH)
                    with nc.Block() as block:
                        @block.scalar
                        def _(act):
                            nc.scalar.activation(sq, centred[:, :], ACT.Square).then_inc(fsq.sem, 1)
                    chunk_block([Chunk("dve", mm_T(ones[:, :], sq, c * HALF),
                                       lambda o, c=c: nc.vector.tensor_scalar(rt[:, c * HALF:(c + 1) * HALF], o, 1.0 / D, LN_EPS, ALU.mult, ALU.add))
                                 for c in range(2)], n=l, iters=DEPTH, tag="var_")
                    froot = signal("ff_rooted", 1, DEPTH)
                    fnorm = signal("ff_normed", 3, DEPTH)
                    with nc.Block() as block:
                        @block.scalar
                        def _(act):
                            nc.scalar.activation(rt, rt, ACT.Sqrt).then_inc(froot.sem, 1)

                        @block.vector
                        def _(dve):
                            dve.wait_ge(froot.sem, froot.at(l, 1))
                            nc.vector.reciprocal(rt, rt).then_inc(fnorm.sem, 1)
                            dve.wait_ge(fnorm.sem, fnorm.at(l, 1))
                            nc.vector.tensor_tensor(centred[:, :], centred[:, :], rt, ALU.mult).then_inc(fnorm.sem, 1)
                            dve.wait_ge(fnorm.sem, fnorm.at(l, 2))
                            nc.vector.tensor_scalar(centred[:, :], centred[:, :], vec[:, 2:3], vec[:, 3:4], ALU.mult, ALU.add).then_inc(fnorm.sem, 1)
                    chunks = []
                    for j in range(3):
                        g = GT[j]
                        for c in range(2):
                            k = len(chunks)
                            cc = slice(c * HALF, (c + 1) * HALF)
                            chunks.append(Chunk("act", mm_T(w1[:, GLU + j * P:GLU + j * P + g], centred, c * HALF, m=g),
                                                lambda o, g=g, j=j, c=c: nc.scalar.activation(gelu[0:g, c, :], o[0:g, :], ACT.Gelu, bias=vec[0:g, 7 + j:8 + j]),
                                                after=(k - 3,) if j else ()))
                            chunks.append(Chunk("dve", mm_T(w1[:, j * P:j * P + g], centred, c * HALF, m=g),
                                                lambda o, g=g, j=j, c=c, cc=cc: nc.vector.scalar_tensor_tensor(
                                                    acts[0:g, j, cc], o[0:g, :], vec[0:g, 4 + j:5 + j], gelu[0:g, c, :], ALU.add, ALU.mult),
                                                after=(k,)))
                    for t in (0, 4):
                        def downs(o, t=t):
                            for q in range(4):
                                for j in range(3):
                                    nc.tensor.matmul(o[:, q * D:(q + 1) * D], acts[0:GT[j], j, (t + q) * P:(t + q + 1) * P],
                                                     w2[0:GT[j], j, :], start=(j == 0), stop=False)
                                last = nc.tensor.matmul(o[:, q * D:(q + 1) * D], ones[0:1, :], brow[0:1, 0:D], start=False, stop=True)
                            return last
                        chunks.append(Chunk("dve", downs, add_to(xin, t), after=(11,)))
                    chunk_block(chunks, n=l, iters=DEPTH, tag="glu_")
                add_all(x, xin)

        def store():
            sent = signal("stored_out", 1, step=16)
            with nc.Block() as block:
                @block.sync
                def _(sp):
                    sp.dma_start(out.rearrange("b (t p) d -> p (b t) d", p=P), x[:, :, :]).then_inc(sent.sem, 16)
                    sp.wait_ge(sent.sem, sent.at(0, 1))

        stages = dict(l0_attn=l0_attn, l0_xattn=l0_xattn, l0_ffn=l0_ffn, l1_attn=l1_attn, l1_xattn=l1_xattn, l1_ffn=l1_ffn,
                      l2_attn=l2_attn, l2_xattn=l2_xattn, l2_ffn=l2_ffn, l3_attn=l3_attn, l3_xattn=l3_xattn, l3_ffn=l3_ffn)
        setup()
        for name in STAGES:
            stages[name]()
        store()


STAGES = ("l0_attn", "l0_xattn", "l0_ffn", "l1_attn", "l1_xattn", "l1_ffn", "l2_attn", "l2_xattn", "l2_ffn", "l3_attn",
          "l3_xattn", "l3_ffn")


AHEAD = (
    "bank_filled", "bank_emptied_act", "bank_emptied_dve", "measured", "gathered", "eps_added", "rooted",
    "inverted", "normed", "norm_turned", "norm_moved_act", "norm_moved_dve", "masked_q", "scores_ready",
    "max_ready", "probs_ready", "ipa_rescaled", "probs_turned", "turned_moved_act", "turned_moved_dve",
    "values_ready", "rowinv_ready", "head_stored", "consts_made", "ipa_made", "rope_done", "added_all",
    "gate_step", "gate_exp", "expert_up", "expert_silu", "expert_gated", "expert_down",
    "expert_added", "mixed", "squared", "mask_made", "qk_rooted", "fp4_cleared", "fp4_step",
    "cos_done", "rotated", "root_done", "root_inverted", "qk_done",
    "ff_squared", "ff_rooted", "ff_normed",
    "mean_bank_filled", "mean_bank_emptied_act", "mean_bank_emptied_dve", "var_bank_filled",
    "var_bank_emptied_act", "var_bank_emptied_dve", "glu_bank_filled", "glu_bank_emptied_act",
    "glu_bank_emptied_dve", "attn_shift_cleared", "attn_shift_turned", "attn_shift_lower", "attn_shift_upper",
    "ff_shift_cleared", "ff_shift_turned", "ff_shift_lower", "ff_shift_upper",
)


def constants():
    f = np.float32
    i, j = np.arange(P)[:, None], np.arange(P)[None, :]
    keep = np.stack([j <= i, j >= i, (j <= i) & (j >= i - WINDOW), j >= i + P - WINDOW], 1)

    def rotation(width):
        r, half = np.zeros((P, P), f), width // 2
        for d in range(P):
            if d % width < half:
                r[d + half, d] = -1.0
            else:
                r[d - half, d] = 1.0
        return r

    def angles(width):
        inv = (f(1.0) / f(10000.0) ** (np.arange(0, width, 2, dtype=f) / f(width))).astype(f)
        ang = np.arange(N, dtype=f)[:, None] * inv[None, :]
        return np.concatenate([ang, ang], 1).astype(f)

    a8, a64 = angles(HS), angles(DH)
    half = np.arange(0, DH, 2, dtype=f)
    base = ((half + f(0.4 * DH)) / f(1.4 * DH)).astype(f)
    power = ((np.arange(N, dtype=f) - f(N // 2)) / f(WINDOW // 2)).astype(f)
    scale = (base[None, :] ** power[:, None]).astype(f)
    scale = np.concatenate([scale, scale], 1)
    tile = lambda t: np.ascontiguousarray(np.tile(t.T, (P // t.shape[1], 1))).astype(f)
    waves = np.stack([np.stack([tile(np.cos(a64) * s), tile(np.sin(a64) * s)], 1) for s in (scale, f(1.0) / scale)], 1)
    return {
        "c_ident": np.eye(P, dtype=f),
        "c_masks": np.where(keep, f(0), f(NEG)).astype(f),
        "c_head_mask": (np.arange(P)[:, None] // HS == np.arange(H)[None, :]).astype(f),
        "c_rot8": rotation(HS), "c_rot64": rotation(DH),
        "c_block64": (i // DH == j // DH).astype(f),
        "c_cos8": tile(np.cos(a8)), "c_sin8": tile(np.sin(a8)),
        "c_waves": np.ascontiguousarray(waves),
    }


def laid_out(inp):
    g = {k: np.asarray(v) for k, v in inp.items()}
    t = lambda m: np.ascontiguousarray(m.T)
    o = dict(g)
    for nm in "qkvo":
        o[f"L0_xattn_{nm}_downT"] = t(o.pop(f"L0_xattn_{nm}_down"))
    wqkv = o.pop("L0_ffn_wqkv")
    kv = lambda r: t(np.repeat(wqkv[r:r + 32].reshape(4, 1, HS, D), 4, axis=1).reshape(D, D))
    o["L0_ffn_wqT"], o["L0_ffn_wkT"], o["L0_ffn_wvT"] = t(wqkv[0:D]), kv(D), kv(D + 32)
    o["L0_ffn_woT"], o["L0_ffn_gate_wT"] = t(o.pop("L0_ffn_wo")), t(o.pop("L0_ffn_gate_w"))
    o["L0_ffn_w13T"] = np.ascontiguousarray(o.pop("L0_ffn_w13").transpose(2, 0, 1).reshape(D, EXPERTS * 2 * FFN))
    w2 = o.pop("L0_ffn_w2")
    o["L0_ffn_w2T"] = np.ascontiguousarray(w2.transpose(2, 0, 1).reshape(2, P, EXPERTS, D).transpose(1, 2, 0, 3).reshape(P, EXPERTS * 2 * D))
    for nm in "rkv":
        o[f"L1_ffn_W_{nm}T"] = t(o.pop(f"L1_ffn_W_{nm}"))
    for nm in "QKV":
        o[f"L2_attn_{nm}T"] = t(o.pop(f"L2_attn_{nm}").reshape(H * DH, D))
    o["L2_attn_OT"] = t(o.pop("L2_attn_O"))
    wkv, wlkv = o.pop("L2_xattn_Wkv"), o.pop("L2_xattn_Wlkv")
    o["L2_xattn_WkT"], o["L2_xattn_WvT"] = t(wkv[0:D]), t(wkv[D:])
    o["L2_xattn_WlkT"], o["L2_xattn_WlvT"] = t(wlkv[0:D]), t(wlkv[D:])
    o["L2_xattn_WqT"], o["L2_xattn_WoT"] = t(o.pop("L2_xattn_Wq")), t(o.pop("L2_xattn_Wo"))
    wkv = o.pop("L3_xattn_w_kv")
    o["L3_xattn_w_k"], o["L3_xattn_w_v"] = wkv[:, 0:H * DH], wkv[:, H * DH:]
    b1 = o.pop("L3_ffn_b1")
    b1c = np.zeros((DEPTH, P, 6), b1.dtype)
    for h in range(2):
        for j in range(3):
            n = min(P, GLU - j * P)
            b1c[:, 0:n, 3 * h + j] = b1[:, h * GLU + j * P:h * GLU + j * P + n]
    o["L3_ffn_b1c"] = b1c
    o["mask_BxS2_bk0"] = o["mask_BxS2_bk0"].reshape(1, B * M)
    return o


def kernel(**inputs):
    import concourse.bacc as bacc
    from concourse.bass_utils import run_bass_kernel_spmd

    nc = bacc.Bacc("TRN2", target_bir_lowering=False, num_devices=1)
    arrays, args = {}, {}
    for name, v in {**laid_out(inputs), **constants()}.items():
        v = np.ascontiguousarray(v)
        arrays[f"in_{name}"] = v
        args[name] = nc.dram_tensor(f"in_{name}", v.shape, mybir.dt.from_np(v.dtype), kind="ExternalInput").ap()
    y = nc.dram_tensor("out_0", (B, N, D), F32, kind="ExternalOutput").ap()
    decoder(nc, args, y)
    r = run_bass_kernel_spmd(nc, [arrays], core_ids=[0])
    return r.results[0]["out_0"]
```

```python
from contextlib import ExitStack, contextmanager

import numpy as np
import concourse.bass as bass
from concourse import mybir

F32 = mybir.dt.float32
BF16 = mybir.dt.bfloat16
U8 = mybir.dt.uint8
ALU = mybir.AluOpType
ACT = mybir.ActivationFunctionType
AX = mybir.AxisListType

P = 128
B, N, D = 4, 256, 128
T = B * N
NT = T // P
QT = N // P
M, C = 512, 96
MT = B * M // P
KT = M // P
BANK = 512
H, DH = 16, 64
HS = D // H
PAIRS = H // 2
RANK = 32
IPA = 4
EXPERTS, FFN = 8, 256
FP4_FFN, FP4_BLOCK = 352, 16
DEPTH, GLU, WINDOW, QK_SCALE = 6, int(D * 4 * 2 / 3), 32, 8.0
NEG = -1.0e30
LN_EPS = 1e-5


class Count:

    def __init__(self, sem, base, per, step):
        self.sem, self.base, self.per, self.step = sem, base, per, step

    def at(self, i, k):
        return i * (self.per * self.step) + (self.base + k * self.step)


class Signals:

    def __init__(self, nc, ctx, ahead):
        self.nc, self.ctx, self.sems, self.base = nc, ctx, {}, {}
        for name, n in ahead:
            self(name, n)
            nc.sync.sem_inc(self.sems[name], n)
        nc.all_engine_barrier()

    def __call__(self, name, per, iters=1, step=1):
        if name not in self.sems:
            self.sems[name] = self.ctx.enter_context(self.nc.semaphore(name))
            self.base[name] = 0
        out = Count(self.sems[name], self.base[name], per, step)
        self.base[name] += per * iters * step
        return out


@contextmanager
def rounds(eng, iters):
    if iters == 1:
        yield 0
    else:
        with eng.Fori(0, iters) as i:
            yield i


class Chunk:

    def __init__(self, engine, mm, out, after=()):
        self.engine, self.mm, self.out, self.after = engine, mm, out, after


def emptied_before(chunks, j, banks):
    need = {}
    for d in ([j - banks] if j >= banks else []) + list(chunks[j].after):
        e = chunks[d].engine
        need[e] = max(need.get(e, 0), sum(c.engine == e for c in chunks[:d + 1]))
    return sorted(need.items())


class Unit:

    def __init__(self, nk, scores, values, store, width, base=None):
        self.nk, self.scores, self.values, self.store, self.width = nk, scores, values, store, width


def decoder(nc, a, out):
    ctx = ExitStack()
    with ctx:
        signal = Signals(nc, ctx, [(name, 1) for name in AHEAD] + [(name, STEPS_AHEAD) for name in AHEAD_BY_STEPS])

        def sb(name, shape, dt=F32):
            return ctx.enter_context(nc.sbuf_tensor(name, shape, dt))

        def ps(name, shape):
            psum_names[0] += 1
            return nc.psum_tensor(f"{name}_{psum_names[0]}", shape, F32)
        psum_names = [0]

        def copy(engine, dst, src, scale=1.0):
            if engine == "act":
                return nc.scalar.activation(dst, src, ACT.Copy, scale=scale)
            if isinstance(scale, float) and scale == 1.0:
                return nc.vector.tensor_copy(dst, src)
            return nc.vector.tensor_scalar(dst, src, scale, None, ALU.mult)

        def affine(engine, dst, src, scale, bias):
            if engine == "act":
                return nc.scalar.activation(dst, src, ACT.Identity, bias=bias, scale=scale)
            return nc.vector.tensor_scalar(dst, src, scale, bias, ALU.mult, ALU.add)

        x = sb("x", [P, NT, D])
        xin = sb("xin", [P, NT, D])
        z = sb("z", [P, NT, D])
        xnT = sb("xnT", [P, T])
        stats = sb("stats", [P, MT, 6])
        meanvar = sb("meanvar", [P, MT, 2])
        spread = sb("spread", [P, MT])
        rstd = sb("rstd", [P, MT])
        ident = sb("ident", [P, P])
        ident16 = sb("ident16", [P, P], BF16)
        masks = sb("masks", [P, 2, P])
        masks16 = sb("masks16", [P, 2, P], BF16)
        ones = sb("ones", [P, P])
        ones16 = sb("ones16", [P, P], BF16)
        head_mask = sb("head_mask", [P, H])
        rot8 = sb("rot8", [P, P])
        block64 = sb("block64", [P, P])
        cols = sb("cols", [P, 32])
        brow = sb("brow", [1, 512])
        early = ctx.enter_context(ExitStack())

        def sbe(name, shape):
            return early.enter_context(nc.sbuf_tensor(name, shape, F32))

        ctx_tok = sbe("ctx_tok", [P, MT, C])
        ctxT = sbe("ctxT", [P, B * M])
        qT = sbe("qT", [P, 2, T])
        qM = sbe("qM", [P, 2, T])
        kT = sbe("kT", [P, B * (M + N)])
        V = sbe("V", [P, MT + NT, D])
        probs = sbe("probs", [P, 3, M + N])
        turned = sbe("turned", [P, 4, BANK])
        negmax = sbe("negmax", [P, 32])
        rowsum = sbe("rowsum", [P, 32])
        rowinv = sbe("rowinv", [P, 32])
        heads_out = sbe("heads_out", [P, NT, D])
        outT = sbe("outT", [P, T])
        wq = sbe("wq", [P, D])
        wk = sbe("wk", [P, D])
        wv = sbe("wv", [P, D])
        wo = sbe("wo", [P, D])

        def columns(c0, c1=None):
            return cols[:, c0:(c0 + 1 if c1 is None else c1)]

        def load(pairs):
            arrived = signal("small_loads", len(pairs), step=16)
            with nc.Block() as block:
                @block.sync
                def _(sp):
                    for dst, src in pairs:
                        sp.dma_start(dst, src).then_inc(arrived.sem, 16)
                    sp.wait_ge(arrived.sem, arrived.at(0, len(pairs)))

        def col_of(vec):
            return vec.rearrange("(d o) -> d o", o=1)

        def row_of(vec):
            return vec.rearrange("(o d) -> o d", o=1)

        def chunk_block(chunks, n=0, iters=1, tag=""):
            filled = signal(tag + "bank_filled", len(chunks), iters)
            count = {e: sum(c.engine == e for c in chunks) for e in ("act", "dve")}
            emptied = {e: signal(f"{tag}bank_emptied_{e}", count[e], iters) for e in ("act", "dve")}
            slots = 4
            with ps("bank", [P, slots, BANK]) as bank, nc.Block() as block:
                @block.tensor
                def _(pe):
                    for j, c in enumerate(chunks):
                        for e, k in emptied_before(chunks, j, slots):
                            pe.wait_ge(emptied[e].sem, emptied[e].at(n, k))
                        c.mm(bank[:, j % slots, :]).then_inc(filled.sem, 1)

                def empty(eng, e):
                    for j, c in enumerate(chunks):
                        if c.engine == e:
                            eng.wait_ge(filled.sem, filled.at(n, j + 1))
                            c.out(bank[:, j % slots, :]).then_inc(emptied[e].sem, 1)

                @block.scalar
                def _(act):
                    empty(act, "act")

                @block.vector
                def _(dve):
                    empty(dve, "dve")

        def norm(src, tiles, width, dst, dstT=None, rms=False, gain=None, bias=None, eps=LN_EPS, n=0, iters=1):
            measured = signal("measured", tiles, iters)
            gathered = signal("gathered", tiles, iters)
            eps_added = signal("eps_added", 2, iters)
            rooted = signal("rooted", 1, iters)
            inverted = signal("inverted", 1, iters)
            normed = signal("normed", tiles, iters)
            nbank = (tiles + 3) // 4 if dstT is not None else 0
            turned_in = signal("norm_turned", nbank, iters)
            moved_act = signal("norm_moved_act", (nbank + 1) // 2, iters)
            moved_dve = signal("norm_moved_dve", nbank // 2, iters)
            with ps("bank", [P, 4, BANK]) as bank, nc.Block() as block:
                def move(e, j):
                    s, d = bank[0:width, j % 4, :], dstT[0:width, j * BANK:(j + 1) * BANK]
                    if bias is not None:
                        return affine(e, d, s, gain[0:width], bias[0:width])
                    return copy(e, d, s, 1.0 if gain is None else gain[0:width])

                @block.vector
                def _(dve):
                    for t in range(tiles):
                        nc.vector.bn_stats(stats[:, t, :], src[:, t, 0:width]).then_inc(measured.sem, 1)
                    if iters > 1:
                        dve.wait_ge(measured.sem, measured.at(n, tiles))
                        nc.vector.memset(spread[:, 0:tiles], 0.0)
                    for t in range(tiles):
                        if iters == 1:
                            dve.wait_ge(measured.sem, measured.at(n, t + 1))
                        nc.vector.bn_aggr(meanvar[:, t, :], stats[:, t, :]).then_inc(gathered.sem, 1)
                    dve.wait_ge(gathered.sem, gathered.at(n, tiles))
                    if rms:
                        nc.vector.tensor_tensor(spread[:, 0:tiles], meanvar[:, 0:tiles, 0], meanvar[:, 0:tiles, 0],
                                                ALU.mult).then_inc(eps_added.sem, 1)
                        dve.wait_ge(eps_added.sem, eps_added.at(n, 1))
                        nc.vector.scalar_tensor_tensor(spread[:, 0:tiles], meanvar[:, 0:tiles, 1], eps,
                                                       spread[:, 0:tiles], ALU.add, ALU.add).then_inc(eps_added.sem, 1)
                    else:
                        nc.vector.tensor_scalar(spread[:, 0:tiles], meanvar[:, 0:tiles, 1], eps, None,
                                                ALU.add).then_inc(eps_added.sem, 2)
                    dve.wait_ge(rooted.sem, rooted.at(n, 1))
                    nc.vector.reciprocal(rstd[:, 0:tiles], spread[:, 0:tiles]).then_inc(inverted.sem, 1)
                    dve.wait_ge(inverted.sem, inverted.at(n, 1))
                    for t in range(tiles):
                        if rms:
                            last = nc.vector.tensor_scalar(dst[:, t, 0:width], src[:, t, 0:width], rstd[:, t:t + 1],
                                                           None, ALU.mult)
                        else:
                            last = nc.vector.tensor_scalar(dst[:, t, 0:width], src[:, t, 0:width],
                                                           meanvar[:, t, 0:1], rstd[:, t:t + 1],
                                                           ALU.subtract, ALU.mult)
                        last.then_inc(normed.sem, 1)
                    for j in range(1, nbank, 2):
                        dve.wait_ge(turned_in.sem, turned_in.at(n, j + 1))
                        move("dve", j).then_inc(moved_dve.sem, 1)

                @block.scalar
                def _(act):
                    act.wait_ge(eps_added.sem, eps_added.at(n, 2))
                    nc.scalar.activation(spread[:, 0:tiles], spread[:, 0:tiles], ACT.Sqrt).then_inc(rooted.sem, 1)
                    for j in range(0, nbank, 2):
                        act.wait_ge(turned_in.sem, turned_in.at(n, j + 1))
                        move("act", j).then_inc(moved_act.sem, 1)

                @block.tensor
                def _(pe):
                    for j in range(nbank):
                        pe.wait_ge(normed.sem, normed.at(n, 4 * j + 4))
                        for q in range(4):
                            last = nc.tensor.transpose(bank[0:width, j % 4, q * P:(q + 1) * P],
                                                       dst[:, 4 * j + q, 0:width], ident[:, :])
                        last.then_inc(turned_in.sem, 1)

        def attention(units, iters=1, n_of=lambda i: i, total=None, head=(), tail=(), head_loads=None, tail_loads=None,
                      loads=(0, 0), mask_heads=False, ipa=False, wide=1):
            total = iters if total is None else total
            chunks = list(head) + list(tail)
            nh, U = len(head), len(units)
            turns = [[(g, min(g + 4, u.nk // P)) for g in range(0, u.nk // P, 4)] if wide == 1 else
                     [(0, 3), (3, 6)] for u in units]
            G = len(turns[0])
            slots = {1: 4, 2: 2}[wide]
            banks = 2
            lag_v = 3
            ow = units[0].width

            weights_in = signal("weights_in", loads[0], total, 16)
            out_weights_in = signal("out_weights_in", loads[1], total, 16)
            filled = signal("bank_filled", len(chunks), total)
            count = {e: sum(c.engine == e for c in chunks) for e in ("act", "dve")}
            emptied = {e: signal(f"bank_emptied_{e}", count[e], total) for e in ("act", "dve")}
            nhead = {e: sum(c.engine == e for c in head) for e in ("act", "dve")}
            masked = signal("masked_q", 2 if mask_heads else 0, total)
            scored = signal("scores_ready", U, total)
            maxed = signal("max_ready", U, total)
            exped = signal("probs_ready", U, total)
            rescaled = signal("ipa_rescaled", 2 * U if ipa else 0, total)
            flipped = signal("probs_turned", U * G, total)
            moved = [signal(f"turned_moved_{e}", U * G // 2, total) for e in ("act", "dve")]
            summed = signal("values_ready", U, total)
            inverse = signal("rowinv_ready", U, total)
            stored = signal("head_stored", U, total)

            with ExitStack() as inner:
                proj = inner.enter_context(ps("proj", [P, banks, BANK]))
                scores = inner.enter_context(ps("scores", [P, slots, wide * BANK]))
                flip = inner.enter_context(ps("flip", [P, 2, BANK]))
                block = inner.enter_context(nc.Block())

                def weighted(u):
                    return proj[:, u % banks, 0:ow]

                @block.sync
                def _(sp):
                    if loads[0]:
                        head_loads(sp, n_of(0) if iters == 1 else 0, weights_in.sem)
                    if loads[1]:
                        tail_loads(sp, n_of(0) if iters == 1 else 0, out_weights_in.sem)
                    if iters > 1 and loads[0]:
                        with sp.Fori(0, iters - 1) as i:
                            n = n_of(i)
                            sp.wait_ge(filled.sem, filled.at(n, nh))
                            head_loads(sp, i + 1, weights_in.sem)
                            if loads[1]:
                                sp.wait_ge(filled.sem, filled.at(n, len(chunks)))
                                tail_loads(sp, i + 1, out_weights_in.sem)

                @block.gpsimd
                def _(pool):
                    def mask(i, s):
                        nc.gpsimd.tensor_tensor(qM[:, s, :], qT[:, 0, :],
                                                head_mask[:, bass.ds(2 * i + s, 1)].to_broadcast([P, T]),
                                                ALU.mult).then_inc(masked.sem, 1)
                    if mask_heads:
                        mask(0, 0)
                        mask(0, 1)
                        with pool.Fori(0, iters - 1) as i:
                            for s in range(2):
                                pool.wait_ge(scored.sem, scored.at(i, (s + 1) * U // 2))
                                mask(i + 1, s)

                @block.tensor
                def _(pe):
                    def fill(n, j):
                        c = chunks[j]
                        if j < banks:
                            for e in ("act", "dve"):
                                pe.wait_ge(emptied[e].sem, emptied[e].at(n, 0))
                        for e, k in emptied_before(chunks, j, banks):
                            pe.wait_ge(emptied[e].sem, emptied[e].at(n, k))
                        c.mm(proj[:, j % banks, :]).then_inc(filled.sem, 1)

                    with rounds(pe, iters) as i:
                        n = n_of(i)
                        if loads[0]:
                            pe.wait_ge(weights_in.sem, weights_in.at(n, loads[0]))
                        for j in range(nh):
                            fill(n, j)
                        for e in ("act", "dve"):
                            pe.wait_ge(emptied[e].sem, emptied[e].at(n, nhead[e]))
                        for s in range(U + lag_v):
                            if s < U:
                                if mask_heads and s % (U // 2) == 0:
                                    pe.wait_ge(masked.sem, masked.at(n, s // (U // 2) + 1))
                                pe.wait_ge(exped.sem, exped.at(n, max(0, s - slots + 1)))
                                units[s].scores(scores[:, s % slots, :]).then_inc(scored.sem, 1)
                            t = s - 2
                            if 0 <= t < U:
                                if ipa:
                                    pe.wait_ge(rescaled.sem, rescaled.at(n, 2 * t + 2))
                                else:
                                    pe.wait_ge(exped.sem, exped.at(n, t + 1))
                                for g, (b0, b1) in enumerate(turns[t]):
                                    q = t * G + g
                                    pe.wait_ge(moved[q % 2].sem, moved[q % 2].at(n, q // 2))
                                    for j in range(b0, b1):
                                        last = nc.tensor.transpose(flip[:, q % 2, (j - b0) * P:(j - b0 + 1) * P],
                                                                   probs[:, t % 3, j * P:(j + 1) * P], ident[:, :])
                                    last.then_inc(flipped.sem, 1)
                            t = s - lag_v
                            if 0 <= t < U:
                                pe.wait_ge(stored.sem, stored.at(n, max(0, t - banks + 1)))
                                for g, (b0, b1) in enumerate(turns[t]):
                                    q = t * G + g
                                    pe.wait_ge(moved[q % 2].sem, moved[q % 2].at(n, q // 2 + 1))
                                    for j in range(b0, b1):
                                        last = nc.tensor.matmul(weighted(t),
                                                                turned[:, q % 4, (j - b0) * P:(j - b0 + 1) * P],
                                                                units[t].values(j, i),
                                                                start=(j == 0), stop=(j == units[t].nk // P - 1))
                                last.then_inc(summed.sem, 1)
                        if tail:
                            pe.wait_ge(stored.sem, stored.at(n, U))
                            if loads[1]:
                                pe.wait_ge(out_weights_in.sem, out_weights_in.at(n, loads[1]))
                            for j in range(nh, len(chunks)):
                                fill(n, j)

                def empty(eng, e, n, js):
                    for j in js:
                        if chunks[j].engine == e:
                            eng.wait_ge(filled.sem, filled.at(n, j + 1))
                            chunks[j].out(proj[:, j % banks, :]).then_inc(emptied[e].sem, 1)

                def move_turned(eng, k, n, t):
                    for g, (b0, b1) in enumerate(turns[t]):
                        q = t * G + g
                        if q % 2 == k:
                            w = (b1 - b0) * P
                            eng.wait_ge(flipped.sem, flipped.at(n, q + 1))
                            if q >= 4:
                                eng.wait_ge(summed.sem, summed.at(n, (q - 4) // G + 1))
                            else:
                                eng.wait_ge(summed.sem, summed.at(n, 0))
                            copy(("act", "dve")[k], turned[:, q % 4, 0:w],
                                 flip[:, q % 2, 0:w]).then_inc(moved[k].sem, 1)

                @block.scalar
                def _(act):
                    with rounds(act, iters) as i:
                        n = n_of(i)
                        empty(act, "act", n, range(nh))
                        act.wait_ge(stored.sem, stored.at(n, 0))
                        for s in range(U + 2):
                            if s < U:
                                nk = units[s].nk
                                act.wait_ge(maxed.sem, maxed.at(n, s + 1))
                                act.wait_ge(flipped.sem, flipped.at(n, max(0, s - 2) * G))
                                if ipa:
                                    nc.scalar.activation(probs[:, s % 3, 0:nk - IPA], scores[:, s % slots, 0:nk - IPA],
                                                         ACT.Exp, bias=negmax[:, s:s + 1],
                                                         accum_out=rowsum[:, s:s + 1])
                                    nc.scalar.activation(probs[:, s % 3, nk - IPA:nk], scores[:, s % slots, nk - IPA:nk],
                                                         ACT.Exp, bias=negmax[:, U + s:U + s + 1],
                                                         accum_out=rowsum[:, U + s:U + s + 1]).then_inc(exped.sem, 1)
                                else:
                                    nc.scalar.activation(probs[:, s % 3, 0:nk], scores[:, s % slots, 0:nk], ACT.Exp,
                                                         bias=negmax[:, s:s + 1],
                                                         accum_out=rowsum[:, s:s + 1]).then_inc(exped.sem, 1)
                            if 0 <= s - 2 < U:
                                move_turned(act, 0, n, s - 2)
                        empty(act, "act", n, range(nh, len(chunks)))

                @block.vector
                def _(dve):
                    with rounds(dve, iters) as i:
                        n = n_of(i)
                        empty(dve, "dve", n, range(nh))
                        for s in range(U + lag_v):
                            if s < U:
                                nk = units[s].nk
                                dve.wait_ge(scored.sem, scored.at(n, s + 1))
                                if ipa:
                                    nc.vector.tensor_reduce(negmax[:, U + s:U + s + 1],
                                                            scores[:, s % slots, nk - IPA:nk], AX.X, ALU.max,
                                                            negate=True)
                                    nc.vector.tensor_reduce(negmax[:, s:s + 1], scores[:, s % slots, 0:nk - IPA],
                                                            AX.X, ALU.max, negate=True).then_inc(maxed.sem, 1)
                                else:
                                    nc.vector.tensor_reduce(negmax[:, s:s + 1], scores[:, s % slots, 0:nk], AX.X,
                                                            ALU.max, negate=True).then_inc(maxed.sem, 1)
                            t = s - 1
                            if ipa and 0 <= t < U:
                                nk = units[t].nk
                                dve.wait_ge(exped.sem, exped.at(n, t + 1))
                                nc.vector.reciprocal(rowinv[:, U + t:U + t + 1],
                                                     rowsum[:, U + t:U + t + 1]).then_inc(rescaled.sem, 1)
                                dve.wait_ge(rescaled.sem, rescaled.at(n, 2 * t + 1))
                                tail_p = probs[:, t % 3, nk - IPA:nk]
                                nc.vector.tensor_scalar(tail_p, tail_p, rowsum[:, t:t + 1],
                                                        rowinv[:, U + t:U + t + 1], ALU.mult,
                                                        ALU.mult).then_inc(rescaled.sem, 1)
                            t = s - 2
                            if 0 <= t < U:
                                dve.wait_ge(exped.sem, exped.at(n, t + 1))
                                nc.vector.reciprocal(rowinv[:, t:t + 1], rowsum[:, t:t + 1]).then_inc(inverse.sem, 1)
                                move_turned(dve, 1, n, t)
                            t = s - lag_v
                            if 0 <= t < U:
                                dve.wait_ge(inverse.sem, inverse.at(n, t + 1))
                                dve.wait_ge(summed.sem, summed.at(n, t + 1))
                                units[t].store(weighted(t), rowinv[:, t:t + 1], i).then_inc(stored.sem, 1)
                        empty(dve, "dve", n, range(nh, len(chunks)))

        HALF = BANK

        def mm_T(w, srcT, c0, k=P, m=P, cols_n=HALF):
            return lambda o: nc.tensor.matmul(o[0:m, 0:cols_n], w, srcT[0:k, c0:c0 + cols_n], start=True, stop=True)

        def mm_tok(srcT, w, t0, k=P, m=D, bias=None, tiles=4):
            def f(o):
                for q in range(tiles):
                    last = nc.tensor.matmul(o[:, q * m:(q + 1) * m], srcT[0:k, (t0 + q) * P:(t0 + q + 1) * P], w,
                                            start=True, stop=bias is None)
                    if bias is not None:
                        last = nc.tensor.matmul(o[:, q * m:(q + 1) * m], ones[0:1, :], bias, start=False, stop=True)
                return last
            return f

        def tiles_of(o, m=D, n=4):
            return o[:, 0:n * m].rearrange("p (t d) -> p t d", t=n)

        def turn_chunk(engine, src, t0, dstT):
            def f(o):
                for q in range(4):
                    last = nc.tensor.transpose(o[:, q * P:(q + 1) * P], src[:, t0 + q, :], ident[:, :])
                return last
            return Chunk(engine, f, lambda o: copy(engine, dstT[:, t0 * P:(t0 + 4) * P], o))

        def add_to(acc, t0):
            return lambda o: nc.vector.tensor_tensor(acc[:, t0:t0 + 4, :], acc[:, t0:t0 + 4, :], tiles_of(o), ALU.add)

        def out_chunks(first, acc, w, bias=None):
            return [turn_chunk("act", heads_out, 0, outT), turn_chunk("dve", heads_out, 4, outT),
                    Chunk("dve", mm_tok(outT, w, 0, bias=bias), add_to(acc, 0), after=(first,)),
                    Chunk("dve", mm_tok(outT, w, 4, bias=bias), add_to(acc, 4), after=(first + 1,))]

        ENG = ("act", "dve")

        def self_chunks(qs=1.0, srcT=xnT, first=0, vbias=None, qbias=None, kbias=None, m=D, mv=D, split=False):
            out_list = []
            for w, dst, s, bcol in ((wq, qT[:, 0, :], qs, qbias), (wk, kT, 1.0, kbias)):
                for c in range(T // HALF):
                    e = ENG[c % 2]
                    d = dst[0:m, c * HALF:(c + 1) * HALF]
                    if split and w is wq:
                        f = lambda o, e=e, c=c, s=s: put_heads(e, o, c, s)
                    elif bcol is None:
                        f = lambda o, e=e, d=d, s=s: copy(e, d, o[0:m, :], s)
                    else:
                        f = lambda o, d=d, s=s, bcol=bcol: nc.vector.tensor_scalar(d, o[0:m, :], bcol, s, ALU.add, ALU.mult)
                        e = "dve"
                    out_list.append(Chunk(e, mm_T(w[:, 0:m], srcT, c * HALF, m=m), f))
            for t in range(0, NT, 4):
                e = ENG[t // 4 % 2]
                out_list.append(Chunk(e, mm_tok(srcT, wv[:, 0:mv], t, bias=vbias),
                                      lambda o, e=e, t=t: copy(e, V[:, t:t + 4, :], tiles_of(o))))
            return out_list

        def score_mm(segments):
            def f(o):
                for c0, w, q, k, mk in segments:
                    last = nc.tensor.matmul(o[:, c0:c0 + w], q, k, start=True, stop=not mk)
                    for j, (ml, mr, m0, mw) in enumerate(mk):
                        last = nc.tensor.matmul(o[:, m0:m0 + mw], ml, mr, start=False, stop=(j == len(mk) - 1))
                return last
            return f

        CAUSAL, NOT_BEFORE = range(2)

        def block_mask(kind, c0):
            return (ident16[:, :], masks16[:, kind, :], c0, P)

        def self_units(q_of, k_of, v_of, store_of, kind, heads, width):
            us = []
            for h in range(heads):
                for b in range(B):
                    for qt in range(QT):
                        t = b * QT + qt
                        nk, mk = N, []
                        if kind == "causal":
                            nk, mk = (qt + 1) * P, [block_mask(CAUSAL, qt * P)]
                        elif kind == "near":
                            mk = [block_mask(CAUSAL, P)] if qt == 0 else [block_mask(NOT_BEFORE, 0)]
                        us.append(Unit(nk, score_mm([(0, nk, q_of(h, t), k_of(h, b * N, nk), mk)]),
                                       lambda j, i, h=h, b=b: v_of(h, b * QT + j, i), store_of(h, t), width))
            return us

        def cross_units(q_of, k_of, v_of, store_of, heads, width):
            us = []
            for h in range(heads):
                for b in range(B):
                    for qt in range(QT):
                        t = b * QT + qt
                        us.append(Unit(M, score_mm([(0, M, q_of(h, t), k_of(h, b * M, M), [])]),
                                       lambda j, i, h=h, b=b: v_of(h, b * KT + j, i), store_of(h, t), width))
            return us

        def pair_rows(h):
            return slice(h * DH, (h + 1) * DH)

        def clear_heads():
            cleared = signal("heads_cleared", 1)
            with nc.Block() as block:
                @block.vector
                def _(dve):
                    nc.vector.memset(qM[:, :, :], 0.0).then_inc(cleared.sem, 1)

        def put_heads(engine, o, c, scale=1.0):
            for h in range(2):
                last = copy(engine, qM[pair_rows(h), h, c * HALF:(c + 1) * HALF], o[pair_rows(h), :], scale)
            return last

        pair_v = lambda h, t, i: V[:, t, pair_rows(h)]

        def pair_store(h, t):
            return lambda o, r, i: nc.vector.tensor_scalar(heads_out[:, t, pair_rows(h)], o, r, None, ALU.mult)

        slot_q = lambda h, t: qM[:, h, t * P:(t + 1) * P]
        all_k = lambda h, k0, w: kT[:, k0:k0 + w]
        slot_v = lambda h, t, i: V[:, t, bass.ds(i * (2 * HS) + h * HS, HS)]

        def slot_store(h, t):
            return lambda o, r, i: nc.vector.tensor_scalar(heads_out[:, t, bass.ds(i * (2 * HS) + h * HS, HS)], o, r,
                                                           None, ALU.mult)

        def add_store(h, t):
            return lambda o, r, i: nc.vector.scalar_tensor_tensor(x[:, t, :], o, r, x[:, t, :], ALU.mult, ALU.add)

        def pair_of(w, i):
            return w[:, bass.ds(i * D, D)]

        def pair_rows_of(w, i):
            return w[bass.ds(i * D, D), :]

        def setup():
            load([(x[:, :, :], a["x"].rearrange("b (t p) d -> p (b t) d", p=P)),
                  (ctx_tok[:, :, :], a["ctx_768"].rearrange("b (t p) d -> p (b t) d", p=P)),
                  (ident[:, :], a["c_ident"]), (masks[:, :, :], a["c_masks"]), (head_mask[:, :], a["c_head_mask"]),
                  (rot8[:, :], a["c_rot8"]), (block64[:, :], a["c_block64"])])
            made = signal("consts_made", 4)
            with nc.Block() as block:
                @block.vector
                def _(dve):
                    nc.vector.tensor_copy(ident16[:, :], ident[:, :]).then_inc(made.sem, 1)
                    nc.vector.tensor_copy(masks16[:, :, :], masks[:, :, :]).then_inc(made.sem, 1)
                    nc.vector.memset(ones[:, :], 1.0).then_inc(made.sem, 1)
                    nc.vector.memset(ones16[:, :], 1.0).then_inc(made.sem, 1)
                    dve.wait_ge(made.sem, made.at(0, 4))

            def turn(t):
                def f(o):
                    for q in range(4):
                        last = nc.tensor.transpose(o[0:C, q * P:(q + 1) * P], ctx_tok[:, t + q, :], ident[:, :])
                    return last
                e = ENG[t // 4 % 2]
                return Chunk(e, f, lambda o: copy(e, ctxT[0:C, t * P:(t + 4) * P], o[0:C, :]))
            chunk_block([turn(t) for t in range(0, MT, 4)])

        def l0_attn():
            load([(wq[:, :], a["L0_attn_W"][:, 0:D]), (wk[:, :], a["L0_attn_W"][:, D:2 * D]),
                  (wv[:, :], a["L0_attn_W"][:, 2 * D:3 * D]),
                  (columns(0), col_of(a["L0_attn_b"][0:D])), (columns(1), col_of(a["L0_attn_b"][D:2 * D])),
                  (brow[0:1, 0:D], row_of(a["L0_attn_b"][2 * D:3 * D]))])
            norm(x, NT, D, z, xnT)
            attention(self_units(lambda h, t: qT[:, 0, t * P:(t + 1) * P], all_k, lambda h, t, i: V[:, t, :],
                                 add_store, "all", 1, D),
                      head=self_chunks(qs=float(D) ** -0.5, qbias=columns(0), kbias=columns(1), vbias=brow[0:1, 0:D]))

        def l0_xattn():
            sub = ExitStack()
            with sub:
                def sbl(name, shape):
                    return sub.enter_context(nc.sbuf_tensor("lora_" + name, shape, F32))
                low = {}
                for nm, k in (("q", D), ("k", C), ("v", C)):
                    low[nm] = (sbl(f"{nm}_downT", [RANK, k]), sbl(f"{nm}_up", [RANK, D]), k)
                o_downT, o_up = sbl("o_downT", [RANK, D]), sbl("o_up", [RANK, D])
                raw = {nm: sbl(f"{nm}_raw", [P, D]) for nm in "qkvo"}
                wki, wvi = sbl("wk_ipa", [C, D]), sbl("wv_ipa", [C, D])
                org, img = sbl("org_ctxT", [C, B, P]), sbl("img_ctxT", [C, B, P])
                load([(columns(j), a[f"L0_xattn_{nm}_alpha"].rearrange("(p o) -> p o", o=1).to_broadcast([P, 1]))
                      for j, nm in enumerate("qkvo")]
                     + [(low[nm][0][:, :], a[f"L0_xattn_{nm}_downT"]) for nm in "qkv"]
                     + [(o_up[:, :], a["L0_xattn_o_up"]), (brow[0:1, 0:D], row_of(a["L0_xattn_bo"]))])
                made = signal("ipa_made", 5)
                last_tiles = ctxT[0:C, :].rearrange("c (b t k) -> c b t k", b=B, t=KT)[:, :, KT - 1, :]
                with nc.Block() as block:
                    @block.vector
                    def _(dve):
                        nc.vector.memset(org[:, :, :], 0.0).then_inc(made.sem, 1)
                        nc.vector.memset(img[:, :, :], 0.0).then_inc(made.sem, 1)
                        dve.wait_ge(made.sem, made.at(0, 2))
                        nc.vector.tensor_copy(org[:, :, 0:P - IPA], last_tiles[:, :, 0:P - IPA]).then_inc(made.sem, 1)
                        nc.vector.tensor_copy(img[:, :, P - IPA:P], last_tiles[:, :, P - IPA:P]).then_inc(made.sem, 1)
                        nc.vector.tensor_scalar(columns(4, 8), columns(0, 4), 1.0 / RANK, None,
                                                ALU.mult).then_inc(made.sem, 1)
                        dve.wait_ge(made.sem, made.at(0, 5))
                clear_heads()
                norm(x, NT, D, z, xnT)

                def head_loads(sp, i, s):
                    for nm in "qkv":
                        sp.dma_start(raw[nm][0:low[nm][2], :], pair_of(a[f"L0_xattn_W{nm}"], i)).then_inc(s, 16)
                        sp.dma_start(low[nm][1][:, :], pair_of(a[f"L0_xattn_{nm}_up"], i)).then_inc(s, 16)
                    sp.dma_start(wki[:, :], pair_of(a["L0_xattn_Wk_ipa"], i)).then_inc(s, 16)
                    sp.dma_start(wvi[:, :], pair_of(a["L0_xattn_Wv_ipa"], i)).then_inc(s, 16)

                def tail_loads(sp, i, s):
                    sp.dma_start(raw["o"][:, :], pair_rows_of(a["L0_xattn_Wo"], i)).then_inc(s, 16)
                    sp.dma_start(o_downT[:, :], pair_of(a["L0_xattn_o_downT"], i)).then_inc(s, 16)

                def fold(nm, j, dst):
                    k = P if nm in "qo" else C
                    down, up = (o_downT, o_up) if nm == "o" else low[nm][:2]
                    return Chunk("dve", lambda o: nc.tensor.matmul(o[0:k, 0:D], down[:, 0:k], up[:, :], start=True, stop=True),
                                 lambda o: nc.vector.scalar_tensor_tensor(dst[0:k, :], o[0:k, 0:D], cols[0:k, 4 + j:5 + j],
                                                                          raw[nm][0:k, :], ALU.mult, ALU.add))

                head = [fold("q", 0, wq), fold("k", 1, wk), fold("v", 2, wv)]
                for c in range(2):
                    e = ENG[c % 2]
                    head.append(Chunk(e, mm_T(wq[:, :], xnT, c * HALF),
                                      lambda o, e=e, c=c: put_heads(e, o, c, DH ** -0.5),
                                      after=(0,)))
                for b in range(B):
                    e = ENG[b % 2]

                    def keys(o, b=b):
                        nc.tensor.matmul(o[:, 0:M - IPA], wk[0:C, :], ctxT[0:C, b * M:(b + 1) * M - IPA],
                                         start=True, stop=True)
                        return nc.tensor.matmul(o[:, M - IPA:M], wki[:, :], ctxT[0:C, (b + 1) * M - IPA:(b + 1) * M],
                                                start=True, stop=True)
                    head.append(Chunk(e, keys, lambda o, e=e, b=b: copy(e, kT[:, b * M:(b + 1) * M], o), after=(1,)))
                for b in range(B):
                    e = ENG[b % 2]

                    def vals(o, b=b):
                        for q in range(KT - 1):
                            nc.tensor.matmul(o[:, q * D:(q + 1) * D], ctxT[0:C, b * M + q * P:b * M + (q + 1) * P],
                                             wv[0:C, :], start=True, stop=True)
                        nc.tensor.matmul(o[:, (KT - 1) * D:KT * D], org[:, b, :], wv[0:C, :], start=True, stop=False)
                        return nc.tensor.matmul(o[:, (KT - 1) * D:KT * D], img[:, b, :], wvi[:, :], start=False, stop=True)
                    head.append(Chunk(e, vals, lambda o, e=e, b=b: copy(e, V[:, b * KT:(b + 1) * KT, :], tiles_of(o)),
                                      after=(2,)))
                nh = len(head)
                tail = [fold("o", 3, wo)] + out_chunks(nh + 1, x, wo[:, :])
                for c in tail[3:]:
                    c.after = tuple(c.after) + (nh,)
                attention(cross_units(slot_q, all_k, pair_v, pair_store, 2, DH), iters=PAIRS, head=head, tail=tail,
                          head_loads=head_loads, tail_loads=tail_loads, loads=(8, 2), ipa=True)
                add_row(x, brow[0:1, 0:D])

        def add_row(acc, row):
            chunk_block([Chunk("dve", (lambda o: [nc.tensor.matmul(o[:, q * D:(q + 1) * D], ones[0:1, :], row, start=True,
                                                                   stop=True) for q in range(4)][-1]), add_to(acc, t))
                         for t in range(0, NT, 4)])

        def l0_ffn():
            sub = ExitStack()
            with sub:
                def sbl(name, shape):
                    return sub.enter_context(nc.sbuf_tensor("gqa_" + name, shape, F32))
                cos, sin = sbl("cos8", [P, N]), sbl("sin8", [P, N])
                gate = sbl("gate_w", [P, EXPERTS])
                sums = sbl("rope_sum", [P, 2, T])
                load([(wq[:, :], a["L0_ffn_wqT"]), (wk[:, :], a["L0_ffn_wkT"]), (wv[:, :], a["L0_ffn_wvT"]),
                      (wo[:, :], a["L0_ffn_woT"]), (columns(0), col_of(a["L0_ffn_ln1_w"])),
                      (columns(1), col_of(a["L0_ffn_ln2_w"])), (cos[:, :], a["c_cos8"]), (sin[:, :], a["c_sin8"]),
                      (gate[:, :], a["L0_ffn_gate_wT"])])
                norm(x, NT, D, xin)
                norm(xin, NT, D, z, xnT, rms=True, gain=columns(0))
                chunks = []
                for s, w in ((0, wq), (1, wk)):
                    for c in range(2):
                        chunks.append(Chunk("act", mm_T(w[:, :], xnT, c * HALF),
                                            lambda o, s=s, c=c: copy("act", sums[:, s, c * HALF:(c + 1) * HALF], o,
                                                                     (HS ** -0.5, 1.0)[s])))
                for t in (0, 4):
                    chunks.append(Chunk("dve", mm_tok(xnT, wv[:, :], t), lambda o, t=t: copy("dve", V[:, t:t + 4, :], tiles_of(o))))
                wave = lambda tab: tab[:, :].rearrange("p (o n) -> p o n", o=1).to_broadcast([P, HALF // N, N])
                dsts = (qT[:, 0, :], kT)
                for s in range(2):
                    for c in range(2):
                        chunks.append(Chunk("dve", mm_T(rot8[:, :], sums[:, s, :], c * HALF),
                                            lambda o, s=s, c=c: nc.vector.tensor_tensor(
                                                dsts[s][:, c * HALF:(c + 1) * HALF].rearrange("p (b n) -> p b n", n=N),
                                                o.rearrange("p (b n) -> p b n", n=N), wave(sin), ALU.mult),
                                            after=(2 * s + c,)))
                chunk_block(chunks)
                turned_q = signal("rope_done", 4)
                with nc.Block() as block:
                    @block.vector
                    def _(dve):
                        for s in range(2):
                            v4 = sums[:, s, :].rearrange("p (b n) -> p b n", n=N)
                            nc.vector.tensor_tensor(v4, v4, cos[:, :].rearrange("p (o n) -> p o n", o=1).to_broadcast([P, B, N]),
                                                    ALU.mult).then_inc(turned_q.sem, 1)
                        for s in range(2):
                            dve.wait_ge(turned_q.sem, turned_q.at(0, s + 1))
                            nc.vector.tensor_tensor(dsts[s][:, 0:T], dsts[s][:, 0:T], sums[:, s, :],
                                                    ALU.add).then_inc(turned_q.sem, 1)
                attention(self_units(slot_q, all_k, slot_v, slot_store, "causal", 2, HS), iters=PAIRS, mask_heads=True)
                chunk_block(out_chunks(0, xin, wo[:, :]))
                norm(xin, NT, D, z, xnT, rms=True, gain=columns(1))
                experts(gate)
                add_all(x, xin)

        def add_all(acc, src):
            added = signal("added_all", 1)
            with nc.Block() as block:
                @block.vector
                def _(dve):
                    nc.vector.tensor_tensor(acc[:, :, :], acc[:, :, :], src[:, :, :], ALU.add).then_inc(added.sem, 1)
                    dve.wait_ge(added.sem, added.at(0, 1))

        def experts(gate):
            sub = ExitStack()
            with sub:
                def sbl(name, shape):
                    return sub.enter_context(nc.sbuf_tensor("moe_" + name, shape, F32))
                logit = sbl("logit", [P, NT, EXPERTS])
                prob = sbl("gate_prob", [P, NT, EXPERTS])
                best = sbl("gate_best", [P, NT, 8])
                above = sbl("gate_above", [P, NT, EXPERTS])
                equal = sbl("gate_equal", [P, NT, EXPERTS])
                before = sbl("gate_before", [P, NT, EXPERTS])
                room = sbl("gate_room", [P, NT, 1])
                total = sbl("gate_total", [P, NT, 1])
                share = sbl("gate_share", [P, NT, EXPERTS])
                w13 = sbl("w13", [P, 2 * FFN])
                w2 = sbl("w2", [P, 2, D])
                gated = sbl("gated", [P, 2, T])
                silu = sbl("silu", [P, 2, BANK])
                hT = xnT

                def logits(o):
                    for t in range(NT):
                        last = nc.tensor.matmul(o[:, t * EXPERTS:(t + 1) * EXPERTS], hT[:, t * P:(t + 1) * P], gate[:, :],
                                                start=True, stop=True)
                    return last
                chunk_block([Chunk("dve", logits, lambda o: nc.vector.tensor_copy(
                    logit[:, :, :], o[:, 0:NT * EXPERTS].rearrange("p (t e) -> p t e", e=EXPERTS)))])

                step = signal("gate_step", 64)
                exped = signal("gate_exp", 1)
                with nc.Block() as block:
                    @block.vector
                    def _(dve):
                        done = [0]

                        def then(ins):
                            done[0] += 1
                            ins.then_inc(step.sem, 1)
                            dve.wait_ge(step.sem, step.at(0, done[0]))
                        wide = lambda v: v[:, :, 0:1].to_broadcast([P, NT, EXPERTS])
                        then(nc.vector.tensor_reduce(room[:, :, :], logit[:, :, :], AX.X, ALU.max))
                        then(nc.vector.tensor_tensor(logit[:, :, :], logit[:, :, :], wide(room), ALU.subtract))
                        dve.wait_ge(exped.sem, exped.at(0, 1))
                        then(nc.vector.tensor_reduce(total[:, :, :], prob[:, :, :], AX.X, ALU.add))
                        then(nc.vector.reciprocal(room[:, :, :], total[:, :, :]))
                        then(nc.vector.tensor_tensor(prob[:, :, :], prob[:, :, :], wide(room), ALU.mult))
                        for t in range(NT):
                            then(nc.vector.max(best[:, t, :], prob[:, t, :]))
                        second = best[:, :, 1:2].to_broadcast([P, NT, EXPERTS])
                        then(nc.vector.tensor_tensor(above[:, :, :], prob[:, :, :], second, ALU.is_gt))
                        then(nc.vector.tensor_tensor(equal[:, :, :], prob[:, :, :], second, ALU.is_equal))
                        then(nc.vector.tensor_reduce(room[:, :, :], above[:, :, :], AX.X, ALU.add))
                        then(nc.vector.tensor_scalar(room[:, :, :], room[:, :, :], -1.0, 2.0, ALU.mult, ALU.add))
                        then(nc.vector.memset(before[:, :, 0:1], 0.0))
                        for e in range(1, EXPERTS):
                            then(nc.vector.tensor_tensor(before[:, :, e:e + 1], before[:, :, e - 1:e],
                                                         equal[:, :, e - 1:e], ALU.add))
                        then(nc.vector.tensor_tensor(before[:, :, :], before[:, :, :], wide(room), ALU.is_lt))
                        then(nc.vector.tensor_tensor(equal[:, :, :], equal[:, :, :], before[:, :, :], ALU.mult))
                        then(nc.vector.tensor_tensor(above[:, :, :], above[:, :, :], equal[:, :, :], ALU.add))
                        then(nc.vector.tensor_tensor(share[:, :, :], prob[:, :, :], above[:, :, :], ALU.mult))
                        then(nc.vector.tensor_tensor(total[:, :, :], best[:, :, 0:1], best[:, :, 1:2], ALU.add))
                        then(nc.vector.reciprocal(room[:, :, :], total[:, :, :]))
                        then(nc.vector.tensor_tensor(share[:, :, :], share[:, :, :], wide(room), ALU.mult))

                    @block.scalar
                    def _(act):
                        act.wait_ge(step.sem, step.at(0, 2))
                        nc.scalar.activation(prob[:, :, :], logit[:, :, :], ACT.Exp).then_inc(exped.sem, 1)

                w_in = signal("expert_up_in", 1, EXPERTS, 16)
                w2_in = signal("expert_down_in", 1, EXPERTS, 16)
                up = signal("expert_up", 4, EXPERTS)
                silued = signal("expert_silu", 4, EXPERTS)
                gated_up = signal("expert_gated", 4, EXPERTS)
                down = signal("expert_down", 2, EXPERTS)
                added = signal("expert_added", NT, EXPERTS)
                w13_d, w2_d = a["L0_ffn_w13T"], a["L0_ffn_w2T"]
                with ps("gu", [P, 2, 2, BANK]) as gu, ps("eo", [P, 2, BANK]) as eo, \
                        nc.Block() as block:
                    @block.sync
                    def _(sp):
                        def fetch_up(e):
                            sp.dma_start(w13[:, :], w13_d[:, bass.ds(e * 2 * FFN, 2 * FFN)]).then_inc(w_in.sem, 16)

                        def fetch_down(e):
                            sp.dma_start(w2[:, :, :], w2_d[:, bass.ds(e * 2 * D, 2 * D)].rearrange("p (f d) -> p f d", f=2)).then_inc(w2_in.sem, 16)
                        fetch_up(0)
                        fetch_down(0)
                        with sp.Fori(0, EXPERTS - 1) as e:
                            sp.wait_ge(up.sem, up.at(e, 4))
                            fetch_up(e + 1)
                            sp.wait_ge(down.sem, down.at(e, 2))
                            fetch_down(e + 1)

                    @block.tensor
                    def _(pe):
                        with pe.Fori(0, EXPERTS) as e:
                            pe.wait_ge(w_in.sem, w_in.at(e, 1))
                            for c in range(4):
                                f, th = c // 2, c % 2
                                pe.wait_ge(gated_up.sem, gated_up.at(e, max(0, c - 1)))
                                for g in range(2):
                                    last = nc.tensor.matmul(gu[:, c % 2, g, :], w13[:, g * FFN + f * P:g * FFN + (f + 1) * P],
                                                            hT[:, th * HALF:(th + 1) * HALF], start=True, stop=True)
                                last.then_inc(up.sem, 1)
                            pe.wait_ge(gated_up.sem, gated_up.at(e, 4))
                            pe.wait_ge(w2_in.sem, w2_in.at(e, 1))
                            pe.wait_ge(added.sem, added.at(e, 0))
                            for g in range(2):
                                for q in range(4):
                                    t = 4 * g + q
                                    for f in range(2):
                                        last = nc.tensor.matmul(eo[:, g, q * D:(q + 1) * D], gated[:, f, t * P:(t + 1) * P],
                                                                w2[:, f, :], start=(f == 0), stop=(f == 1))
                                last.then_inc(down.sem, 1)

                    @block.scalar
                    def _(act):
                        with act.Fori(0, EXPERTS) as e:
                            for c in range(4):
                                act.wait_ge(up.sem, up.at(e, c + 1))
                                act.wait_ge(gated_up.sem, gated_up.at(e, max(0, c - 1)))
                                nc.scalar.activation(silu[:, c % 2, :], gu[:, c % 2, 0, :], ACT.Silu).then_inc(silued.sem, 1)

                    @block.vector
                    def _(dve):
                        with dve.Fori(0, EXPERTS) as e:
                            dve.wait_ge(down.sem, down.at(e, 0))
                            for c in range(4):
                                f, th = c // 2, c % 2
                                dve.wait_ge(silued.sem, silued.at(e, c + 1))
                                nc.vector.tensor_tensor(gated[:, f, th * HALF:(th + 1) * HALF], silu[:, c % 2, :],
                                                        gu[:, c % 2, 1, :], ALU.mult).then_inc(gated_up.sem, 1)
                            for t in range(NT):
                                dve.wait_ge(down.sem, down.at(e, t // 4 + 1))
                                nc.vector.scalar_tensor_tensor(xin[:, t, :], eo[:, t // 4, (t % 4) * D:(t % 4 + 1) * D],
                                                               share[:, t, bass.ds(e, 1)], xin[:, t, :], ALU.mult,
                                                               ALU.add).then_inc(added.sem, 1)

        def l1_attn():
            w = a["L1_attn_Wqkv"]
            load([(wq[:, :], w[:, 0:D]), (wk[:, :], w[:, D:2 * D]), (wv[:, :], w[:, 2 * D:3 * D]),
                  (columns(0), col_of(a["L1_attn_bqkv"][0:D])), (columns(1), col_of(a["L1_attn_bqkv"][D:2 * D])),
                  (brow[0:1, 0:D], row_of(a["L1_attn_bqkv"][2 * D:3 * D])),
                  (brow[0:1, D:2 * D], row_of(a["L1_attn_bout"])), (wo[:, :], a["L1_attn_Wout"])])
            norm(x, NT, D, z, xnT)
            chunk_block(self_chunks(qs=float(D) ** -0.5, qbias=columns(0), kbias=columns(1), vbias=brow[0:1, 0:D]))
            attention(self_units(slot_q, all_k, slot_v, slot_store, "near", 2, HS), iters=PAIRS, mask_heads=True)
            chunk_block(out_chunks(0, x, wo[:, :], bias=brow[0:1, D:2 * D]))

        def context_chunks(qs, qbias=None, kbias=None, vbias=None):
            cs = []
            for c in range(2):
                d = qT[:, 0, c * HALF:(c + 1) * HALF]
                if qbias is None:
                    cs.append(Chunk(ENG[c], mm_T(wq[:, :], xnT, c * HALF), lambda o, c=c: put_heads(ENG[c], o, c, qs)))
                else:
                    cs.append(Chunk("dve", mm_T(wq[:, :], xnT, c * HALF),
                                    lambda o, d=d: nc.vector.tensor_scalar(d, o, qbias, qs, ALU.add, ALU.mult)))
            for b in range(B):
                e, d = ENG[b % 2], kT[:, b * M:(b + 1) * M]
                cs.append(Chunk(e, mm_T(wk[0:C, :], ctxT, b * M, k=C),
                                (lambda o, e=e, d=d: copy(e, d, o)) if kbias is None else
                                (lambda o, e=e, d=d: affine(e, d, o, 1.0, kbias))))
            for b in range(B):
                e = ENG[b % 2]
                cs.append(Chunk(e, mm_tok(ctxT, wv[0:C, :], b * KT, k=C, bias=vbias),
                                lambda o, e=e, b=b: copy(e, V[:, b * KT:(b + 1) * KT, :], tiles_of(o))))
            return cs

        def l1_xattn():
            p = lambda s: a["L1_xattn_" + s]
            load([(wq[:, :], p("wq")), (wk[0:C, :], p("wk")), (wv[0:C, :], p("wv")), (wo[:, :], p("wo")),
                  (columns(0), col_of(p("bq"))), (columns(1), col_of(p("bk"))), (brow[0:1, 0:D], row_of(p("bv"))),
                  (brow[0:1, D:2 * D], row_of(p("bo")))])
            norm(x, NT, D, z, xnT)
            chunk_block(context_chunks(HS ** -0.5, columns(0), columns(1), brow[0:1, 0:D]))
            attention(cross_units(slot_q, all_k, slot_v, slot_store, 2, HS), iters=PAIRS, mask_heads=True)
            chunk_block(out_chunks(0, x, wo[:, :], bias=brow[0:1, D:2 * D]))

        def l1_ffn():
            load([(wq[:, :], a["L1_ffn_W_rT"]), (wk[:, :], a["L1_ffn_W_kT"]), (wv[:, :], a["L1_ffn_W_vT"]),
                  (columns(0), col_of(a["L1_ffn_mu_r"])), (columns(1), col_of(a["L1_ffn_mu_k"]))])
            norm(x, NT, D, z, xnT)
            mixed = signal("mixed", 9)
            prev = V[:, 0:NT, :].rearrange("p t d -> p (t d)").rearrange("p (b n) -> p b n", b=B)
            now = xnT[:, :].rearrange("p (b n) -> p b n", b=B)
            r, k, act_k = qT[:, 0, :], qT[:, 1, :], kT[:, 0:T]
            with nc.Block() as block:
                @block.vector
                def _(dve):
                    nc.vector.memset(prev[:, :, 0:1], 0.0).then_inc(mixed.sem, 1)
                    nc.vector.tensor_copy(prev[:, :, 1:N], now[:, :, 0:N - 1]).then_inc(mixed.sem, 1)
                    nc.vector.tensor_scalar(columns(2, 4), columns(0, 2), -1.0, 1.0, ALU.mult, ALU.add).then_inc(mixed.sem, 1)
                    dve.wait_ge(mixed.sem, mixed.at(0, 3))
                    flat = V[:, 0:NT, :].rearrange("p t d -> p (t d)")
                    nc.vector.tensor_scalar(r, flat, columns(2), None, ALU.mult).then_inc(mixed.sem, 1)
                    nc.vector.tensor_scalar(k, flat, columns(3), None, ALU.mult).then_inc(mixed.sem, 1)
                    dve.wait_ge(mixed.sem, mixed.at(0, 5))
                    nc.vector.scalar_tensor_tensor(r, xnT[:, :], columns(0), r, ALU.mult, ALU.add).then_inc(mixed.sem, 2)
                    nc.vector.scalar_tensor_tensor(k, xnT[:, :], columns(1), k, ALU.mult, ALU.add).then_inc(mixed.sem, 2)
            sig = heads_out
            chunks = []
            for t in (0, 4):
                chunks.append(Chunk("act", mm_tok(r, wq[:, :], t),
                                    lambda o, t=t: nc.scalar.activation(sig[:, t:t + 4, :], tiles_of(o), ACT.Sigmoid)))
            for c in range(2):
                chunks.append(Chunk("dve", mm_T(wk[:, :], k, c * HALF),
                                    lambda o, c=c: nc.vector.tensor_scalar(outT[:, c * HALF:(c + 1) * HALF], o, 0.0, None, ALU.max)))
            chunk_block(chunks)
            squared = signal("squared", 1)
            with nc.Block() as block:
                @block.scalar
                def _(act):
                    nc.scalar.activation(act_k, outT[:, :], ACT.Square).then_inc(squared.sem, 1)
            chunk_block([Chunk("dve", mm_tok(kT, wv[:, :], t),
                               lambda o, t=t: nc.vector.tensor_tensor(z[:, t:t + 4, :], sig[:, t:t + 4, :], tiles_of(o), ALU.mult))
                         for t in (0, 4)])
            add_all(x, z)

        def wide_loads(pre, wo_name):
            def head_loads(sp, i, s):
                for nm, buf, k in pre:
                    sp.dma_start(buf[0:k, :], pair_of(a[nm], i)).then_inc(s, 16)

            def tail_loads(sp, i, s):
                sp.dma_start(wo[:, :], pair_rows_of(a[wo_name], i)).then_inc(s, 16)
            return dict(head_loads=head_loads, tail_loads=tail_loads, loads=(len(pre), 1))

        def l2_attn():
            clear_heads()
            norm(x, NT, D, z, xnT)
            head = self_chunks(split=True)
            attention(self_units(slot_q, all_k, pair_v, pair_store, "causal", 2, DH), iters=PAIRS, head=head,
                      tail=out_chunks(len(head), x, wo[:, :]),
                      **wide_loads((("L2_attn_QT", wq, D), ("L2_attn_KT", wk, D), ("L2_attn_VT", wv, D)), "L2_attn_OT"))

        def l3_xattn():
            load([(brow[0:1, 0:D], row_of(a["L3_xattn_b_out"]))])
            clear_heads()
            norm(x, NT, D, z, xnT)
            head = context_chunks(DH ** -0.5)
            attention(cross_units(slot_q, all_k, pair_v, pair_store, 2, DH), iters=PAIRS, head=head,
                      tail=out_chunks(len(head), x, wo[:, :]),
                      **wide_loads((("L3_xattn_w_q", wq, D), ("L3_xattn_w_k", wk, C), ("L3_xattn_w_v", wv, C)), "L3_xattn_w_out"))
            add_row(x, brow[0:1, 0:D])

        def l2_xattn():
            sub = ExitStack()
            with sub:
                def sbl(name, shape, dt=F32):
                    return sub.enter_context(nc.sbuf_tensor("latent_" + name, shape, dt))
                p = lambda s: a["L2_xattn_" + s]
                wlk, wlv = sbl("wlk", [P, D]), sbl("wlv", [P, D])
                ctx_z, ctx_nT = sbl("ctx_z", [P, MT, C]), sbl("ctx_nT", [P, B * M])
                keep8, keep = sbl("keep8", [1, B * M], U8), sbl("keep", [1, B * M], BF16)
                squares, root = sbl("squares", [P, 4 * T]), sbl("root", [P, 4 * T])
                two = lambda v: v.rearrange("(o d) -> o d", o=1)
                load([(wq[:, :], p("WqT")), (wk[0:C, :], p("WkT")), (wv[0:C, :], p("WvT")), (wlk[:, :], p("WlkT")),
                      (wlv[:, :], p("WlvT")), (wo[:, :], p("WoT")), (cols[0:C, 0:1], col_of(p("ln_x_g"))),
                      (cols[0:C, 1:2], col_of(p("ln_x_b"))), (columns(2), col_of(p("ln_l_g"))),
                      (columns(3), col_of(p("ln_l_b"))), (cols[0:DH, 4:5], col_of(p("qn_g"))),
                      (cols[DH:2 * DH, 4:5], col_of(p("qn_g"))), (cols[0:DH, 5:6], col_of(p("kn_g"))),
                      (cols[DH:2 * DH, 5:6], col_of(p("kn_g"))), (brow[0:1, 0:D], row_of(p("bo"))),
                      (keep8[:, :], a["mask_BxS2_bk0"])])
                kept = signal("mask_made", 2)
                with nc.Block() as block:
                    @block.vector
                    def _(dve):
                        nc.vector.tensor_scalar(keep[:, :], keep8[:, :], -1.0, -NEG, ALU.add, ALU.mult).then_inc(kept.sem, 1)
                        nc.vector.tensor_scalar(columns(4), columns(4), DH ** -0.5, None, ALU.mult).then_inc(kept.sem, 1)
                clear_heads()
                norm(ctx_tok, MT, C, ctx_z, ctx_nT, gain=columns(0), bias=columns(1))
                norm(x, NT, D, z)
                norm(z, NT, D, heads_out, xnT, gain=columns(2), bias=columns(3))

                k4 = kT[:, :].rearrange("p (b m) -> p b m", b=B)
                chunks = []
                q0 = [(qT[:, 0, c * HALF:(c + 1) * HALF], squares[:, c * HALF:(c + 1) * HALF],
                       mm_T(wq[:, :], xnT, c * HALF), None) for c in range(2)]
                sq4 = squares[:, T:4 * T].rearrange("p (b m) -> p b m", b=B)
                kc = [(k4[:, b, 0:M], sq4[:, b, 0:M], mm_T(wk[0:C, :], ctx_nT, b * M, k=C), None) for b in range(B)]
                kl = [(k4[:, 2 * c:2 * c + 2, M:M + N], sq4[:, 2 * c:2 * c + 2, M:M + N], mm_T(wlk[:, :], xnT, c * HALF), 2)
                      for c in range(2)]
                for dst, sq, mm, split in q0 + kc + kl:
                    def both(o, dst=dst, sq=sq, split=split):
                        o = o if split is None else o.rearrange("p (b n) -> p b n", b=split)
                        nc.scalar.activation(dst, o, ACT.Copy)
                        return nc.scalar.activation(sq, o, ACT.Square)
                    chunks.append(Chunk("act", mm, both))
                for b in range(B):
                    chunks.append(Chunk("dve", mm_tok(ctx_nT, wv[0:C, :], b * KT, k=C),
                                        lambda o, b=b: copy("dve", V[:, b * KT:(b + 1) * KT, :], tiles_of(o))))
                for t in (0, 4):
                    chunks.append(Chunk("dve", mm_tok(xnT, wlv[:, :], t),
                                        lambda o, t=t: copy("dve", V[:, MT + t:MT + t + 4, :], tiles_of(o))))
                chunk_block(chunks)
                chunk_block([Chunk("dve", mm_T(block64[:, :], squares, c * HALF),
                                   lambda o, c=c: nc.vector.tensor_scalar(root[:, c * HALF:(c + 1) * HALF], o, 1.0 / DH, 1e-16,
                                                                          ALU.mult, ALU.max))
                             for c in range(4 * T // HALF)])
                rooted, inverted, scaled = signal("qk_rooted", 4), signal("qk_inverted", 4), signal("qk_scaled", 4)
                with nc.Block() as block:
                    @block.scalar
                    def _(act):
                        for c in range(4):
                            v = root[:, c * T:(c + 1) * T]
                            nc.scalar.activation(v, v, ACT.Sqrt).then_inc(rooted.sem, 1)

                    @block.vector
                    def _(dve):
                        for c in range(4):
                            v = root[:, c * T:(c + 1) * T]
                            dve.wait_ge(rooted.sem, rooted.at(0, c + 1))
                            nc.vector.reciprocal(v, v).then_inc(inverted.sem, 1)
                            dve.wait_ge(inverted.sem, inverted.at(0, c + 1))
                            if c == 0:
                                for h in range(2):
                                    r = pair_rows(h)
                                    last = nc.vector.scalar_tensor_tensor(qM[r, h, :], qT[r, 0, :], cols[r, 4:5],
                                                                          root[r, 0:T], ALU.mult, ALU.mult)
                            else:
                                d = kT[:, (c - 1) * T:c * T]
                                last = nc.vector.scalar_tensor_tensor(d, d, columns(5), v, ALU.mult, ALU.mult)
                            last.then_inc(scaled.sem, 1)
                us = []
                for h in range(2):
                    for b in range(B):
                        for qt in range(QT):
                            t = b * QT + qt
                            q = slot_q(h, t)
                            seg = [(0, M, q, k4[:, b, 0:M], [(ones16[0:1, :], keep[0:1, b * M:(b + 1) * M], 0, M)]),
                                   (M, N, q, k4[:, b, M:M + N], [])]
                            us.append(Unit(M + N, score_mm(seg),
                                           lambda j, i, h=h, b=b: V[:, b * KT + j if j < KT else MT + b * QT + j - KT, pair_rows(h)],
                                           pair_store(h, t), DH))
                attention(us, wide=2)
                chunk_block(out_chunks(0, x, wo[:, :], bias=brow[0:1, 0:D]))

        def l2_ffn():
            sub = ExitStack()
            with sub:
                def sbl(name, shape):
                    return sub.enter_context(nc.sbuf_tensor("fp4_" + name, shape, F32))
                FT = 3
                FP = [P, P, FP4_FFN - 2 * P]
                w_up = sbl("w_up", [P, 2 * FT, D])
                w_down = sbl("w_down", [P, FP4_FFN])
                wT = sbl("w_upT", [P, 2, FP4_FFN])
                wdT = sbl("w_downT", [P, FT, D])
                hid = sbl("hid", [P, NT, FP4_FFN])
                hidT = sbl("hidT", [P, FT, T])
                silu = sbl("silu", [P, NT, FP4_FFN])
                big = NT * FP4_FFN
                mag, sgn = sbl("mag", [P, big]), sbl("sgn", [P, big])
                amax, inv = sbl("amax", [P, big // FP4_BLOCK]), sbl("amax_inv", [P, big // FP4_BLOCK])
                cleared = signal("fp4_cleared", 1)
                with nc.Block() as block:
                    @block.vector
                    def _(dve):
                        nc.vector.memset(w_up[:, :, :], 0.0).then_inc(cleared.sem, 1)
                        dve.wait_ge(cleared.sem, cleared.at(0, 1))
                pairs = [(w_down[:, :], a["L2_ffn_w_down"])]
                for g, nm in enumerate(("L2_ffn_w_gate", "L2_ffn_w_up")):
                    for f in range(FT):
                        pairs.append((w_up[0:FP[f], g * FT + f, :], a[nm][f * P:f * P + FP[f], :]))
                load(pairs)

                def quantize(v, width):
                    nb = width // FP4_BLOCK
                    blocks = lambda t: t[:, 0:width].rearrange("p (n k) -> p n k", k=FP4_BLOCK)
                    of_block = lambda t: t[:, 0:nb].rearrange("p (n o) -> p n o", o=1).to_broadcast([P, nb, FP4_BLOCK])
                    step, side = signal("fp4_step", 32), signal("fp4_sign", 2)
                    with nc.Block() as block:
                        @block.scalar
                        def _(act):
                            nc.scalar.activation(sgn[:, 0:width], v, ACT.Sign).then_inc(side.sem, 1)
                            nc.scalar.activation(mag[:, 0:width], v, ACT.Abs).then_inc(side.sem, 1)

                        @block.vector
                        def _(dve):
                            done = [0]

                            def then(ins):
                                done[0] += 1
                                ins.then_inc(step.sem, 1)
                                dve.wait_ge(step.sem, step.at(0, done[0]))
                            m = mag[:, 0:width]
                            dve.wait_ge(side.sem, side.at(0, 2))
                            then(nc.vector.tensor_reduce(amax[:, 0:nb], blocks(mag), AX.X, ALU.max))
                            then(nc.vector.tensor_scalar(amax[:, 0:nb], amax[:, 0:nb], 1.0 / 6.0, 1e-12, ALU.mult, ALU.max))
                            then(nc.vector.reciprocal(inv[:, 0:nb], amax[:, 0:nb]))
                            then(nc.vector.tensor_tensor(blocks(mag), blocks(mag), of_block(inv), ALU.mult))
                            then(nc.vector.tensor_scalar(v, m, 5.0, 2.0, ALU.is_gt, ALU.mult))
                            then(nc.vector.scalar_tensor_tensor(v, m, 3.5, v, ALU.is_gt, ALU.add))
                            then(nc.vector.scalar_tensor_tensor(v, m, 2.5, v, ALU.is_gt, ALU.add))
                            then(nc.vector.tensor_scalar(v, v, 2.0, None, ALU.mult))
                            for mid in (1.75, 1.25, 0.75, 0.25):
                                then(nc.vector.scalar_tensor_tensor(v, m, mid, v, ALU.is_gt, ALU.add))
                            then(nc.vector.scalar_tensor_tensor(v, v, 0.5, sgn[:, 0:width], ALU.mult, ALU.mult))
                            v3 = v.rearrange("p (n k) -> p n k", k=FP4_BLOCK)
                            then(nc.vector.tensor_tensor(v3, v3, of_block(amax), ALU.mult))
                            while done[0] < 32:
                                then(nc.vector.memset(inv[:, 0:1], 0.0))

                flat = lambda t: t.rearrange("p t d -> p (t d)")
                quantize(flat(w_up[:, :, :]), 2 * FT * D)
                quantize(w_down[:, :], FP4_FFN)
                norm(x, NT, D, z)
                quantize(flat(z[:, :, :]), T)

                chunks = [turn_chunk("act", z, 0, xnT), turn_chunk("dve", z, 4, xnT)]

                def turn_rows(g):
                    def f(o):
                        for j in range(FT):
                            last = nc.tensor.transpose(o[:, j * P:j * P + FP[j]], w_up[0:FP[j], g * FT + j, :],
                                                       ident[0:FP[j], 0:FP[j]])
                        return last
                    return Chunk(ENG[g], f, lambda o: copy(ENG[g], wT[:, g, :], o[:, 0:FP4_FFN]))
                chunks += [turn_rows(0), turn_rows(1)]

                def turn_down(j):
                    return Chunk("dve", lambda o: nc.tensor.transpose(o[0:FP[j], 0:D], w_down[:, j * P:j * P + FP[j]], ident[:, :]),
                                 lambda o: copy("dve", wdT[0:FP[j], j, :], o[0:FP[j], 0:D]))
                chunks += [turn_down(j) for j in range(FT)]
                chunk_block(chunks)
                chunks = []
                for t in range(NT):
                    for g in range(2):
                        mm = lambda o, t=t, g=g: nc.tensor.matmul(o[:, 0:FP4_FFN], xnT[:, t * P:(t + 1) * P], wT[:, g, :],
                                                                  start=True, stop=True)
                        if g == 0:
                            chunks.append(Chunk("act", mm, lambda o, t=t: nc.scalar.activation(silu[:, t, :], o[:, 0:FP4_FFN], ACT.Silu)))
                        else:
                            chunks.append(Chunk("dve", mm, lambda o, t=t: nc.vector.tensor_tensor(hid[:, t, :], o[:, 0:FP4_FFN], silu[:, t, :], ALU.mult),
                                                after=(2 * t,)))
                chunk_block(chunks)
                quantize(flat(hid[:, :, :]), big)
                chunks = []
                for j in range(FT):
                    for t in (0, 4):
                        def turn(o, j=j, t=t):
                            for q in range(4):
                                last = nc.tensor.transpose(o[0:FP[j], q * P:(q + 1) * P], hid[:, t + q, j * P:j * P + FP[j]], ident[:, :])
                            return last
                        e = ENG[t // 4]
                        chunks.append(Chunk(e, turn, lambda o, e=e, j=j, t=t: copy(e, hidT[0:FP[j], j, t * P:(t + 4) * P], o[0:FP[j], :])))
                for t in (0, 4):
                    def downs(o, t=t):
                        for q in range(4):
                            for j in range(FT):
                                last = nc.tensor.matmul(o[:, q * D:(q + 1) * D], hidT[0:FP[j], j, (t + q) * P:(t + q + 1) * P],
                                                        wdT[0:FP[j], j, :], start=(j == 0), stop=(j == FT - 1))
                        return last
                    chunks.append(Chunk("dve", downs, add_to(x, t), after=tuple(range(2 * FT))))
                chunk_block(chunks)

        def l3_attn():
            DQ = 64
            load([(wq[:, 0:DQ], a["L3_attn_Wq"]), (wk[:, 0:DQ], a["L3_attn_Wk"]), (wv[:, :], a["L3_attn_Wv"])])
            norm(x, NT, D, z, xnT)
            attention(self_units(lambda h, t: qT[0:DQ, 0, t * P:(t + 1) * P], lambda h, k0, w: kT[0:DQ, k0:k0 + w],
                                 lambda h, t, i: V[:, t, :], add_store, "causal", 1, D),
                      head=self_chunks(qs=float(DQ) ** -0.5, m=DQ))

        def l3_ffn():
            sub = ExitStack()
            with sub:
                def sbl(name, shape, dt=F32):
                    return sub.enter_context(nc.sbuf_tensor("net_" + name, shape, dt))
                p = lambda s: a["L3_ffn_" + s]
                INNER, HALVES = H * DH, H * DH // BANK
                GT = [P, P, GLU - 2 * P]
                NK = WINDOW + P
                raw = sbl("raw_qk", [P, NT, 2, INNER])
                vals = sbl("vals", [P, NT, INNER])
                w_qkv = sbl("w_qkv", [P, 3 * INNER])
                w_out = sbl("w_out", [P, PAIRS, D])
                w1 = sbl("w1", [P, 2 * GLU])
                w2 = sbl("w2", [P, 3, D])
                vec = sbl("layer_cols", [P, 8])
                qk_scale = sbl("qk_scale", [P, DEPTH * 2, DH])
                waves = sbl("waves", [P, QT, 2, 2, DH])
                tables = sbl("tables", [P, QT, 2, 2, DH])
                norms = sbl("qk_norms", [P, NT, 2, H])
                unit = sbl("unit_qk", [P, 4, 2, D])
                turned_cos = sbl("cos_qk", [P, NT, 2, D])
                turned_sin = sbl("sin_qk", [P, 4, 2, D])
                q_slots = sbl("q_slots", [P, 2, T])
                k_rows = sbl("k_rows", [P, T])
                probs0 = sbl("probs_first", [P, 2, 2, P])
                probs1 = sbl("probs_second", [P, 2, 2, 2 * P])
                flat_p = sbl("probs_turned", [P, 4, BANK])
                squares = flat_p
                maxima, sums, inverse = sbl("negmax", [P, NT, 2]), sbl("sums", [P, NT, 2]), sbl("inverse", [P, NT, 2])
                late = sbl("late", [P, 2, P])
                window, window16 = sbl("window", [P, NK]), sbl("window16", [P, NK], BF16)
                heads_T = vals[:, :, :].rearrange("p t d -> p (t d)").rearrange("p (c t) -> p c t", c=PAIRS)
                flat_raw = raw[:, :, :, :].rearrange("p t s d -> p (t s d)")
                acts = flat_raw[:, 0:3 * T].rearrange("p (j t) -> p j t", j=3)
                gelu = flat_raw[:, 3 * T:3 * T + 2 * BANK].rearrange("p (s n) -> p s n", s=2)
                by_batch = lambda v: v.rearrange("p (b n) -> p b n", b=B)
                qkv_in = signal("qkv_weights_in", 1, DEPTH + 1, 16)
                NLOADS = 9
                loaded = signal("layer_loads", NLOADS, DEPTH, 16)
                load([(waves[:, :, :, :, :], a["c_waves"].rearrange("p t (s w d) -> p t s w d", s=2, w=2)),
                      (late[:, :, :], a["c_late"]), (window[:, :], a["c_window"]),
                      (qk_scale[:, :, :], p("qk_scale").to_broadcast([P, DEPTH * 2 * DH]).rearrange("p (s d) -> p s d", d=DH))])
                made = signal("window_made", 3)
                with nc.Block() as block:
                    @block.sync
                    def _(sp):
                        sp.dma_start(w_qkv[:, :], p("Wqkv")[0]).then_inc(qkv_in.sem, 16)

                    @block.vector
                    def _(dve):
                        nc.vector.tensor_copy(window16[:, :], window[:, :]).then_inc(made.sem, 1)
                        nc.vector.memset(q_slots[:, :, :], 0.0).then_inc(made.sem, 1)
                        nc.vector.memset(probs1[:, :, :, 0:P - WINDOW], 0.0).then_inc(made.sem, 1)
                norm(x, NT, D, xin)

                with nc.Fori(0, DEPTH) as l:
                    cleared = signal("shift_cleared", 1, DEPTH)
                    turned_in = signal("shift_turned", 2, DEPTH)
                    lower = signal("shift_lower", 2, DEPTH)
                    upper = signal("shift_upper", 2, DEPTH)
                    with ps("bank", [P, 2, BANK]) as bank, nc.Block() as block:
                        @block.tensor
                        def _(pe):
                            pe.wait_ge(qkv_in.sem, qkv_in.at(l, 1))
                            for j in range(2):
                                for q in range(4):
                                    last = nc.tensor.transpose(bank[:, j, q * P:(q + 1) * P], xin[:, 4 * j + q, :], ident[:, :])
                                last.then_inc(turned_in.sem, 1)

                        @block.scalar
                        def _(act):
                            for j in range(2):
                                act.wait_ge(turned_in.sem, turned_in.at(l, j + 1))
                                copy("act", xnT[0:D // 2, j * BANK:(j + 1) * BANK], bank[0:D // 2, j, :]).then_inc(lower.sem, 1)

                        @block.vector
                        def _(dve):
                            up = slice(D // 2, D)
                            nc.vector.memset(by_batch(xnT[up, :])[:, :, 0:1], 0.0).then_inc(cleared.sem, 1)
                            for j in range(2):
                                dve.wait_ge(turned_in.sem, turned_in.at(l, j + 1))
                                copy("dve", by_batch(xnT[up, :])[:, 2 * j:2 * j + 2, 1:N],
                                     bank[up, j, :].rearrange("p (b n) -> p b n", b=2)[:, :, 0:N - 1]).then_inc(upper.sem, 1)

                    project(l, p, raw, vals, w_qkv, squares, norms, waves, tables, qk_scale, qkv_in, loaded, NLOADS,
                            (vec, w1, w2, w_out, GT))
                    local_attention(l, p, raw, vals, w_qkv, norms, tables, unit, turned_cos, turned_sin, q_slots, k_rows,
                                    probs0, probs1, flat_p, maxima, sums, inverse, window16, qkv_in)

                    chunks = []
                    for c in range(PAIRS):
                        for t in (0, 4):
                            def turn(o, c=c, t=t):
                                for q in range(4):
                                    last = nc.tensor.transpose(o[:, q * P:(q + 1) * P], raw[:, t + q, 0, c * D:(c + 1) * D], ident[:, :])
                                return last
                            e = ENG[t // 4]
                            chunks.append(Chunk(e, turn, lambda o, e=e, c=c, t=t: copy(e, heads_T[:, c, t * P:(t + 4) * P], o)))
                    for t in (0, 4):
                        def outs(o, t=t):
                            for q in range(4):
                                for c in range(PAIRS):
                                    last = nc.tensor.matmul(o[:, q * D:(q + 1) * D], heads_T[:, c, (t + q) * P:(t + q + 1) * P],
                                                            w_out[:, c, :], start=(c == 0), stop=(c == PAIRS - 1))
                            return last
                        chunks.append(Chunk("dve", outs, add_to(xin, t), after=tuple(range(t // 4, 2 * PAIRS, 2))))
                    chunk_block(chunks, n=l, iters=DEPTH, tag="heads_")

                    shifted = signal("late_shifted", 2, DEPTH)
                    moved = signal("late_moved", 3, DEPTH)
                    with ps("bank", [P, 2, BANK]) as bank, nc.Block() as block:
                        half = D // 2
                        tiles = lambda v, q: v[:, :, half:D].rearrange("p (b q) d -> p b q d", q=QT)[:, :, q, :]
                        late_bank = lambda q: bank[:, q, 0:B * half]

                        @block.tensor
                        def _(pe):
                            nc.tensor.matmul(late_bank(0), late[:, 0, :], tiles(xin, 0), start=True, stop=True).then_inc(shifted.sem, 1)
                            nc.tensor.matmul(late_bank(1), late[:, 0, :], tiles(xin, 1), start=True, stop=False)
                            nc.tensor.matmul(late_bank(1), late[:, 1, :], tiles(xin, 0), start=False, stop=True).then_inc(shifted.sem, 1)

                        @block.scalar
                        def _(act):
                            copy("act", z[:, :, 0:half], xin[:, :, 0:half]).then_inc(moved.sem, 1)

                        @block.vector
                        def _(dve):
                            for q in range(QT):
                                dve.wait_ge(shifted.sem, shifted.at(l, q + 1))
                                copy("dve", tiles(z, q), late_bank(q).rearrange("p (b d) -> p b d", b=B)).then_inc(moved.sem, 1)
                    norm(z, NT, D, z, xnT, gain=vec[:, 0:1], bias=vec[:, 1:2], n=l, iters=DEPTH)
                    chunks = []
                    for j in range(3):
                        g = GT[j]
                        for c in range(2):
                            k = len(chunks)
                            cc = slice(c * HALF, (c + 1) * HALF)
                            chunks.append(Chunk("act", mm_T(w1[:, GLU + j * P:GLU + j * P + g], xnT, c * HALF, m=g),
                                                lambda o, g=g, j=j, c=c: nc.scalar.activation(gelu[0:g, c, :], o[0:g, :], ACT.Gelu,
                                                                                              bias=vec[0:g, 5 + j:6 + j]),
                                                after=(k - 3,) if j else ()))
                            chunks.append(Chunk("dve", mm_T(w1[:, j * P:j * P + g], xnT, c * HALF, m=g),
                                                lambda o, g=g, j=j, c=c, cc=cc: nc.vector.scalar_tensor_tensor(
                                                    acts[0:g, j, cc], o[0:g, :], vec[0:g, 2 + j:3 + j], gelu[0:g, c, :], ALU.add, ALU.mult),
                                                after=(k,)))
                    for t in (0, 4):
                        def downs(o, t=t):
                            for q in range(4):
                                for j in range(3):
                                    nc.tensor.matmul(o[:, q * D:(q + 1) * D], acts[0:GT[j], j, (t + q) * P:(t + q + 1) * P],
                                                     w2[0:GT[j], j, :], start=(j == 0), stop=False)
                                last = nc.tensor.matmul(o[:, q * D:(q + 1) * D], ones[0:1, :], brow[0:1, 0:D], start=False, stop=True)
                            return last
                        chunks.append(Chunk("dve", downs, add_to(xin, t), after=(11,)))
                    chunk_block(chunks, n=l, iters=DEPTH, tag="glu_")
                with nc.Block() as block:
                    @block.sync
                    def _(sp):
                        sp.wait_ge(qkv_in.sem, qkv_in.at(DEPTH, 1))
                add_all(x, xin)

        def project(l, p, raw, vals, w_qkv, squares, norms, waves, tables, qk_scale, qkv_in, loaded, nloads, buffers):
            vec, w1, w2, w_out, GT = buffers
            INNER, HALVES = H * DH, H * DH // BANK
            HB = BANK // DH
            BANKS, SLOTS, LAG = 3 * NT, 8, 2
            total = DEPTH * HALVES
            filled = signal("qkv_filled", BANKS, total)
            copied = signal("qk_copied", 2 * NT, total)
            v_copied = signal("v_copied", NT, total)
            squared = signal("qk_squared", 2 * NT, total)
            added = signal("squares_added", 2 * NT, total)
            tabled = signal("tables_made", 6, DEPTH)
            guarded = signal("squares_guarded", 1, DEPTH)
            rooted = signal("norms_rooted", 1, DEPTH)
            inverted = signal("norms_inverted", 1, DEPTH)
            all_norms = norms[:, :, :, :].rearrange("p t s h -> p (t s h)")
            with ps("bank", [P, SLOTS, BANK]) as bank, nc.Block() as block:
                @block.sync
                def _(sp):
                    one = lambda w: w[bass.ds(l, 1), :]
                    sp.dma_start(w_out[:, :, :], p("Wo")[bass.ds(l, 1), :, :].rearrange("o (c p) d -> p (o c) d", p=P)).then_inc(loaded.sem, 16)
                    sp.dma_start(vec[:, 0:1], one(p("ln_g")).rearrange("o d -> d o")).then_inc(loaded.sem, 16)
                    sp.dma_start(vec[:, 1:2], one(p("ln_b")).rearrange("o d -> d o")).then_inc(loaded.sem, 16)
                    sp.dma_start(vec[:, 2:8], p("b1c")[bass.ds(l, 1), :, :].rearrange("o p c -> p (o c)")).then_inc(loaded.sem, 16)
                    sp.dma_start(brow[0:1, 0:D], one(p("b2"))).then_inc(loaded.sem, 16)
                    sp.dma_start(w1[:, :], p("W1")[bass.ds(l, 1), :, :].rearrange("o p c -> p (o c)")).then_inc(loaded.sem, 16)
                    for j in range(3):
                        sp.dma_start(w2[0:GT[j], j, :], p("W2")[bass.ds(l, 1), j * P:j * P + GT[j], :].rearrange("o p c -> (o p) c")).then_inc(loaded.sem, 16)

                @block.tensor
                def _(pe):
                    with pe.Fori(0, HALVES) as c:
                        n = l * HALVES + c
                        for j in range(BANKS):
                            t, kind = (j - SLOTS) // 3, (j - SLOTS) % 3
                            if kind < 2:
                                pe.wait_ge(copied.sem, copied.at(n, 2 * t + kind + 1))
                            else:
                                pe.wait_ge(v_copied.sem, v_copied.at(n, t + 1))
                            nc.tensor.matmul(bank[:, j % SLOTS, :], xnT[:, j // 3 * P:(j // 3 + 1) * P],
                                             w_qkv[:, bass.ds(c * BANK + (j % 3) * INNER, BANK)],
                                             start=True, stop=True).then_inc(filled.sem, 1)

                @block.scalar
                def _(act):
                    with act.Fori(0, HALVES) as c:
                        n = l * HALVES + c
                        for t in range(NT):
                            for kind in range(2):
                                u = 2 * t + kind
                                act.wait_ge(copied.sem, copied.at(n, u + 1))
                                act.wait_ge(added.sem, added.at(n, u - 3))
                                nc.scalar.activation(squares[:, u % 4, :], raw[:, t, kind, bass.ds(c * BANK, BANK)],
                                                     ACT.Square).then_inc(squared.sem, 1)
                            act.wait_ge(filled.sem, filled.at(n, 3 * t + 3))
                            copy("act", vals[:, t, bass.ds(c * BANK, BANK)], bank[:, (3 * t + 2) % SLOTS, :]).then_inc(v_copied.sem, 1)
                    act.wait_ge(guarded.sem, guarded.at(l, 1))
                    nc.scalar.activation(all_norms, all_norms, ACT.Sqrt).then_inc(rooted.sem, 1)

                @block.vector
                def _(dve):
                    for s in range(2):
                        scale = qk_scale[:, bass.ds(l * 2 + s, 1), :]
                        half = DH // 2
                        nc.vector.tensor_tensor(tables[:, :, s, 0, :], waves[:, :, s, 0, :], scale.to_broadcast([P, QT, DH]),
                                                ALU.mult).then_inc(tabled.sem, 1)
                        for h0, h1 in ((0, half), (half, 0)):
                            nc.vector.tensor_tensor(tables[:, :, s, 1, h0:h0 + half], waves[:, :, s, 1, h0:h0 + half],
                                                    scale[:, :, h1:h1 + half].to_broadcast([P, QT, half]),
                                                    ALU.mult).then_inc(tabled.sem, 1)
                    with dve.Fori(0, HALVES) as c:
                        n = l * HALVES + c
                        for u in range(2 * NT + LAG):
                            if u < 2 * NT:
                                t, kind = u // 2, u % 2
                                j = 3 * t + kind
                                dve.wait_ge(filled.sem, filled.at(n, j + 1))
                                copy("dve", raw[:, t, kind, bass.ds(c * BANK, BANK)], bank[:, j % SLOTS, :]).then_inc(copied.sem, 1)
                            v = u - LAG
                            if v >= 0:
                                dve.wait_ge(squared.sem, squared.at(n, v + 1))
                                nc.vector.tensor_reduce(norms[:, v // 2, v % 2, bass.ds(c * HB, HB)],
                                                        squares[:, v % 4, :].rearrange("p (h d) -> p h d", d=DH), AX.X,
                                                        ALU.add).then_inc(added.sem, 1)
                    dve.wait_ge(added.sem, added.at(l * HALVES + HALVES - 1, 2 * NT))
                    nc.vector.tensor_scalar(all_norms, all_norms, 1e-24, None, ALU.max).then_inc(guarded.sem, 1)
                    dve.wait_ge(rooted.sem, rooted.at(l, 1))
                    dve.wait_ge(loaded.sem, loaded.at(l, nloads))
                    nc.vector.reciprocal(all_norms, all_norms).then_inc(inverted.sem, 1)

        def local_attention(l, p, raw, vals, w_qkv, norms, tables, unit, turned_cos, turned_sin, q_slots, k_rows,
                            probs0, probs1, flat_p, maxima, sums, inverse, window16, qkv_in):
            UNIT, WAVES, ROTATE, TURN, STORE = 9, 8, 7, 4, 4
            total = DEPTH * PAIRS
            scaled = [signal(f"unit_{k}_done", NT, total) for k in "qk"]
            cosed = signal("cos_done", NT, total)
            sined = signal("sin_done", NT, total)
            rotated = signal("rotated", NT, total)
            qk_turned = signal("qk_turned", B, total)
            qk_moved = signal("qk_moved", B, total)
            scored = signal("tile_scored", NT, total)
            maxed = signal("tile_maxed", NT, total)
            exped = signal("tile_exped", NT, total)
            flipped = signal("tile_flipped", NT, total)
            moved = [signal(f"{nm}_tile_moved", NT // QT, total) for nm in ("first", "second")]
            inverted = signal("tile_inverted", NT, total)
            summed = signal("tile_summed", NT, total)
            stored = signal("tile_stored", NT, total)
            FIRST = -UNIT
            with ExitStack() as inner:
                scores = inner.enter_context(ps("scores", [P, 2, BANK]))
                flip = inner.enter_context(ps("flip", [P, 2, BANK]))
                weighted = inner.enter_context(ps("weighted", [P, 2, BANK]))
                turn = inner.enter_context(ps("turn", [P, 2, BANK]))
                block = inner.enter_context(nc.Block())

                def keys_of(g):
                    return P if g % QT == 0 else P + WINDOW

                def score_bank(g):
                    return scores[:, g % 2, 0:2 * keys_of(g)].rearrange("p (h k) -> p h k", h=2)

                def probs_of(g):
                    return (probs0, probs1)[g % QT][:, g // QT % 2, :, :]

                def pair_cols(i, g, width=D, at=0):
                    return bass.ds((i + g // NT) * D + at, width)

                def through(eng, step):
                    for s in range(FIRST, STORE):
                        step(s, l * PAIRS, 0, lambda g: g >= 0)
                    with eng.Fori(0, PAIRS - 2) as i:
                        for s in range(STORE, NT + STORE):
                            step(s, l * PAIRS + i, i, lambda g: True)
                    for s in range(STORE, 2 * NT + STORE):
                        step(s, l * PAIRS + (PAIRS - 2), PAIRS - 2, lambda g: g < 2 * NT)

                def by_head(v, g, slots=4):
                    return v[:, g % slots, :, :].rearrange("p s (h d) -> p s h d", h=2)

                def make_unit(engine, k, g, i):
                    heads = bass.ds((i + g // NT) * 2, 2)
                    return engine.tensor_tensor(
                        by_head(unit, g)[:, k, :, :], raw[:, g % NT, k, pair_cols(i, g)].rearrange("p (h d) -> p h d", h=2),
                        norms[:, g % NT, k, heads].rearrange("p (h o) -> p h o", o=1).to_broadcast([P, 2, DH]), ALU.mult)

                def move_turned(eng, e, n, g):
                    eng.wait_ge(flipped.sem, flipped.at(n, g + 1))
                    eng.wait_ge(summed.sem, summed.at(n, g - 3))
                    w = (1 + g % QT) * 2 * P
                    copy(e, flat_p[:, g % 4, 0:w], flip[:, g % 2, 0:w]).then_inc(moved[g % QT].sem, 1)

                @block.sync
                def _(sp):
                    sp.dma_start(w_qkv[:, :], p("Wqkv")[bass.ds(l + 1, 1), :, :].rearrange("o p c -> p (o c)")).then_inc(qkv_in.sem, 16)

                @block.gpsimd
                def _(pool):
                    def step(s, n, i, live):
                        g = s + ROTATE
                        if live(g):
                            pool.wait_ge(cosed.sem, cosed.at(n, g + 1))
                            pool.wait_ge(sined.sem, sined.at(n, g + 1))
                            both = lambda v, slot: v[:, slot, :, :].rearrange("p s d -> p (s d)")
                            qk = both(turned_cos, g % NT)
                            nc.gpsimd.tensor_tensor(qk, qk, both(turned_sin, g % 4), ALU.add).then_inc(rotated.sem, 1)
                        g = s + UNIT
                        if live(g):
                            make_unit(nc.gpsimd, 1, g, i).then_inc(scaled[1].sem, 1)
                        g = s + WAVES
                        if live(g):
                            for k in range(2):
                                pool.wait_ge(scaled[k].sem, scaled[k].at(n, g + 1))
                            pool.wait_ge(qk_turned.sem, qk_turned.at(n, (g - NT) // QT + 1))
                            nc.gpsimd.tensor_tensor(by_head(turned_cos, g, NT), by_head(unit, g),
                                                    tables[:, g % QT, :, 0:1, :].to_broadcast([P, 2, 2, DH]),
                                                    ALU.mult).then_inc(cosed.sem, 1)
                    through(pool, step)

                @block.tensor
                def _(pe):
                    def step(s, n, i, live):
                        g = s
                        if live(g):
                            t, nk = g % NT, keys_of(g)
                            pe.wait_ge(qk_moved.sem, qk_moved.at(n, g // QT + 1))
                            pe.wait_ge(exped.sem, exped.at(n, g - 1))
                            bank = score_bank(g)
                            mask = window16[:, (WINDOW + P) - nk:(WINDOW + P)].rearrange("p (o k) -> p o k", o=1).to_broadcast([P, 2, nk])
                            nc.tensor.matmul(bank, ident16[:, :], mask, start=True, stop=False)
                            k0 = (t + 1) * P - nk
                            for h in range(2):
                                last = nc.tensor.matmul(bank[:, h, :], q_slots[:, h, t * P:(t + 1) * P], k_rows[:, k0:k0 + nk],
                                                        start=False, stop=(h == 1))
                            last.then_inc(scored.sem, 1)
                        g = s - 2
                        if live(g):
                            pe.wait_ge(exped.sem, exped.at(n, g + 1))
                            pe.wait_ge(moved[g % QT].sem, moved[g % QT].at(n, g // QT))
                            blocks = 1 + g % QT
                            for h in range(2):
                                for j in range(blocks):
                                    last = nc.tensor.transpose(flip[:, g % 2, (h * blocks + j) * P:(h * blocks + j + 1) * P],
                                                               probs_of(g)[:, h, j * P:(j + 1) * P], ident[:, :])
                            last.then_inc(flipped.sem, 1)
                        g = s - STORE
                        if live(g):
                            t, blocks = g % NT, 1 + g % QT
                            pe.wait_ge(moved[g % QT].sem, moved[g % QT].at(n, g // QT + 1))
                            pe.wait_ge(stored.sem, stored.at(n, g - 1))
                            for h in range(2):
                                for j in range(blocks):
                                    last = nc.tensor.matmul(weighted[:, g % 2, h * DH:(h + 1) * DH],
                                                            flat_p[:, g % 4, (h * blocks + j) * P:(h * blocks + j + 1) * P],
                                                            vals[:, t + 1 - blocks + j, pair_cols(i, g, DH, h * DH)],
                                                            start=(j == 0), stop=(j == blocks - 1))
                            last.then_inc(summed.sem, 1)
                        g = s + TURN
                        if g % QT == 0 and live(g):
                            m = g // QT
                            pe.wait_ge(rotated.sem, rotated.at(n, g + 2))
                            pe.wait_ge(qk_moved.sem, qk_moved.at(n, m - 1))
                            for k in range(2):
                                for q in range(QT):
                                    last = nc.tensor.transpose(turn[:, m % 2, (k * QT + q) * P:(k * QT + q + 1) * P],
                                                               turned_cos[:, (g + q) % NT, k, :], ident[:, :])
                            last.then_inc(qk_turned.sem, 1)
                    through(pe, step)

                @block.scalar
                def _(act):
                    def step(s, n, i, live):
                        g = s
                        if live(g):
                            nk = keys_of(g)
                            act.wait_ge(maxed.sem, maxed.at(n, g + 1))
                            act.wait_ge(flipped.sem, flipped.at(n, g - 3))
                            for h in range(2):
                                pr = probs_of(g)[:, h, :]
                                c0 = (1 + g % QT) * P - nk
                                last = nc.scalar.activation(pr[:, c0:c0 + nk], score_bank(g)[:, h, :], ACT.Exp,
                                                            bias=maxima[:, g % NT, h:h + 1], accum_out=sums[:, g % NT, h:h + 1])
                            last.then_inc(exped.sem, 1)
                        g = s + TURN - 1
                        if g % QT == 0 and live(g):
                            m, t = g // QT, g % NT
                            act.wait_ge(qk_turned.sem, qk_turned.at(n, m + 1))
                            cols_ = slice(t * P, (t + QT) * P)
                            for h in range(2):
                                copy("act", q_slots[h * DH:(h + 1) * DH, h, cols_], turn[h * DH:(h + 1) * DH, m % 2, 0:QT * P])
                            copy("act", k_rows[:, cols_], turn[:, m % 2, QT * P:2 * QT * P]).then_inc(qk_moved.sem, 1)
                        g = s - 2
                        if g % QT == 0 and live(g):
                            move_turned(act, "act", n, g)
                    through(act, step)

                @block.vector
                def _(dve):
                    def step(s, n, i, live):
                        g = s
                        if live(g):
                            dve.wait_ge(scored.sem, scored.at(n, g + 1))
                            nc.vector.tensor_reduce(maxima[:, g % NT, :], score_bank(g), AX.X, ALU.max,
                                                    negate=True).then_inc(maxed.sem, 1)
                        g = s + UNIT
                        if live(g):
                            dve.wait_ge(cosed.sem, cosed.at(n, g - 3))
                            make_unit(nc.vector, 0, g, i).then_inc(scaled[0].sem, 1)
                        g = s + WAVES
                        if live(g):
                            for k in range(2):
                                dve.wait_ge(scaled[k].sem, scaled[k].at(n, g + 1))
                            dve.wait_ge(rotated.sem, rotated.at(n, g - 3))
                            half = DH // 2
                            for d, src in ((0, half), (half, 0)):
                                last = nc.vector.tensor_tensor(
                                    by_head(turned_sin, g)[:, :, :, d:d + half], by_head(unit, g)[:, :, :, src:src + half],
                                    tables[:, g % QT, :, 1:2, d:d + half].to_broadcast([P, 2, 2, half]), ALU.mult)
                            last.then_inc(sined.sem, 1)
                        g = s - 2
                        if live(g):
                            dve.wait_ge(exped.sem, exped.at(n, g + 1))
                            nc.vector.reciprocal(inverse[:, g % NT, :], sums[:, g % NT, :]).then_inc(inverted.sem, 1)
                            if g % QT == 1:
                                move_turned(dve, "dve", n, g)
                        g = s - STORE
                        if live(g):
                            dve.wait_ge(inverted.sem, inverted.at(n, g + 1))
                            dve.wait_ge(summed.sem, summed.at(n, g + 1))
                            nc.vector.tensor_tensor(
                                raw[:, g % NT, 0, pair_cols(i, g)].rearrange("p (h d) -> p h d", h=2),
                                weighted[:, g % 2, 0:D].rearrange("p (h d) -> p h d", h=2),
                                inverse[:, g % NT, :].rearrange("p (h o) -> p h o", o=1).to_broadcast([P, 2, DH]),
                                ALU.mult).then_inc(stored.sem, 1)
                    through(dve, step)

        def store():
            sent = signal("stored_out", 1, step=16)
            with nc.Block() as block:
                @block.sync
                def _(sp):
                    sp.dma_start(out.rearrange("b (t p) d -> p (b t) d", p=P), x[:, :, :]).then_inc(sent.sem, 16)
                    sp.wait_ge(sent.sem, sent.at(0, 1))

        stages = dict(l0_attn=l0_attn, l0_xattn=l0_xattn, l0_ffn=l0_ffn, l1_attn=l1_attn, l1_xattn=l1_xattn, l1_ffn=l1_ffn,
                      l2_attn=l2_attn, l2_xattn=l2_xattn, l2_ffn=l2_ffn, l3_attn=l3_attn, l3_xattn=l3_xattn, l3_ffn=l3_ffn)
        setup()
        for name in STAGES:
            if name == "l3_ffn":
                early.close()
            stages[name]()
        store()


STAGES = ("l0_attn", "l0_xattn", "l0_ffn", "l1_attn", "l1_xattn", "l1_ffn", "l2_attn", "l2_xattn", "l2_ffn", "l3_attn",
          "l3_xattn", "l3_ffn")


AHEAD = (
    "bank_filled", "bank_emptied_act", "bank_emptied_dve", "measured", "gathered", "eps_added", "rooted",
    "inverted", "normed", "norm_turned", "norm_moved_act", "norm_moved_dve", "masked_q", "scores_ready",
    "max_ready", "probs_ready", "ipa_rescaled", "probs_turned", "turned_moved_act", "turned_moved_dve",
    "values_ready", "rowinv_ready", "head_stored", "consts_made", "ipa_made", "rope_done", "added_all",
    "gate_step", "gate_exp", "expert_up", "expert_silu", "expert_gated", "expert_down",
    "expert_added", "mixed", "squared", "mask_made", "qk_rooted", "fp4_cleared", "fp4_step",
    "heads_cleared", "window_made", "squares_guarded", "norms_rooted", "norms_inverted", "tables_made",
    "heads_bank_filled", "heads_bank_emptied_act", "heads_bank_emptied_dve", "late_shifted", "late_moved",
    "glu_bank_filled", "glu_bank_emptied_act", "glu_bank_emptied_dve", "shift_cleared", "shift_turned",
    "shift_lower", "shift_upper",
)

STEPS_AHEAD = 16
AHEAD_BY_STEPS = (
    "qkv_filled", "qk_copied", "v_copied", "qk_squared", "squares_added", "unit_q_done", "unit_k_done", "cos_done", "sin_done",
    "rotated", "qk_turned", "qk_moved", "tile_scored", "tile_maxed", "tile_exped", "tile_flipped", "first_tile_moved", "second_tile_moved",
    "tile_inverted", "tile_summed", "tile_stored",
)


def constants():
    f = np.float32
    i, j = np.arange(P)[:, None], np.arange(P)[None, :]
    keep = np.stack([j <= i, j >= i], 1)
    reach = np.arange(WINDOW + P)[None, :] - WINDOW
    keep_window = (reach <= i) & (reach >= i - WINDOW)

    def rotation(width):
        r, half = np.zeros((P, P), f), width // 2
        for d in range(P):
            if d % width < half:
                r[d + half, d] = -1.0
            else:
                r[d - half, d] = 1.0
        return r

    def angles(width):
        inv = (f(1.0) / f(10000.0) ** (np.arange(0, width, 2, dtype=f) / f(width))).astype(f)
        ang = np.arange(N, dtype=f)[:, None] * inv[None, :]
        return np.concatenate([ang, ang], 1).astype(f)

    a8, a64 = angles(HS), angles(DH)
    half = np.arange(0, DH, 2, dtype=f)
    base = ((half + f(0.4 * DH)) / f(1.4 * DH)).astype(f)
    power = ((np.arange(N, dtype=f) - f(N // 2)) / f(WINDOW // 2)).astype(f)
    scale = (base[None, :] ** power[:, None]).astype(f)
    scale = np.concatenate([scale, scale], 1)
    tile = lambda t: np.ascontiguousarray(np.tile(t.T, (P // t.shape[1], 1))).astype(f)
    sign = np.where(np.arange(DH) < DH // 2, f(-1), f(1))
    waves = np.stack([np.stack([np.cos(a64) * c, np.sin(a64) * c * sign], 1) for c in (scale * f(QK_SCALE), f(1.0) / scale)], 1)
    waves = waves.astype(f).reshape(QT, P, 2 * 2 * DH).transpose(1, 0, 2)
    return {
        "c_ident": np.eye(P, dtype=f),
        "c_masks": np.where(keep, f(0), f(NEG)).astype(f),
        "c_late": np.stack([np.eye(P, k=1, dtype=f), np.eye(P, k=1 - P, dtype=f)], 1),
        "c_window": np.where(keep_window, f(0), f(NEG)).astype(f),
        "c_head_mask": (np.arange(P)[:, None] // HS == np.arange(H)[None, :]).astype(f),
        "c_rot8": rotation(HS),
        "c_block64": (i // DH == j // DH).astype(f),
        "c_cos8": tile(np.cos(a8)), "c_sin8": tile(np.sin(a8)),
        "c_waves": np.ascontiguousarray(waves),
    }


def laid_out(inp):
    g = {k: np.asarray(v) for k, v in inp.items()}
    t = lambda m: np.ascontiguousarray(m.T)
    o = dict(g)
    for nm in "qkvo":
        o[f"L0_xattn_{nm}_downT"] = t(o.pop(f"L0_xattn_{nm}_down"))
    wqkv = o.pop("L0_ffn_wqkv")
    kv = lambda r: t(np.repeat(wqkv[r:r + 32].reshape(4, 1, HS, D), 4, axis=1).reshape(D, D))
    o["L0_ffn_wqT"], o["L0_ffn_wkT"], o["L0_ffn_wvT"] = t(wqkv[0:D]), kv(D), kv(D + 32)
    o["L0_ffn_woT"], o["L0_ffn_gate_wT"] = t(o.pop("L0_ffn_wo")), t(o.pop("L0_ffn_gate_w"))
    o["L0_ffn_w13T"] = np.ascontiguousarray(o.pop("L0_ffn_w13").transpose(2, 0, 1).reshape(D, EXPERTS * 2 * FFN))
    w2 = o.pop("L0_ffn_w2")
    o["L0_ffn_w2T"] = np.ascontiguousarray(w2.transpose(2, 0, 1).reshape(2, P, EXPERTS, D).transpose(1, 2, 0, 3).reshape(P, EXPERTS * 2 * D))
    for nm in "rkv":
        o[f"L1_ffn_W_{nm}T"] = t(o.pop(f"L1_ffn_W_{nm}"))
    for nm in "QKV":
        o[f"L2_attn_{nm}T"] = t(o.pop(f"L2_attn_{nm}").reshape(H * DH, D))
    o["L2_attn_OT"] = t(o.pop("L2_attn_O"))
    wkv, wlkv = o.pop("L2_xattn_Wkv"), o.pop("L2_xattn_Wlkv")
    o["L2_xattn_WkT"], o["L2_xattn_WvT"] = t(wkv[0:D]), t(wkv[D:])
    o["L2_xattn_WlkT"], o["L2_xattn_WlvT"] = t(wlkv[0:D]), t(wlkv[D:])
    o["L2_xattn_WqT"], o["L2_xattn_WoT"] = t(o.pop("L2_xattn_Wq")), t(o.pop("L2_xattn_Wo"))
    wkv = o.pop("L3_xattn_w_kv")
    o["L3_xattn_w_k"], o["L3_xattn_w_v"] = wkv[:, 0:H * DH], wkv[:, H * DH:]
    b1 = o.pop("L3_ffn_b1")
    b1c = np.zeros((DEPTH, P, 6), b1.dtype)
    for h in range(2):
        for j in range(3):
            n = min(P, GLU - j * P)
            b1c[:, 0:n, 3 * h + j] = b1[:, h * GLU + j * P:h * GLU + j * P + n]
    o["L3_ffn_b1c"] = b1c
    o["L3_ffn_Wqkv"] = np.concatenate([o["L3_ffn_Wqkv"], o["L3_ffn_Wqkv"][0:1]])
    o["L3_ffn_qk_scale"] = np.stack([o.pop("L3_ffn_q_scale"), o.pop("L3_ffn_k_scale")], 1).reshape(1, DEPTH * 2 * DH)
    o["mask_BxS2_bk0"] = o["mask_BxS2_bk0"].reshape(1, B * M)
    return o


def kernel(**inputs):
    import concourse.bacc as bacc
    from concourse.bass_utils import run_bass_kernel_spmd

    nc = bacc.Bacc("TRN2", target_bir_lowering=False, num_devices=1)
    arrays, args = {}, {}
    for name, v in {**laid_out(inputs), **constants()}.items():
        v = np.ascontiguousarray(v)
        arrays[f"in_{name}"] = v
        args[name] = nc.dram_tensor(f"in_{name}", v.shape, mybir.dt.from_np(v.dtype), kind="ExternalInput").ap()
    y = nc.dram_tensor("out_0", (B, N, D), F32, kind="ExternalOutput").ap()
    decoder(nc, args, y)
    r = run_bass_kernel_spmd(nc, [arrays], core_ids=[0])
    return r.results[0]["out_0"]
```

```python
from contextlib import ExitStack

import numpy as np
import concourse.bass as bass
from concourse import mybir

F32 = mybir.dt.float32
BF16 = mybir.dt.bfloat16
U8 = mybir.dt.uint8
ALU = mybir.AluOpType
ACT = mybir.ActivationFunctionType
AX = mybir.AxisListType

P = 128
B, N, D = 4, 256, 128
T = B * N
NT = T // P
QT = N // P
M, C = 512, 96
MT = B * M // P
KT = M // P
BANK = 512
H, DH = 16, 64
HS = D // H
PAIRS = H // 2
U_PAIR = 2 * NT
ENG = ("act", "dve")
RANK = 32
WARM = 20
IPA = 4
EXPERTS, FFN = 8, 256
FP4_FFN, FP4_BLOCK = 352, 16
DEPTH, GLU, WINDOW, QK_SCALE = 6, int(D * 4 * 2 / 3), 32, 8.0
NEG = -1.0e30
LN_EPS = 1e-5


class Count:

    def __init__(self, sem, base, per, step):
        self.sem, self.base, self.per, self.step = sem, base, per, step

    def at(self, i, k):
        return i * (self.per * self.step) + (self.base + k * self.step)


class Signals:

    def __init__(self, nc, ctx, ahead):
        self.nc, self.ctx, self.sems, self.base = nc, ctx, {}, {}
        engines = (nc.sync, nc.scalar, nc.vector, nc.gpsimd, nc.tensor)
        for j, (name, n) in enumerate(ahead):
            self(name, n)
            engines[j % len(engines)].sem_inc(self.sems[name], n)
        nc.all_engine_barrier()

    def __call__(self, name, per, iters=1, step=1):
        if name not in self.sems:
            self.sems[name] = self.ctx.enter_context(self.nc.semaphore(name))
            self.base[name] = 0
        out = Count(self.sems[name], self.base[name], per, step)
        self.base[name] += per * iters * step
        return out


class Chunk:

    def __init__(self, engine, mm, out, after=(), stored=0):
        self.engine, self.mm, self.out, self.after, self.stored = engine, mm, out, after, stored


def emptied_before(chunks, j, banks):
    need = {}
    for d in ([j - banks] if j >= banks else []) + list(chunks[j].after):
        e = chunks[d].engine
        need[e] = max(need.get(e, 0), sum(c.engine == e for c in chunks[:d + 1]))
    return sorted(need.items())


class Unit:

    def __init__(self, nk, scores, values, store, width, base=None):
        self.nk, self.scores, self.values, self.store, self.width = nk, scores, values, store, width


def decoder(nc, a, out):
    ctx = ExitStack()
    with ctx:
        signal = Signals(nc, ctx, [(name, 1) for name in AHEAD] + [(name, STEPS_AHEAD) for name in AHEAD_BY_STEPS])

        def sb(name, shape, dt=F32):
            return ctx.enter_context(nc.sbuf_tensor(name, shape, dt))

        def ps(name, shape):
            psum_names[0] += 1
            return nc.psum_tensor(f"{name}_{psum_names[0]}", shape, F32)
        psum_names = [0]

        def copy(engine, dst, src, scale=1.0):
            if engine == "act":
                return nc.scalar.activation(dst, src, ACT.Copy, scale=scale)
            if isinstance(scale, float) and scale == 1.0:
                return nc.vector.tensor_copy(dst, src)
            return nc.vector.tensor_scalar(dst, src, scale, None, ALU.mult)

        def affine(engine, dst, src, scale, bias):
            if engine == "act":
                return nc.scalar.activation(dst, src, ACT.Identity, bias=bias, scale=scale)
            return nc.vector.tensor_scalar(dst, src, scale, bias, ALU.mult, ALU.add)

        x = sb("x", [P, NT, D])
        xin = sb("xin", [P, NT, D])
        z = sb("z", [P, NT, D])
        xnT = sb("xnT", [P, T])
        stats = sb("stats", [P, MT, 6])
        meanvar = sb("meanvar", [P, MT, 2])
        spread = sb("spread", [P, MT])
        rstd = sb("rstd", [P, MT])
        ident = sb("ident", [P, P])
        ident16 = sb("ident16", [P, P], BF16)
        masks = sb("masks", [P, 2, P])
        masks16 = sb("masks16", [P, 2, P], BF16)
        ones = sb("ones", [P, P])
        ones16 = sb("ones16", [P, P], BF16)
        head_mask = sb("head_mask", [P, H])
        pair_mask = sb("pair_mask", [P, 2, 2])
        rot8 = sb("rot8", [P, P])
        cols = sb("cols", [P, 32])
        brow = sb("brow", [1, 512])
        early = ctx.enter_context(ExitStack())

        def sbe(name, shape):
            return early.enter_context(nc.sbuf_tensor(name, shape, F32))

        ctx_tok = sbe("ctx_tok", [P, MT, C])
        ctxT = sbe("ctxT", [P, B * M])
        qT = sbe("qT", [P, 2, T])
        qM = sbe("qM", [P, 2, T])
        kT = sbe("kT", [P, B * (M + N)])
        V = sbe("V", [P, MT + NT, D])
        probs = sbe("probs", [P, 3, M + N])
        turned = sbe("turned", [P, 4, BANK])
        negmax = sbe("negmax", [P, 32])
        rowsum = sbe("rowsum", [P, 32])
        rowinv = sbe("rowinv", [P, 32])
        heads_out = sbe("heads_out", [P, NT, D])
        outT = sbe("outT", [P, T])
        wq = sbe("wq", [P, D])
        wk = sbe("wk", [P, D])
        wv = sbe("wv", [P, D])
        wo = sbe("wo", [P, D])

        def columns(c0, c1=None):
            return cols[:, c0:(c0 + 1 if c1 is None else c1)]

        def load(pairs):
            arrived = signal("small_loads", len(pairs), step=16)
            with nc.Block() as block:
                @block.sync
                def _(sp):
                    for dst, src in pairs:
                        sp.dma_start(dst, src).then_inc(arrived.sem, 16)
                    sp.wait_ge(arrived.sem, arrived.at(0, len(pairs)))

        def col_of(vec):
            return vec.rearrange("(d o) -> d o", o=1)

        def row_of(vec):
            return vec.rearrange("(o d) -> o d", o=1)

        def chunk_block(chunks, n=0, iters=1, tag=""):
            filled = signal(tag + "bank_filled", len(chunks), iters)
            count = {e: sum(c.engine == e for c in chunks) for e in ("act", "dve")}
            emptied = {e: signal(f"{tag}bank_emptied_{e}", count[e], iters) for e in ("act", "dve")}
            slots = 4
            with ps("bank", [P, slots, BANK]) as bank, nc.Block() as block:
                @block.tensor
                def _(pe):
                    for j, c in enumerate(chunks):
                        for e, k in emptied_before(chunks, j, slots):
                            pe.wait_ge(emptied[e].sem, emptied[e].at(n, k))
                        c.mm(bank[:, j % slots, :]).then_inc(filled.sem, 1)

                def empty(eng, e):
                    for j, c in enumerate(chunks):
                        if c.engine == e:
                            eng.wait_ge(filled.sem, filled.at(n, j + 1))
                            c.out(bank[:, j % slots, :]).then_inc(emptied[e].sem, 1)

                @block.scalar
                def _(act):
                    empty(act, "act")

                @block.vector
                def _(dve):
                    empty(dve, "dve")

        def keep_warm(bank):
            for _ in range(WARM):
                nc.tensor.matmul(bank, ident16[:, :], ident16[:, :].rearrange("p (o k) -> p o k", o=1).to_broadcast([P, 4, P]),
                                 start=True, stop=True)

        def norm(src, tiles, width, dst, dstT=None, rms=False, gain=None, bias=None, eps=LN_EPS, n=0, iters=1, loads=(),
                 clear=False):
            arrived = signal("loads_in", len(loads), step=16)
            cleared = signal("heads_cleared", 1 if clear else 0)
            measured = signal("measured", tiles, iters)
            gathered = signal("gathered", tiles, iters)
            eps_added = signal("eps_added", 2, iters)
            rooted = signal("rooted", 1, iters)
            inverted = signal("inverted", 1, iters)
            normed = signal("normed", tiles, iters)
            nbank = (tiles + 3) // 4 if dstT is not None else 0
            turned_in = signal("norm_turned", nbank, iters)
            moved_act = signal("norm_moved_act", (nbank + 1) // 2, iters)
            moved_dve = signal("norm_moved_dve", nbank // 2, iters)
            with ps("bank", [P, 4, BANK]) as bank, nc.Block() as block:
                def move(e, j):
                    s, d = bank[0:width, j % 4, :], dstT[0:width, j * BANK:(j + 1) * BANK]
                    if bias is not None:
                        return affine(e, d, s, gain[0:width], bias[0:width])
                    return copy(e, d, s, 1.0 if gain is None else gain[0:width])

                if loads:
                    @block.sync
                    def _(sp):
                        for d, source in loads:
                            sp.dma_start(d, source).then_inc(arrived.sem, 16)
                        sp.wait_ge(arrived.sem, arrived.at(0, len(loads)))

                if clear:
                    @block.gpsimd
                    def _(pool):
                        nc.gpsimd.memset(qM[:, :, :], 0.0).then_inc(cleared.sem, 1)

                @block.vector
                def _(dve):
                    for t in range(tiles):
                        nc.vector.bn_stats(stats[:, t, :], src[:, t, 0:width]).then_inc(measured.sem, 1)
                    if iters > 1:
                        dve.wait_ge(measured.sem, measured.at(n, tiles))
                        nc.vector.memset(spread[:, 0:tiles], 0.0)
                    for t in range(tiles):
                        if iters == 1:
                            dve.wait_ge(measured.sem, measured.at(n, t + 1))
                        nc.vector.bn_aggr(meanvar[:, t, :], stats[:, t, :]).then_inc(gathered.sem, 1)
                    dve.wait_ge(gathered.sem, gathered.at(n, tiles))
                    if rms:
                        nc.vector.tensor_tensor(spread[:, 0:tiles], meanvar[:, 0:tiles, 0], meanvar[:, 0:tiles, 0],
                                                ALU.mult).then_inc(eps_added.sem, 1)
                        dve.wait_ge(eps_added.sem, eps_added.at(n, 1))
                        nc.vector.scalar_tensor_tensor(spread[:, 0:tiles], meanvar[:, 0:tiles, 1], eps,
                                                       spread[:, 0:tiles], ALU.add, ALU.add).then_inc(eps_added.sem, 1)
                    else:
                        nc.vector.tensor_scalar(spread[:, 0:tiles], meanvar[:, 0:tiles, 1], eps, None,
                                                ALU.add).then_inc(eps_added.sem, 2)
                    dve.wait_ge(rooted.sem, rooted.at(n, 1))
                    nc.vector.reciprocal(rstd[:, 0:tiles], spread[:, 0:tiles]).then_inc(inverted.sem, 1)
                    dve.wait_ge(inverted.sem, inverted.at(n, 1))
                    for t in range(tiles):
                        if rms:
                            last = nc.vector.tensor_scalar(dst[:, t, 0:width], src[:, t, 0:width], rstd[:, t:t + 1],
                                                           None, ALU.mult)
                        else:
                            last = nc.vector.tensor_scalar(dst[:, t, 0:width], src[:, t, 0:width],
                                                           meanvar[:, t, 0:1], rstd[:, t:t + 1],
                                                           ALU.subtract, ALU.mult)
                        last.then_inc(normed.sem, 1)
                    for j in range(1, nbank, 2):
                        dve.wait_ge(turned_in.sem, turned_in.at(n, j + 1))
                        move("dve", j).then_inc(moved_dve.sem, 1)

                @block.scalar
                def _(act):
                    act.wait_ge(eps_added.sem, eps_added.at(n, 2))
                    nc.scalar.activation(spread[:, 0:tiles], spread[:, 0:tiles], ACT.Sqrt).then_inc(rooted.sem, 1)
                    for j in range(0, nbank, 2):
                        act.wait_ge(turned_in.sem, turned_in.at(n, j + 1))
                        move("act", j).then_inc(moved_act.sem, 1)

                @block.tensor
                def _(pe):
                    if nbank:
                        keep_warm(bank[:, 3, :])
                    for j in range(nbank):
                        pe.wait_ge(normed.sem, normed.at(n, 4 * j + 4))
                        for q in range(4):
                            last = nc.tensor.transpose(bank[0:width, j % 4, q * P:(q + 1) * P],
                                                       dst[:, 4 * j + q, 0:width], ident[:, :])
                        last.then_inc(turned_in.sem, 1)

        def attention(units, head=(), wide=1):
            U, banks, lag_v = len(units), 2, 3
            turns = [[(g, min(g + 4, u.nk // P)) for g in range(0, u.nk // P, 4)] if wide == 1 else
                     [(0, 3), (3, 6)] for u in units]
            G = len(turns[0])
            slots = {1: 4, 2: 2}[wide]
            ow = units[0].width

            filled = signal("bank_filled", len(head))
            count = {e: sum(c.engine == e for c in head) for e in ENG}
            emptied = {e: signal(f"bank_emptied_{e}", count[e]) for e in ENG}
            scored = signal("scores_ready", U)
            maxed = signal("max_ready", U)
            exped = signal("probs_ready", U)
            flipped = signal("probs_turned", U * G)
            moved = [signal(f"turned_moved_{e}", U * G // 2) for e in ENG]
            summed = signal("values_ready", U)
            inverse = signal("rowinv_ready", U)
            stored = signal("head_stored", U)

            with ExitStack() as inner:
                proj = inner.enter_context(ps("proj", [P, banks, BANK]))
                scores = inner.enter_context(ps("scores", [P, slots, wide * BANK]))
                flip = inner.enter_context(ps("flip", [P, 2, BANK]))
                block = inner.enter_context(nc.Block())

                def weighted(u):
                    return proj[:, u % banks, 0:ow]

                @block.tensor
                def _(pe):
                    for j, c in enumerate(head):
                        for e, k in emptied_before(head, j, banks):
                            pe.wait_ge(emptied[e].sem, emptied[e].at(0, k))
                        c.mm(proj[:, j % banks, :]).then_inc(filled.sem, 1)
                    for e in ENG:
                        pe.wait_ge(emptied[e].sem, emptied[e].at(0, count[e]))
                    for s in range(U + lag_v):
                        if s < U:
                            pe.wait_ge(exped.sem, exped.at(0, max(0, s - slots + 1)))
                            units[s].scores(scores[:, s % slots, :]).then_inc(scored.sem, 1)
                        t = s - 2
                        if 0 <= t < U:
                            pe.wait_ge(exped.sem, exped.at(0, t + 1))
                            for g, (b0, b1) in enumerate(turns[t]):
                                q = t * G + g
                                pe.wait_ge(moved[q % 2].sem, moved[q % 2].at(0, q // 2))
                                for j in range(b0, b1):
                                    last = nc.tensor.transpose(flip[:, q % 2, (j - b0) * P:(j - b0 + 1) * P],
                                                               probs[:, t % 3, j * P:(j + 1) * P], ident[:, :])
                                last.then_inc(flipped.sem, 1)
                        t = s - lag_v
                        if 0 <= t < U:
                            pe.wait_ge(stored.sem, stored.at(0, max(0, t - banks + 1)))
                            for g, (b0, b1) in enumerate(turns[t]):
                                q = t * G + g
                                pe.wait_ge(moved[q % 2].sem, moved[q % 2].at(0, q // 2 + 1))
                                for j in range(b0, b1):
                                    last = nc.tensor.matmul(weighted(t), turned[:, q % 4, (j - b0) * P:(j - b0 + 1) * P],
                                                            units[t].values(j, 0), start=(j == 0),
                                                            stop=(j == units[t].nk // P - 1))
                            last.then_inc(summed.sem, 1)

                def empty(eng, e):
                    for j, c in enumerate(head):
                        if c.engine == e:
                            eng.wait_ge(filled.sem, filled.at(0, j + 1))
                            c.out(proj[:, j % banks, :]).then_inc(emptied[e].sem, 1)

                def move_turned(eng, k, t):
                    for g, (b0, b1) in enumerate(turns[t]):
                        q = t * G + g
                        if q % 2 == k:
                            w = (b1 - b0) * P
                            eng.wait_ge(flipped.sem, flipped.at(0, q + 1))
                            eng.wait_ge(summed.sem, summed.at(0, (q - 4) // G + 1 if q >= 4 else 0))
                            copy(ENG[k], turned[:, q % 4, 0:w], flip[:, q % 2, 0:w]).then_inc(moved[k].sem, 1)

                @block.scalar
                def _(act):
                    empty(act, "act")
                    for s in range(U + 2):
                        if s < U:
                            nk = units[s].nk
                            act.wait_ge(maxed.sem, maxed.at(0, s + 1))
                            act.wait_ge(flipped.sem, flipped.at(0, max(0, s - 2) * G))
                            nc.scalar.activation(probs[:, s % 3, 0:nk], scores[:, s % slots, 0:nk], ACT.Exp,
                                                 bias=negmax[:, s:s + 1], accum_out=rowsum[:, s:s + 1]).then_inc(exped.sem, 1)
                        if 0 <= s - 2 < U:
                            move_turned(act, 0, s - 2)

                @block.vector
                def _(dve):
                    empty(dve, "dve")
                    for s in range(U + lag_v):
                        if s < U:
                            nk = units[s].nk
                            dve.wait_ge(scored.sem, scored.at(0, s + 1))
                            nc.vector.tensor_reduce(negmax[:, s:s + 1], scores[:, s % slots, 0:nk], AX.X, ALU.max,
                                                    negate=True).then_inc(maxed.sem, 1)
                        t = s - 2
                        if 0 <= t < U:
                            dve.wait_ge(exped.sem, exped.at(0, t + 1))
                            nc.vector.reciprocal(rowinv[:, t:t + 1], rowsum[:, t:t + 1]).then_inc(inverse.sem, 1)
                            move_turned(dve, 1, t)
                        t = s - lag_v
                        if 0 <= t < U:
                            dve.wait_ge(inverse.sem, inverse.at(0, t + 1))
                            dve.wait_ge(summed.sem, summed.at(0, t + 1))
                            units[t].store(weighted(t), rowinv[:, t:t + 1], 0).then_inc(stored.sem, 1)

        HALF = BANK

        def mm_T(w, srcT, c0, k=P, m=P, cols_n=HALF):
            return lambda o: nc.tensor.matmul(o[0:m, 0:cols_n], w, srcT[0:k, c0:c0 + cols_n], start=True, stop=True)

        def mm_tok(srcT, w, t0, k=P, m=D, bias=None, tiles=4):
            def f(o):
                for q in range(tiles):
                    last = nc.tensor.matmul(o[:, q * m:(q + 1) * m], srcT[0:k, (t0 + q) * P:(t0 + q + 1) * P], w,
                                            start=True, stop=bias is None)
                    if bias is not None:
                        last = nc.tensor.matmul(o[:, q * m:(q + 1) * m], ones[0:1, :], bias, start=False, stop=True)
                return last
            return f

        def tiles_of(o, m=D, n=4):
            return o[:, 0:n * m].rearrange("p (t d) -> p t d", t=n)

        def turn_chunk(engine, src, t0, dstT):
            def f(o):
                for q in range(4):
                    last = nc.tensor.transpose(o[:, q * P:(q + 1) * P], src[:, t0 + q, :], ident[:, :])
                return last
            return Chunk(engine, f, lambda o: copy(engine, dstT[:, t0 * P:(t0 + 4) * P], o))

        def ahead_of(firsts, seconds, lead=2):
            order = []
            for k in range(len(firsts) + lead):
                if k < len(firsts):
                    order.append(firsts[k])
                if k >= lead:
                    seconds[k - lead].after = (order.index(firsts[k - lead]),)
                    order.append(seconds[k - lead])
            return order

        def add_to(acc, t0):
            return lambda o: nc.vector.tensor_tensor(acc[:, t0:t0 + 4, :], acc[:, t0:t0 + 4, :], tiles_of(o), ALU.add)

        def out_chunks(first, acc, w, bias=None):
            return [turn_chunk("act", heads_out, 0, outT), turn_chunk("dve", heads_out, 4, outT),
                    Chunk("dve", mm_tok(outT, w, 0, bias=bias), add_to(acc, 0), after=(first,)),
                    Chunk("dve", mm_tok(outT, w, 4, bias=bias), add_to(acc, 4), after=(first + 1,))]

        def self_chunks(qs=1.0, srcT=xnT, first=0, vbias=None, qbias=None, kbias=None, m=D, mv=D):
            out_list = []
            for w, dst, s, bcol in ((wq, qT[:, 0, :], qs, qbias), (wk, kT, 1.0, kbias)):
                for c in range(T // HALF):
                    e = ENG[c % 2]
                    d = dst[0:m, c * HALF:(c + 1) * HALF]
                    if bcol is None:
                        f = lambda o, e=e, d=d, s=s: copy(e, d, o[0:m, :], s)
                    else:
                        f = lambda o, d=d, s=s, bcol=bcol: nc.vector.tensor_scalar(d, o[0:m, :], bcol, s, ALU.add, ALU.mult)
                        e = "dve"
                    out_list.append(Chunk(e, mm_T(w[:, 0:m], srcT, c * HALF, m=m), f))
            for t in range(0, NT, 4):
                e = ENG[t // 4 % 2]
                out_list.append(Chunk(e, mm_tok(srcT, wv[:, 0:mv], t, bias=vbias),
                                      lambda o, e=e, t=t: copy(e, V[:, t:t + 4, :], tiles_of(o))))
            return out_list

        def score_mm(segments):
            def f(o):
                for c0, w, q, k, mk in segments:
                    last = nc.tensor.matmul(o[:, c0:c0 + w], q, k, start=True, stop=not mk)
                    for j, (ml, mr, m0, mw) in enumerate(mk):
                        last = nc.tensor.matmul(o[:, m0:m0 + mw], ml, mr, start=False, stop=(j == len(mk) - 1))
                return last
            return f

        CAUSAL, NOT_BEFORE = range(2)

        def block_mask(kind, c0):
            return (ident16[:, :], masks16[:, kind, :], c0, P)

        def self_units(q_of, k_of, v_of, store_of, kind, heads, width):
            us = []
            for h in range(heads):
                for b in range(B):
                    for qt in range(QT):
                        t = b * QT + qt
                        nk, mk = N, []
                        if kind == "causal":
                            nk, mk = (qt + 1) * P, [block_mask(CAUSAL, qt * P)]
                        elif kind == "near":
                            mk = [block_mask(CAUSAL, P)] if qt == 0 else [block_mask(NOT_BEFORE, 0)]
                        us.append(Unit(nk, score_mm([(0, nk, q_of(h, t), k_of(h, b * N, nk), mk)]),
                                       lambda j, i, h=h, b=b: v_of(h, b * QT + j, i), store_of(h, t), width))
            return us

        def pair_rows(h):
            return slice(h * DH, (h + 1) * DH)

        def put_heads(engine, o, c, scale=1.0):
            for h in range(2):
                last = copy(engine, qM[pair_rows(h), h, c * HALF:(c + 1) * HALF], o[pair_rows(h), :], scale)
            return last


        def pair_store(h, t):
            return lambda o, r, i: nc.vector.tensor_scalar(heads_out[:, t, pair_rows(h)], o, r, None, ALU.mult)

        slot_q = lambda h, t: qM[:, h, t * P:(t + 1) * P]
        all_k = lambda h, k0, w: kT[:, k0:k0 + w]
        def add_store(h, t):
            return lambda o, r, i: nc.vector.scalar_tensor_tensor(x[:, t, :], o, r, x[:, t, :], ALU.mult, ALU.add)

        def streamed(units, ins=(), outs=(), where=None, slots=None, masks=False, ipa=False):
            U, STORE, FIRST, START = len(units), 4, -9, 7
            G = 2 if ins else 4
            pr = probs[:, :, :].rearrange("p s k -> p (s k)")[:, 0:4 * BANK].rearrange("p (s k) -> p s k", s=4)
            span = U // sum(name[0] == "k" for name in where) if ins else None
            in_chunks, out_chunks_ = [c for _, c in ins], [c for _, c in outs]
            per = lambda cs, e: sum(c.engine == e for c in cs)
            scored = signal("unit_scored", U, PAIRS)
            maxed = signal("unit_maxed", U, PAIRS)
            exped = signal("unit_exped", U, PAIRS)
            rescaled = signal("unit_rescaled", 2 * U if ipa else 0, PAIRS)
            flipped = signal("unit_flipped", U, PAIRS)
            moved = [signal(f"unit_moved_{e}", U // 2, PAIRS) for e in ENG]
            inverted = signal("unit_inverted", U, PAIRS)
            summed = signal("unit_summed", U, PAIRS)
            stored = signal("unit_stored", U, PAIRS)
            in_filled = signal("in_filled", len(ins), PAIRS)
            in_emptied = {e: signal(f"in_emptied_{e}", per(in_chunks, e), PAIRS) for e in ENG}
            out_filled = signal("out_filled", len(outs), PAIRS)
            out_emptied = {e: signal(f"out_emptied_{e}", per(out_chunks_, e), PAIRS) for e in ENG}
            slots_in = signal("slots_copied", 1 if slots else 0, PAIRS)
            mask_there = signal("pair_mask_there", 2 if masks else 0, PAIRS)
            masked = signal("halves_masked", 2 if masks else 0, PAIRS)

            def emptied_to(cs, j, e):
                return sum(c.engine == e for c in cs[:j + 1])

            def through(eng, step):
                for s in range(FIRST, START):
                    step(s, 0, lambda pair: pair >= 0)
                with eng.Fori(0, PAIRS - 1) as i:
                    for s in range(START, START + U):
                        step(s, i, lambda pair: True)
                for s in range(START, START + U):
                    step(s, PAIRS - 1, lambda pair: pair < 1)

            def at_step(s, offset, live):
                pair, rest = divmod(s - offset, U)
                return pair if rest == 0 and live(pair) else None

            def unit_at(s, lag, live):
                pair, u = divmod(s - lag, U)
                return (pair, u) if live(pair) else (None, None)

            with ExitStack() as inner:
                scores = inner.enter_context(ps("scores", [P, G, BANK]))
                flip = inner.enter_context(ps("flip", [P, 2, BANK]))
                weighted = inner.enter_context(ps("weighted", [P, 2, BANK]))
                proj = inner.enter_context(ps("proj", [P, 2, BANK])) if ins else None
                block = inner.enter_context(nc.Block())

                def move_turned(eng, k, n, u):
                    nk = units[u].nk
                    eng.wait_ge(flipped.sem, flipped.at(n, u + 1))
                    eng.wait_ge(summed.sem, summed.at(n, u - 3))
                    copy(ENG[k], turned[:, u % 4, 0:nk], flip[:, u % 2, 0:nk]).then_inc(moved[k].sem, 1)

                def empty(eng, e, s, i, live):
                    for cs, steps, bank, filled, emptied in ((in_chunks, ins, 0, in_filled, in_emptied),
                                                             (out_chunks_, outs, 1, out_filled, out_emptied)):
                        for j, (offset, c) in enumerate(steps):
                            pair = at_step(s, offset, live)
                            if pair is not None and c.engine == e:
                                eng.wait_ge(filled.sem, filled.at(i + pair, j + 1))
                                c.out(proj[:, bank, :]).then_inc(emptied[e].sem, 1)

                @block.gpsimd
                def _(pool):
                    def step(s, i, live):
                        for half, offset in enumerate((-6, 2)):
                            pair = at_step(s, offset, live)
                            if pair is not None:
                                n = i + pair
                                nc.gpsimd.tensor_tensor(pair_mask[:, half, :], head_mask[:, bass.ds(2 * n, 2)], ones[:, 0:2],
                                                        ALU.mult).then_inc(mask_there.sem, 1)
                                pool.wait_ge(mask_there.sem, mask_there.at(n, half + 1))
                                pool.wait_ge(masked.sem, masked.at(n, half))
                                pool.wait_ge(scored.sem, scored.at(n, (half + 1) * U // 2 - U))
                                cols_ = slice(half * HALF, (half + 1) * HALF)
                                for h in range(2):
                                    last = nc.gpsimd.tensor_tensor(qM[:, h, cols_], qT[:, 0, cols_],
                                                                   pair_mask[:, half, h:h + 1].to_broadcast([P, HALF]), ALU.mult)
                                last.then_inc(masked.sem, 1)
                    if masks:
                        through(pool, step)

                def wait_in(eng, n, j):
                    e = in_chunks[j].engine
                    eng.wait_ge(in_emptied[e].sem, in_emptied[e].at(n, emptied_to(in_chunks, j, e)))

                @block.tensor
                def _(pe):
                    def step(s, i, live):
                        pair, u = unit_at(s, 0, live)
                        if pair is not None:
                            n = i + pair
                            if masks and u % (U // 2) == 0:
                                pe.wait_ge(masked.sem, masked.at(n, u // (U // 2) + 1))
                            if ins and u % (U // 2) == 0:
                                wait_in(pe, n, where["q", u // (U // 2)])
                            if ins and u % span == 0:
                                wait_in(pe, n, where["k", u // span])
                            pe.wait_ge(exped.sem, exped.at(n, u + 1 - G))
                            units[u].scores(scores[:, u % G, :]).then_inc(scored.sem, 1)
                        pair, u = unit_at(s, 2, live)
                        if pair is not None:
                            n = i + pair
                            if ipa:
                                pe.wait_ge(rescaled.sem, rescaled.at(n, 2 * u + 2))
                            else:
                                pe.wait_ge(exped.sem, exped.at(n, u + 1))
                            pe.wait_ge(moved[u % 2].sem, moved[u % 2].at(n, u // 2))
                            for j in range(units[u].nk // P):
                                last = nc.tensor.transpose(flip[:, u % 2, j * P:(j + 1) * P], pr[:, u % 4, j * P:(j + 1) * P],
                                                           ident[:, :])
                            last.then_inc(flipped.sem, 1)
                        pair, u = unit_at(s, STORE, live)
                        if pair is not None:
                            n, blocks = i + pair, units[u].nk // P
                            pe.wait_ge(moved[u % 2].sem, moved[u % 2].at(n, u // 2 + 1))
                            if ins and u % span == 0:
                                wait_in(pe, n, where["v", u // span])
                            pe.wait_ge(stored.sem, stored.at(n, u - 1))
                            for j in range(blocks):
                                last = nc.tensor.matmul(weighted[:, u % 2, 0:units[u].width], turned[:, u % 4, j * P:(j + 1) * P],
                                                        units[u].values(j, n), start=(j == 0), stop=(j == blocks - 1))
                            last.then_inc(summed.sem, 1)
                        for j, (offset, c) in enumerate(ins):
                            pair = at_step(s, offset, live)
                            if pair is not None:
                                n = i + pair
                                if j == 0:
                                    pe.wait_ge(slots_in.sem, slots_in.at(n, 1))
                                e = in_chunks[j - 1].engine
                                pe.wait_ge(in_emptied[e].sem, in_emptied[e].at(n, emptied_to(in_chunks, j - 1, e) if j else 0))
                                c.mm(proj[:, 0, :], n).then_inc(in_filled.sem, 1)
                        for j, (offset, c) in enumerate(outs):
                            pair = at_step(s, offset, live)
                            if pair is not None:
                                n = i + pair
                                if c.stored:
                                    pe.wait_ge(stored.sem, stored.at(n, c.stored))
                                for d in sorted({j - 1} | set(c.after)):
                                    e = out_chunks_[d].engine
                                    pe.wait_ge(out_emptied[e].sem, out_emptied[e].at(n, emptied_to(out_chunks_, d, e) if d >= 0 else 0))
                                c.mm(proj[:, 1, :], n).then_inc(out_filled.sem, 1)
                    through(pe, step)

                @block.scalar
                def _(act):
                    def step(s, i, live):
                        if slots:
                            copies, last_reader = slots
                            pair = at_step(s, FIRST, live)
                            if pair is not None:
                                n = i + pair
                                act.wait_ge(in_filled.sem, in_filled.at(n, last_reader + 1 - len(ins)))
                                for dst, src in copies:
                                    last = copy("act", dst, src(n))
                                last.then_inc(slots_in.sem, 1)
                        pair, u = unit_at(s, 0, live)
                        if pair is not None:
                            n, nk = i + pair, units[u].nk
                            act.wait_ge(maxed.sem, maxed.at(n, u + 1))
                            act.wait_ge(flipped.sem, flipped.at(n, u - 3))
                            for k0, k1, c in ((0, nk - IPA, u), (nk - IPA, nk, U + u)) if ipa else ((0, nk, u),):
                                last = nc.scalar.activation(pr[:, u % 4, k0:k1], scores[:, u % G, k0:k1], ACT.Exp,
                                                            bias=negmax[:, c:c + 1], accum_out=rowsum[:, c:c + 1])
                            last.then_inc(exped.sem, 1)
                        pair, u = unit_at(s, 2, live)
                        if pair is not None and u % 2 == 0:
                            move_turned(act, 0, i + pair, u)
                        empty(act, "act", s, i, live)
                    through(act, step)

                @block.vector
                def _(dve):
                    def step(s, i, live):
                        pair, u = unit_at(s, 0, live)
                        if pair is not None:
                            n, nk = i + pair, units[u].nk
                            dve.wait_ge(scored.sem, scored.at(n, u + 1))
                            for k0, k1, c in ((nk - IPA, nk, U + u), (0, nk - IPA, u)) if ipa else ((0, nk, u),):
                                last = nc.vector.tensor_reduce(negmax[:, c:c + 1], scores[:, u % G, k0:k1], AX.X, ALU.max,
                                                               negate=True)
                            last.then_inc(maxed.sem, 1)
                        pair, u = unit_at(s, 1, live)
                        if ipa and pair is not None:
                            n, nk = i + pair, units[u].nk
                            dve.wait_ge(exped.sem, exped.at(n, u + 1))
                            nc.vector.reciprocal(rowinv[:, U + u:U + u + 1],
                                                 rowsum[:, U + u:U + u + 1]).then_inc(rescaled.sem, 1)
                            dve.wait_ge(rescaled.sem, rescaled.at(n, 2 * u + 1))
                            tail_p = pr[:, u % 4, nk - IPA:nk]
                            nc.vector.tensor_scalar(tail_p, tail_p, rowsum[:, u:u + 1], rowinv[:, U + u:U + u + 1], ALU.mult,
                                                    ALU.mult).then_inc(rescaled.sem, 1)
                        pair, u = unit_at(s, 2, live)
                        if pair is not None:
                            n = i + pair
                            dve.wait_ge(exped.sem, exped.at(n, u + 1))
                            nc.vector.reciprocal(rowinv[:, u:u + 1], rowsum[:, u:u + 1]).then_inc(inverted.sem, 1)
                            if u % 2 == 1:
                                move_turned(dve, 1, n, u)
                        pair, u = unit_at(s, STORE, live)
                        if pair is not None:
                            n = i + pair
                            dve.wait_ge(inverted.sem, inverted.at(n, u + 1))
                            dve.wait_ge(summed.sem, summed.at(n, u + 1))
                            units[u].store(weighted[:, u % 2, 0:units[u].width], rowinv[:, u:u + 1], n).then_inc(stored.sem, 1)
                        empty(dve, "dve", s, i, live)
                    through(dve, step)

        def pair_chunks(w_q, w_k, w_v, w_o, qs, keys=None, vals=None, batches=1, kdepth=P, src=xnT):
            K = B // batches
            spanned = M if batches == 1 else batches * N
            gap = U_PAIR // K
            cols_of = lambda n: bass.ds(n * D, D)
            ins = []
            for c in range(2):
                ins.append(((-6, 2)[c], Chunk(ENG[c], lambda o, n, c=c: mm_T(wq[:, :], xnT, c * HALF)(o),
                                              lambda o, c=c: put_heads(ENG[c], o, c, qs)), ("q", c)))
            for c in range(K):
                e, d = ENG[c % 2], kT[:, c * spanned:(c + 1) * spanned]
                f = (lambda o, n, c=c: keys(o, c)) if keys else (
                    lambda o, n, c=c: mm_T(wk[0:kdepth, :], src, c * spanned, k=kdepth)(o))
                ins.append((gap * c - 8, Chunk(e, f, lambda o, e=e, d=d: copy(e, d, o)), ("k", c)))
                e = ENG[1 - c % 2]
                f = (lambda o, n, c=c: vals(o, c, n)) if vals else (
                    lambda o, n, c=c: mm_tok(src, w_v[0:kdepth, cols_of(n)], c * 4, k=kdepth)(o))
                ins.append((gap * c - (5 if K == 4 else 1), Chunk(e, f, lambda o, e=e, c=c: copy(e, V[:, 4 * c:4 * c + 4, :], tiles_of(o))),
                            ("v", c)))
            ins.sort(key=lambda v: v[0])
            where = {name: j for j, (_, _, name) in enumerate(ins)}
            outs = []
            for c in range(2):
                turn = turn_chunk("act", heads_out, 4 * c, outT)
                outs.append(((13, 21)[c], Chunk("act", lambda o, n, f=turn.mm: f(o), turn.out, stored=(c + 1) * U_PAIR // 2)))
                outs.append(((17, 22)[c], Chunk("dve", lambda o, n, c=c: mm_tok(outT, w_o[:, bass.ds(n, 1), :].rearrange("p o d -> p (o d)"),
                                                                                4 * c)(o), add_to(x, 4 * c), after=(2 * c,))))
            return [v[:2] for v in ins], outs, where

        def pair_units(kind, narrow=False):
            us = []
            for t in range(NT):
                b, qt = t // QT, t % QT
                for h in range(2):
                    k0, nk, mk = b * N, N, []
                    if kind == "cross":
                        k0, nk = b * M, M
                    elif kind == "causal":
                        nk, mk = (qt + 1) * P, [block_mask(CAUSAL, qt * P)]
                    elif kind == "near":
                        mk = [block_mask(CAUSAL, P)] if qt == 0 else [block_mask(NOT_BEFORE, 0)]
                    v0 = k0 // P
                    if narrow:
                        own = lambda n, h=h: bass.ds(n * (2 * HS) + h * HS, HS)
                    else:
                        own = lambda n, h=h: pair_rows(h)
                    us.append(Unit(nk, score_mm([(0, nk, qM[:, h, t * P:(t + 1) * P], kT[:, k0:k0 + nk], mk)]),
                                   lambda j, n, v0=v0, own=own: V[:, v0 + j, own(n)],
                                   lambda o, r, n, t=t, own=own: nc.vector.tensor_scalar(heads_out[:, t, own(n)], o, r, None, ALU.mult),
                                   HS if narrow else DH))
            return us

        def setup():
            load([(x[:, :, :], a["x"].rearrange("b (t p) d -> p (b t) d", p=P)),
                  (ctx_tok[:, :, :], a["ctx_768"].rearrange("b (t p) d -> p (b t) d", p=P)),
                  (ident[:, :], a["c_ident"]), (masks[:, :, :], a["c_masks"]), (head_mask[:, :], a["c_head_mask"]),
                  (rot8[:, :], a["c_rot8"])])
            made = signal("consts_made", 4)
            with nc.Block() as block:
                @block.vector
                def _(dve):
                    nc.vector.tensor_copy(ident16[:, :], ident[:, :]).then_inc(made.sem, 1)
                    nc.vector.tensor_copy(masks16[:, :, :], masks[:, :, :]).then_inc(made.sem, 1)
                    nc.vector.memset(ones[:, :], 1.0).then_inc(made.sem, 1)
                    nc.vector.memset(ones16[:, :], 1.0).then_inc(made.sem, 1)
                    dve.wait_ge(made.sem, made.at(0, 4))

            def turn(t):
                def f(o):
                    for q in range(4):
                        last = nc.tensor.transpose(o[0:C, q * P:(q + 1) * P], ctx_tok[:, t + q, :], ident[:, :])
                    return last
                e = ENG[t // 4 % 2]
                return Chunk(e, f, lambda o: copy(e, ctxT[0:C, t * P:(t + 4) * P], o[0:C, :]))
            chunk_block([turn(t) for t in range(0, MT, 4)])

        def l0_attn():
            wanted = ([(wq[:, :], a["L0_attn_W"][:, 0:D]), (wk[:, :], a["L0_attn_W"][:, D:2 * D]),
                  (wv[:, :], a["L0_attn_W"][:, 2 * D:3 * D]),
                  (columns(0), col_of(a["L0_attn_b"][0:D])), (columns(1), col_of(a["L0_attn_b"][D:2 * D])),
                  (brow[0:1, 0:D], row_of(a["L0_attn_b"][2 * D:3 * D]))])
            norm(x, NT, D, z, xnT, loads=wanted)
            attention(self_units(lambda h, t: qT[:, 0, t * P:(t + 1) * P], all_k, lambda h, t, i: V[:, t, :],
                                 add_store, "all", 1, D),
                      head=self_chunks(qs=float(D) ** -0.5, qbias=columns(0), kbias=columns(1), vbias=brow[0:1, 0:D]))

        def l0_xattn():
            sub = ExitStack()
            with sub:
                def sbl(name, shape):
                    return sub.enter_context(nc.sbuf_tensor("lora_" + name, shape, F32))
                low, w_of = {}, {}
                for nm, k in (("q", D), ("k", C), ("v", C)):
                    low[nm] = (sbl(f"{nm}_downT", [RANK, k]), sbl(f"{nm}_up", [RANK, H * DH]), k)
                    w_of[nm] = sbl(f"w_{nm}", [P, H * DH])
                o_downT, o_up, w_o = sbl("o_downT", [RANK, H * DH]), sbl("o_up", [RANK, D]), sbl("w_o", [P, PAIRS, D])
                wki_all, wvi_all, wki = sbl("wk_ipa", [C, H * DH]), sbl("wv_ipa", [C, H * DH]), sbl("wk_ipa_pair", [C, D])
                org, img = sbl("org_ctxT", [C, B, P]), sbl("img_ctxT", [C, B, P])
                wanted = ([(columns(j), a[f"L0_xattn_{nm}_alpha"].rearrange("(p o) -> p o", o=1).to_broadcast([P, 1]))
                      for j, nm in enumerate("qkvo")]
                     + [(low[nm][0][:, :], a[f"L0_xattn_{nm}_downT"]) for nm in "qkv"]
                     + [(low[nm][1][:, :], a[f"L0_xattn_{nm}_up"]) for nm in "qkv"]
                     + [(w_of[nm][0:low[nm][2], :], a[f"L0_xattn_W{nm}"]) for nm in "qkv"]
                     + [(wki_all[:, :], a["L0_xattn_Wk_ipa"]), (wvi_all[:, :], a["L0_xattn_Wv_ipa"]),
                        (o_downT[:, :], a["L0_xattn_o_downT"]),
                        (w_o[:, :, :], a["L0_xattn_Wo"].rearrange("(c p) d -> p c d", p=P))]
                     + [(o_up[:, :], a["L0_xattn_o_up"]), (brow[0:1, 0:D], row_of(a["L0_xattn_bo"]))])
                norm(x, NT, D, z, xnT, loads=wanted, clear=True)
                made = signal("ipa_made", 5)
                last_tiles = ctxT[0:C, :].rearrange("c (b t k) -> c b t k", b=B, t=KT)[:, :, KT - 1, :]
                with nc.Block() as block:
                    @block.vector
                    def _(dve):
                        nc.vector.memset(org[:, :, :], 0.0).then_inc(made.sem, 1)
                        nc.vector.memset(img[:, :, :], 0.0).then_inc(made.sem, 1)
                        dve.wait_ge(made.sem, made.at(0, 2))
                        nc.vector.tensor_copy(org[:, :, 0:P - IPA], last_tiles[:, :, 0:P - IPA]).then_inc(made.sem, 1)
                        nc.vector.tensor_copy(img[:, :, P - IPA:P], last_tiles[:, :, P - IPA:P]).then_inc(made.sem, 1)
                        nc.vector.tensor_scalar(columns(4, 8), columns(0, 4), 1.0 / RANK, None,
                                                ALU.mult).then_inc(made.sem, 1)
                        dve.wait_ge(made.sem, made.at(0, 5))
                chunks = []
                for j, nm in enumerate("qkv"):
                    downT, up, k = low[nm]
                    for c in range(0, H * DH, BANK):
                        chunks.append(Chunk("dve", lambda o, downT=downT, up=up, k=k, c=c: nc.tensor.matmul(
                                                o[0:k, :], downT[:, 0:k], up[:, c:c + BANK], start=True, stop=True),
                                            lambda o, nm=nm, j=j, k=k, c=c: nc.vector.scalar_tensor_tensor(
                                                w_of[nm][0:k, c:c + BANK], o[0:k, :], cols[0:k, 4 + j:5 + j],
                                                w_of[nm][0:k, c:c + BANK], ALU.mult, ALU.add)))
                for c in range(0, PAIRS, 4):
                    def fold_out(o, c=c):
                        for q in range(4):
                            last = nc.tensor.matmul(o[:, q * D:(q + 1) * D], o_downT[:, (c + q) * P:(c + q + 1) * P], o_up[:, :],
                                                    start=True, stop=True)
                        return last
                    chunks.append(Chunk("dve", fold_out, lambda o, c=c: nc.vector.scalar_tensor_tensor(
                        w_o[:, c:c + 4, :], tiles_of(o), columns(7), w_o[:, c:c + 4, :], ALU.mult, ALU.add)))
                chunk_block(chunks)

                def keys(o, b):
                    nc.tensor.matmul(o[:, 0:M - IPA], wk[0:C, :], ctxT[0:C, b * M:(b + 1) * M - IPA], start=True, stop=True)
                    return nc.tensor.matmul(o[:, M - IPA:M], wki[:, :], ctxT[0:C, (b + 1) * M - IPA:(b + 1) * M],
                                            start=True, stop=True)

                def vals(o, b, n):
                    own = bass.ds(n * D, D)
                    for q in range(KT - 1):
                        nc.tensor.matmul(o[:, q * D:(q + 1) * D], ctxT[0:C, b * M + q * P:b * M + (q + 1) * P],
                                         w_of["v"][0:C, own], start=True, stop=True)
                    nc.tensor.matmul(o[:, (KT - 1) * D:KT * D], org[:, b, :], w_of["v"][0:C, own], start=True, stop=False)
                    return nc.tensor.matmul(o[:, (KT - 1) * D:KT * D], img[:, b, :], wvi_all[:, own], start=False, stop=True)
                ins, outs, where = pair_chunks(w_of["q"], w_of["k"], w_of["v"], w_o, DH ** -0.5, keys, vals, kdepth=C, src=ctxT)
                last = max(where[v] for v in where if v[0] != "v")
                slot = lambda w, k: lambda n: w[0:k, bass.ds(n * D, D)]
                streamed(pair_units("cross"), ins, outs, where, ipa=True,
                         slots=([(wq[:, :], slot(w_of["q"], P)), (wk[0:C, :], slot(w_of["k"], C)), (wki[:, :], slot(wki_all, C))],
                                last))
                add_row(x, brow[0:1, 0:D])

        def add_row(acc, row):
            chunk_block([Chunk("dve", (lambda o: [nc.tensor.matmul(o[:, q * D:(q + 1) * D], ones[0:1, :], row, start=True,
                                                                   stop=True) for q in range(4)][-1]), add_to(acc, t))
                         for t in range(0, NT, 4)])

        def l0_ffn():
            sub = ExitStack()
            with sub:
                def sbl(name, shape):
                    return sub.enter_context(nc.sbuf_tensor("gqa_" + name, shape, F32))
                cos, sin = sbl("cos8", [P, N]), sbl("sin8", [P, N])
                gate = sbl("gate_w", [P, EXPERTS])
                sums = sbl("rope_sum", [P, 2, T])
                wanted = ([(wq[:, :], a["L0_ffn_wqT"]), (wk[:, :], a["L0_ffn_wkT"]), (wv[:, :], a["L0_ffn_wvT"]),
                      (wo[:, :], a["L0_ffn_woT"]), (columns(0), col_of(a["L0_ffn_ln1_w"])),
                      (columns(1), col_of(a["L0_ffn_ln2_w"])), (cos[:, :], a["c_cos8"]), (sin[:, :], a["c_sin8"]),
                      (gate[:, :], a["L0_ffn_gate_wT"])])
                norm(x, NT, D, xin, loads=wanted)
                norm(xin, NT, D, z, xnT, rms=True, gain=columns(0))
                chunks = []
                for s, w in ((0, wq), (1, wk)):
                    for c in range(2):
                        chunks.append(Chunk("act", mm_T(w[:, :], xnT, c * HALF),
                                            lambda o, s=s, c=c: copy("act", sums[:, s, c * HALF:(c + 1) * HALF], o,
                                                                     (HS ** -0.5, 1.0)[s])))
                for t in (0, 4):
                    chunks.append(Chunk("dve", mm_tok(xnT, wv[:, :], t), lambda o, t=t: copy("dve", V[:, t:t + 4, :], tiles_of(o))))
                wave = lambda tab: tab[:, :].rearrange("p (o n) -> p o n", o=1).to_broadcast([P, HALF // N, N])
                dsts = (qT[:, 0, :], kT)
                for s in range(2):
                    for c in range(2):
                        chunks.append(Chunk("dve", mm_T(rot8[:, :], sums[:, s, :], c * HALF),
                                            lambda o, s=s, c=c: nc.vector.tensor_tensor(
                                                dsts[s][:, c * HALF:(c + 1) * HALF].rearrange("p (b n) -> p b n", n=N),
                                                o.rearrange("p (b n) -> p b n", n=N), wave(sin), ALU.mult),
                                            after=(2 * s + c,)))
                chunk_block(chunks)
                turned_q = signal("rope_done", 4)
                with nc.Block() as block:
                    @block.vector
                    def _(dve):
                        for s in range(2):
                            v4 = sums[:, s, :].rearrange("p (b n) -> p b n", n=N)
                            nc.vector.tensor_tensor(v4, v4, cos[:, :].rearrange("p (o n) -> p o n", o=1).to_broadcast([P, B, N]),
                                                    ALU.mult).then_inc(turned_q.sem, 1)
                        for s in range(2):
                            dve.wait_ge(turned_q.sem, turned_q.at(0, s + 1))
                            nc.vector.tensor_tensor(dsts[s][:, 0:T], dsts[s][:, 0:T], sums[:, s, :],
                                                    ALU.add).then_inc(turned_q.sem, 1)
                streamed(pair_units("causal", narrow=True), masks=True)
                chunk_block(out_chunks(0, xin, wo[:, :]))
                norm(xin, NT, D, z, xnT, rms=True, gain=columns(1))
                experts(gate)
                add_all(x, xin)

        def add_all(acc, src):
            added = signal("added_all", 1)
            with nc.Block() as block:
                @block.vector
                def _(dve):
                    nc.vector.tensor_tensor(acc[:, :, :], acc[:, :, :], src[:, :, :], ALU.add).then_inc(added.sem, 1)
                    dve.wait_ge(added.sem, added.at(0, 1))

        def experts(gate):
            sub = ExitStack()
            with sub:
                def sbl(name, shape):
                    return sub.enter_context(nc.sbuf_tensor("moe_" + name, shape, F32))
                logit = sbl("logit", [P, NT, EXPERTS])
                prob = sbl("gate_prob", [P, NT, EXPERTS])
                best = sbl("gate_best", [P, NT, 8])
                above = sbl("gate_above", [P, NT, EXPERTS])
                equal = sbl("gate_equal", [P, NT, EXPERTS])
                before = sbl("gate_before", [P, NT, EXPERTS])
                room = sbl("gate_room", [P, NT, 1])
                total = sbl("gate_total", [P, NT, 1])
                share = sbl("gate_share", [P, NT, EXPERTS])
                w13 = sbl("w13", [P, 2, 2 * FFN])
                w2 = sbl("w2", [P, 2, 2, D])
                gated = sbl("gated", [P, 2, T])
                silu = sbl("silu", [P, 2, BANK])
                hT = xnT

                def logits(o):
                    for t in range(NT):
                        last = nc.tensor.matmul(o[:, t * EXPERTS:(t + 1) * EXPERTS], hT[:, t * P:(t + 1) * P], gate[:, :],
                                                start=True, stop=True)
                    return last
                chunk_block([Chunk("dve", logits, lambda o: nc.vector.tensor_copy(
                    logit[:, :, :], o[:, 0:NT * EXPERTS].rearrange("p (t e) -> p t e", e=EXPERTS)))])

                step = signal("gate_step", 64)
                exped = signal("gate_exp", 1)
                with nc.Block() as block:
                    @block.vector
                    def _(dve):
                        done = [0]

                        def then(ins):
                            done[0] += 1
                            ins.then_inc(step.sem, 1)
                            dve.wait_ge(step.sem, step.at(0, done[0]))
                        wide = lambda v: v[:, :, 0:1].to_broadcast([P, NT, EXPERTS])
                        then(nc.vector.tensor_reduce(room[:, :, :], logit[:, :, :], AX.X, ALU.max))
                        then(nc.vector.tensor_tensor(logit[:, :, :], logit[:, :, :], wide(room), ALU.subtract))
                        dve.wait_ge(exped.sem, exped.at(0, 1))
                        then(nc.vector.tensor_reduce(total[:, :, :], prob[:, :, :], AX.X, ALU.add))
                        then(nc.vector.reciprocal(room[:, :, :], total[:, :, :]))
                        then(nc.vector.tensor_tensor(prob[:, :, :], prob[:, :, :], wide(room), ALU.mult))
                        for t in range(NT):
                            then(nc.vector.max(best[:, t, :], prob[:, t, :]))
                        second = best[:, :, 1:2].to_broadcast([P, NT, EXPERTS])
                        then(nc.vector.tensor_tensor(above[:, :, :], prob[:, :, :], second, ALU.is_gt))
                        then(nc.vector.tensor_tensor(equal[:, :, :], prob[:, :, :], second, ALU.is_equal))
                        then(nc.vector.tensor_reduce(room[:, :, :], above[:, :, :], AX.X, ALU.add))
                        then(nc.vector.tensor_scalar(room[:, :, :], room[:, :, :], -1.0, 2.0, ALU.mult, ALU.add))
                        then(nc.vector.memset(before[:, :, 0:1], 0.0))
                        for e in range(1, EXPERTS):
                            then(nc.vector.tensor_tensor(before[:, :, e:e + 1], before[:, :, e - 1:e],
                                                         equal[:, :, e - 1:e], ALU.add))
                        then(nc.vector.tensor_tensor(before[:, :, :], before[:, :, :], wide(room), ALU.is_lt))
                        then(nc.vector.tensor_tensor(equal[:, :, :], equal[:, :, :], before[:, :, :], ALU.mult))
                        then(nc.vector.tensor_tensor(above[:, :, :], above[:, :, :], equal[:, :, :], ALU.add))
                        then(nc.vector.tensor_tensor(share[:, :, :], prob[:, :, :], above[:, :, :], ALU.mult))
                        then(nc.vector.tensor_tensor(total[:, :, :], best[:, :, 0:1], best[:, :, 1:2], ALU.add))
                        then(nc.vector.reciprocal(room[:, :, :], total[:, :, :]))
                        then(nc.vector.tensor_tensor(share[:, :, :], share[:, :, :], wide(room), ALU.mult))

                    @block.scalar
                    def _(act):
                        act.wait_ge(step.sem, step.at(0, 2))
                        nc.scalar.activation(prob[:, :, :], logit[:, :, :], ACT.Exp).then_inc(exped.sem, 1)

                w_in = [signal(f"expert_up_in_{k}", 1, EXPERTS // 2, 16) for k in range(2)]
                w2_in = [signal(f"expert_down_in_{k}", 1, EXPERTS // 2, 16) for k in range(2)]
                up = signal("expert_up", 4, EXPERTS)
                silued = signal("expert_silu", 4, EXPERTS)
                gated_up = signal("expert_gated", 4, EXPERTS)
                down = signal("expert_down", 2, EXPERTS)
                added = signal("expert_added", NT, EXPERTS)
                w13_d, w2_d = a["L0_ffn_w13T"], a["L0_ffn_w2T"]

                def through(eng, half, finish):
                    half(0, 0, (0, 1))
                    with eng.Fori(0, EXPERTS // 2 - 1) as i:
                        half(i, 0, (2, 3))
                        half(i, 1, (0, 1))
                        finish(i, 0)
                        half(i, 1, (2, 3))
                        half(i + 1, 0, (0, 1))
                        finish(i, 1)
                    i = EXPERTS // 2 - 1
                    half(i, 0, (2, 3))
                    half(i, 1, (0, 1))
                    finish(i, 0)
                    half(i, 1, (2, 3))
                    finish(i, 1)

                with ps("gu", [P, 2, 2, BANK]) as gu, ps("eo", [P, 2, BANK]) as eo, \
                        nc.Block() as block:
                    @block.sync
                    def _(sp):
                        def fetch_up(i, k):
                            sp.dma_start(w13[:, k, :], w13_d[:, bass.ds((i * 2 + k) * (2 * FFN), 2 * FFN)]).then_inc(w_in[k].sem, 16)

                        def fetch_down(i, k):
                            sp.dma_start(w2[:, k, :, :], w2_d[:, bass.ds((i * 2 + k) * (2 * D), 2 * D)].rearrange(
                                "p (f d) -> p f d", f=2)).then_inc(w2_in[k].sem, 16)
                        for k in range(2):
                            fetch_up(0, k)
                            fetch_down(0, k)
                        with sp.Fori(0, EXPERTS // 2 - 1) as i:
                            for k in range(2):
                                sp.wait_ge(up.sem, up.at(i * 2 + k, 4))
                                fetch_up(i + 1, k)
                                sp.wait_ge(down.sem, down.at(i * 2 + k, 2))
                                fetch_down(i + 1, k)

                    @block.tensor
                    def _(pe):
                        def half(i, k, cs):
                            e = i * 2 + k
                            for c in cs:
                                f, th = c // 2, c % 2
                                if c == 0:
                                    pe.wait_ge(w_in[k].sem, w_in[k].at(i, 1))
                                pe.wait_ge(gated_up.sem, gated_up.at(e, c - 1))
                                for g in range(2):
                                    last = nc.tensor.matmul(gu[:, c % 2, g, :], w13[:, k, g * FFN + f * P:g * FFN + (f + 1) * P],
                                                            hT[:, th * HALF:(th + 1) * HALF], start=True, stop=True)
                                last.then_inc(up.sem, 1)

                        def finish(i, k):
                            e = i * 2 + k
                            pe.wait_ge(w2_in[k].sem, w2_in[k].at(i, 1))
                            for g in range(2):
                                pe.wait_ge(gated_up.sem, gated_up.at(e, 3 + g))
                                pe.wait_ge(added.sem, added.at(e, 4 * g - 4))
                                for q in range(4):
                                    t = 4 * g + q
                                    for f in range(2):
                                        last = nc.tensor.matmul(eo[:, g, q * D:(q + 1) * D], gated[:, f, t * P:(t + 1) * P],
                                                                w2[:, k, f, :], start=(f == 0), stop=(f == 1))
                                last.then_inc(down.sem, 1)
                        through(pe, half, finish)

                    @block.scalar
                    def _(act):
                        def half(i, k, cs):
                            e = i * 2 + k
                            for c in cs:
                                act.wait_ge(up.sem, up.at(e, c + 1))
                                act.wait_ge(gated_up.sem, gated_up.at(e, c - 1))
                                nc.scalar.activation(silu[:, c % 2, :], gu[:, c % 2, 0, :], ACT.Silu).then_inc(silued.sem, 1)
                        through(act, half, lambda i, k: None)

                    @block.vector
                    def _(dve):
                        def half(i, k, cs):
                            e = i * 2 + k
                            for c in cs:
                                f, th = c // 2, c % 2
                                if f == 0:
                                    dve.wait_ge(down.sem, down.at(e, c - 1))
                                dve.wait_ge(silued.sem, silued.at(e, c + 1))
                                nc.vector.tensor_tensor(gated[:, f, th * HALF:(th + 1) * HALF], silu[:, c % 2, :],
                                                        gu[:, c % 2, 1, :], ALU.mult).then_inc(gated_up.sem, 1)

                        def finish(i, k):
                            e = i * 2 + k
                            for t in range(NT):
                                dve.wait_ge(down.sem, down.at(e, t // 4 + 1))
                                nc.vector.scalar_tensor_tensor(xin[:, t, :], eo[:, t // 4, (t % 4) * D:(t % 4 + 1) * D],
                                                               share[:, t, bass.ds(e, 1)], xin[:, t, :], ALU.mult,
                                                               ALU.add).then_inc(added.sem, 1)
                        through(dve, half, finish)

        def l1_attn():
            w = a["L1_attn_Wqkv"]
            wanted = ([(wq[:, :], w[:, 0:D]), (wk[:, :], w[:, D:2 * D]), (wv[:, :], w[:, 2 * D:3 * D]),
                  (columns(0), col_of(a["L1_attn_bqkv"][0:D])), (columns(1), col_of(a["L1_attn_bqkv"][D:2 * D])),
                  (brow[0:1, 0:D], row_of(a["L1_attn_bqkv"][2 * D:3 * D])),
                  (brow[0:1, D:2 * D], row_of(a["L1_attn_bout"])), (wo[:, :], a["L1_attn_Wout"])])
            norm(x, NT, D, z, xnT, loads=wanted)
            chunk_block(self_chunks(qs=float(D) ** -0.5, qbias=columns(0), kbias=columns(1), vbias=brow[0:1, 0:D]))
            streamed(pair_units("near", narrow=True), masks=True)
            chunk_block(out_chunks(0, x, wo[:, :], bias=brow[0:1, D:2 * D]))

        def context_chunks(qs, qbias=None, kbias=None, vbias=None):
            cs = []
            for c in range(2):
                d = qT[:, 0, c * HALF:(c + 1) * HALF]
                if qbias is None:
                    cs.append(Chunk(ENG[c], mm_T(wq[:, :], xnT, c * HALF), lambda o, c=c, d=d: copy(ENG[c], d, o, qs)))
                else:
                    cs.append(Chunk("dve", mm_T(wq[:, :], xnT, c * HALF),
                                    lambda o, d=d: nc.vector.tensor_scalar(d, o, qbias, qs, ALU.add, ALU.mult)))
            for b in range(B):
                e, d = ENG[b % 2], kT[:, b * M:(b + 1) * M]
                cs.append(Chunk(e, mm_T(wk[0:C, :], ctxT, b * M, k=C),
                                (lambda o, e=e, d=d: copy(e, d, o)) if kbias is None else
                                (lambda o, e=e, d=d: affine(e, d, o, 1.0, kbias))))
            for b in range(B):
                e = ENG[b % 2]
                cs.append(Chunk(e, mm_tok(ctxT, wv[0:C, :], b * KT, k=C, bias=vbias),
                                lambda o, e=e, b=b: copy(e, V[:, b * KT:(b + 1) * KT, :], tiles_of(o))))
            return cs

        def l1_xattn():
            p = lambda s: a["L1_xattn_" + s]
            wanted = ([(wq[:, :], p("wq")), (wk[0:C, :], p("wk")), (wv[0:C, :], p("wv")), (wo[:, :], p("wo")),
                  (columns(0), col_of(p("bq"))), (columns(1), col_of(p("bk"))), (brow[0:1, 0:D], row_of(p("bv"))),
                  (brow[0:1, D:2 * D], row_of(p("bo")))])
            norm(x, NT, D, z, xnT, loads=wanted)
            chunk_block(context_chunks(HS ** -0.5, columns(0), columns(1), brow[0:1, 0:D]))
            streamed(pair_units("cross", narrow=True), masks=True)
            chunk_block(out_chunks(0, x, wo[:, :], bias=brow[0:1, D:2 * D]))

        def l1_ffn():
            wanted = ([(wq[:, :], a["L1_ffn_W_rT"]), (wk[:, :], a["L1_ffn_W_kT"]), (wv[:, :], a["L1_ffn_W_vT"]),
                  (columns(0), col_of(a["L1_ffn_mu_r"])), (columns(1), col_of(a["L1_ffn_mu_k"]))])
            norm(x, NT, D, z, xnT, loads=wanted)
            mixed = signal("mixed", 9)
            prev = V[:, 0:NT, :].rearrange("p t d -> p (t d)").rearrange("p (b n) -> p b n", b=B)
            now = xnT[:, :].rearrange("p (b n) -> p b n", b=B)
            r, k, act_k = qT[:, 0, :], qT[:, 1, :], kT[:, 0:T]
            with nc.Block() as block:
                @block.vector
                def _(dve):
                    nc.vector.memset(prev[:, :, 0:1], 0.0).then_inc(mixed.sem, 1)
                    nc.vector.tensor_copy(prev[:, :, 1:N], now[:, :, 0:N - 1]).then_inc(mixed.sem, 1)
                    nc.vector.tensor_scalar(columns(2, 4), columns(0, 2), -1.0, 1.0, ALU.mult, ALU.add).then_inc(mixed.sem, 1)
                    dve.wait_ge(mixed.sem, mixed.at(0, 3))
                    flat = V[:, 0:NT, :].rearrange("p t d -> p (t d)")
                    nc.vector.tensor_scalar(r, flat, columns(2), None, ALU.mult).then_inc(mixed.sem, 1)
                    nc.vector.tensor_scalar(k, flat, columns(3), None, ALU.mult).then_inc(mixed.sem, 1)
                    dve.wait_ge(mixed.sem, mixed.at(0, 5))
                    nc.vector.scalar_tensor_tensor(r, xnT[:, :], columns(0), r, ALU.mult, ALU.add).then_inc(mixed.sem, 2)
                    nc.vector.scalar_tensor_tensor(k, xnT[:, :], columns(1), k, ALU.mult, ALU.add).then_inc(mixed.sem, 2)
            sig = heads_out
            chunks = []
            for t in (0, 4):
                chunks.append(Chunk("act", mm_tok(r, wq[:, :], t),
                                    lambda o, t=t: nc.scalar.activation(sig[:, t:t + 4, :], tiles_of(o), ACT.Sigmoid)))
            for c in range(2):
                chunks.append(Chunk("dve", mm_T(wk[:, :], k, c * HALF),
                                    lambda o, c=c: nc.vector.tensor_scalar(outT[:, c * HALF:(c + 1) * HALF], o, 0.0, None, ALU.max)))
            chunk_block(chunks)
            squared = signal("squared", 1)
            with nc.Block() as block:
                @block.scalar
                def _(act):
                    nc.scalar.activation(act_k, outT[:, :], ACT.Square).then_inc(squared.sem, 1)
            chunk_block([Chunk("dve", mm_tok(kT, wv[:, :], t),
                               lambda o, t=t: nc.vector.tensor_tensor(z[:, t:t + 4, :], sig[:, t:t + 4, :], tiles_of(o), ALU.mult))
                         for t in (0, 4)])
            add_all(x, z)

        def wide(prefix, names, kdepth, kind, qs, src, bias=None):
            with ExitStack() as sub:
                def sbl(name, shape):
                    return sub.enter_context(nc.sbuf_tensor(prefix + "_" + name, shape, F32))
                w_q, w_k, w_v = sbl("w_q", [P, H * DH]), sbl("w_k", [P, H * DH]), sbl("w_v", [P, H * DH])
                w_o = sbl("w_o", [P, PAIRS, D])
                q_name, k_name, v_name, o_name = names
                wanted = ([(w_q[:, :], a[q_name]), (w_k[0:kdepth, :], a[k_name]), (w_v[0:kdepth, :], a[v_name]),
                      (w_o[:, :, :], a[o_name].rearrange("(c p) d -> p c d", p=P))]
                     + ([(brow[0:1, 0:D], row_of(bias))] if bias is not None else []))
                norm(x, NT, D, z, xnT, loads=wanted, clear=True)
                ins, outs, where = pair_chunks(w_q, w_k, w_v, w_o, qs, batches=1 if kind == "cross" else 2, kdepth=kdepth, src=src)
                last = max(where[v] for v in where if v[0] != "v")
                streamed(pair_units(kind), ins, outs, where,
                         slots=([(wq[:, :], lambda n: w_q[:, bass.ds(n * D, D)]),
                                 (wk[0:kdepth, :], lambda n: w_k[0:kdepth, bass.ds(n * D, D)])], last))
            if bias is not None:
                add_row(x, brow[0:1, 0:D])

        def l2_attn():
            wide("l2", ("L2_attn_QT", "L2_attn_KT", "L2_attn_VT", "L2_attn_OT"), D, "causal", 1.0, xnT)

        def l3_xattn():
            wide("l3", ("L3_xattn_w_q", "L3_xattn_w_k", "L3_xattn_w_v", "L3_xattn_w_out"), C, "cross", DH ** -0.5, ctxT,
                 bias=a["L3_xattn_b_out"])

        def l2_xattn():
            sub = ExitStack()
            with sub:
                def sbl(name, shape, dt=F32):
                    return sub.enter_context(nc.sbuf_tensor("latent_" + name, shape, dt))
                p = lambda s: a["L2_xattn_" + s]
                wlk, wlv = sbl("wlk", [P, D]), sbl("wlv", [P, D])
                ctx_z, ctx_nT = sbl("ctx_z", [P, MT, C]), sbl("ctx_nT", [P, B * M])
                keep8, keep = sbl("keep8", [1, B * M], U8), sbl("keep", [1, B * M], BF16)
                TILES = NT + MT + NT
                raw = sbl("raw_qk", [P, TILES, D])
                squares = sbl("squares", [P, TILES, D])
                norms = sbl("norms", [P, TILES * 2])
                two = lambda v: v.rearrange("(o d) -> o d", o=1)
                wanted = ([(wq[:, :], p("WqT")), (wk[0:C, :], p("WkT")), (wv[0:C, :], p("WvT")), (wlk[:, :], p("WlkT")),
                      (wlv[:, :], p("WlvT")), (wo[:, :], p("WoT")), (cols[0:C, 0:1], col_of(p("ln_x_g"))),
                      (cols[0:C, 1:2], col_of(p("ln_x_b"))), (columns(2), col_of(p("ln_l_g"))),
                      (columns(3), col_of(p("ln_l_b"))), (cols[0:DH, 4:5], col_of(p("qn_g"))),
                      (cols[DH:2 * DH, 4:5], col_of(p("qn_g"))), (cols[0:DH, 5:6], col_of(p("kn_g"))),
                      (cols[DH:2 * DH, 5:6], col_of(p("kn_g"))), (brow[0:1, 0:D], row_of(p("bo"))),
                      (keep8[:, :], a["mask_BxS2_bk0"])])
                norm(x, NT, D, z, loads=wanted, clear=True)
                kept = signal("mask_made", 2)
                with nc.Block() as block:
                    @block.vector
                    def _(dve):
                        nc.vector.tensor_scalar(keep[:, :], keep8[:, :], -1.0, -NEG, ALU.add, ALU.mult).then_inc(kept.sem, 1)
                        nc.vector.tensor_scalar(columns(4), columns(4), DH ** -0.5, None, ALU.mult).then_inc(kept.sem, 1)
                norm(ctx_tok, MT, C, ctx_z, ctx_nT, gain=columns(0), bias=columns(1))
                norm(z, NT, D, heads_out, xnT, gain=columns(2), bias=columns(3))

                k4 = kT[:, :].rearrange("p (b m) -> p b m", b=B)
                chunks = []
                for r in range(0, TILES, 4):
                    if r < NT:
                        mm = mm_tok(xnT, wq[:, :], r)
                    elif r < NT + MT:
                        mm = mm_tok(ctx_nT, wk[0:C, :], r - NT, k=C)
                    else:
                        mm = mm_tok(xnT, wlk[:, :], r - NT - MT)

                    def both(o, r=r):
                        nc.scalar.activation(raw[:, r:r + 4, :], tiles_of(o), ACT.Copy)
                        return nc.scalar.activation(squares[:, r:r + 4, :], tiles_of(o), ACT.Square)
                    chunks.append(Chunk("act", mm, both))
                    if r < NT + MT and r >= NT:
                        b = (r - NT) // KT
                        chunks.append(Chunk("dve", mm_tok(ctx_nT, wv[0:C, :], b * KT, k=C),
                                            lambda o, b=b: copy("dve", V[:, b * KT:(b + 1) * KT, :], tiles_of(o))))
                for t in (0, 4):
                    chunks.append(Chunk("dve", mm_tok(xnT, wlv[:, :], t),
                                        lambda o, t=t: copy("dve", V[:, MT + t:MT + t + 4, :], tiles_of(o))))
                chunk_block(chunks)
                PIECES = 4
                summed = signal("head_squares", PIECES)
                guarded, rooted, inverted = signal("norms_guarded", 1), signal("qk_rooted", 1), signal("qk_inverted", 1)
                scaled = signal("qk_scaled", PIECES)
                groups = TILES * 2 // PIECES
                piece = lambda v, c: v[:, :, :].rearrange("p t d -> p (t d)").rearrange("p (g d) -> p g d", d=DH)[:, c * groups:(c + 1) * groups, :]
                with nc.Block() as block:
                    @block.scalar
                    def _(act):
                        act.wait_ge(guarded.sem, guarded.at(0, 1))
                        nc.scalar.activation(norms[:, :], norms[:, :], ACT.Sqrt).then_inc(rooted.sem, 1)

                    @block.vector
                    def _(dve):
                        for c in range(PIECES):
                            nc.vector.tensor_reduce(norms[:, c * groups:(c + 1) * groups], piece(squares, c), AX.X,
                                                    ALU.add).then_inc(summed.sem, 1)
                        dve.wait_ge(summed.sem, summed.at(0, PIECES))
                        nc.vector.tensor_scalar(norms[:, :], norms[:, :], 1.0 / DH, 1e-16, ALU.mult, ALU.max).then_inc(guarded.sem, 1)
                        dve.wait_ge(rooted.sem, rooted.at(0, 1))
                        nc.vector.reciprocal(norms[:, :], norms[:, :]).then_inc(inverted.sem, 1)
                        dve.wait_ge(inverted.sem, inverted.at(0, 1))
                        for c in range(PIECES):
                            factor = norms[:, c * groups:(c + 1) * groups].rearrange("p (g o) -> p g o", o=1)
                            nc.vector.tensor_tensor(piece(raw, c), piece(raw, c), factor.to_broadcast([P, groups, DH]),
                                                    ALU.mult).then_inc(scaled.sem, 1)
                chunks = []
                for r in range(0, TILES, 4):
                    e = ENG[r // 4 % 2]

                    def put(o, r=r, e=e):
                        if r < NT:
                            for h in range(2):
                                rows = pair_rows(h)
                                last = copy(e, qM[rows, h, r * P:(r + 4) * P], o[rows, :], cols[rows, 4:5])
                            return last
                        if r < NT + MT:
                            return copy(e, k4[:, (r - NT) // KT, 0:M], o, columns(5))
                        b = (r - NT - MT) // QT
                        return copy(e, k4[:, b:b + 2, M:M + N], o.rearrange("p (b n) -> p b n", b=2), columns(5))
                    chunks.append(Chunk(e, turn_chunk(e, raw, r, None).mm, put))
                chunk_block(chunks)
                us = []
                for h in range(2):
                    for b in range(B):
                        for qt in range(QT):
                            t = b * QT + qt
                            q = slot_q(h, t)
                            seg = [(0, M, q, k4[:, b, 0:M], [(ones16[0:1, :], keep[0:1, b * M:(b + 1) * M], 0, M)]),
                                   (M, N, q, k4[:, b, M:M + N], [])]
                            us.append(Unit(M + N, score_mm(seg),
                                           lambda j, i, h=h, b=b: V[:, b * KT + j if j < KT else MT + b * QT + j - KT, pair_rows(h)],
                                           pair_store(h, t), DH))
                attention(us, wide=2)
                chunk_block(out_chunks(0, x, wo[:, :], bias=brow[0:1, 0:D]))

        def l2_ffn():
            sub = ExitStack()
            with sub:
                def sbl(name, shape):
                    return sub.enter_context(nc.sbuf_tensor("fp4_" + name, shape, F32))
                FT = 3
                FP = [P, P, FP4_FFN - 2 * P]
                IN = 2 * FT * D + FP4_FFN + T
                inputs = sbl("inputs", [P, IN])
                w_up = inputs[:, 0:2 * FT * D].rearrange("p (t d) -> p t d", d=D)
                w_down = inputs[:, 2 * FT * D:2 * FT * D + FP4_FFN]
                tokens = inputs[:, 2 * FT * D + FP4_FFN:IN].rearrange("p (t d) -> p t d", d=D)
                wT = sbl("w_upT", [P, 2, FP4_FFN])
                wdT = sbl("w_downT", [P, FT, D])
                hid = sbl("hid", [P, NT, FP4_FFN])
                hidT = sbl("hidT", [P, FT, T])
                silu = sbl("silu", [P, NT, FP4_FFN])
                big = NT * FP4_FFN
                mag, sgn = sbl("mag", [P, big]), sbl("sgn", [P, big])
                amax, inv = sbl("amax", [P, big // FP4_BLOCK]), sbl("amax_inv", [P, big // FP4_BLOCK])
                cleared = signal("fp4_cleared", 1)
                with nc.Block() as block:
                    @block.vector
                    def _(dve):
                        nc.vector.memset(w_up[:, :, :], 0.0).then_inc(cleared.sem, 1)
                        dve.wait_ge(cleared.sem, cleared.at(0, 1))
                pairs = [(w_down[:, :], a["L2_ffn_w_down"])]
                for g, nm in enumerate(("L2_ffn_w_gate", "L2_ffn_w_up")):
                    for f in range(FT):
                        pairs.append((w_up[0:FP[f], g * FT + f, :], a[nm][f * P:f * P + FP[f], :]))
                norm(x, NT, D, tokens, loads=pairs)

                def quantize(v, width):
                    nb = width // FP4_BLOCK
                    blocks = lambda t: t[:, 0:width].rearrange("p (n k) -> p n k", k=FP4_BLOCK)
                    of_block = lambda t: t[:, 0:nb].rearrange("p (n o) -> p n o", o=1).to_broadcast([P, nb, FP4_BLOCK])
                    STEPS = 14
                    step, side = signal("fp4_step", STEPS), signal("fp4_sign", 2)
                    with nc.Block() as block:
                        @block.scalar
                        def _(act):
                            nc.scalar.activation(mag[:, 0:width], v, ACT.Abs).then_inc(side.sem, 1)
                            nc.scalar.activation(sgn[:, 0:width], v, ACT.Sign).then_inc(side.sem, 1)

                        @block.vector
                        def _(dve):
                            done = [0]

                            def then(ins):
                                done[0] += 1
                                ins.then_inc(step.sem, 1)
                                dve.wait_ge(step.sem, step.at(0, done[0]))
                            m = mag[:, 0:width]
                            dve.wait_ge(side.sem, side.at(0, 1))
                            then(nc.vector.tensor_reduce(amax[:, 0:nb], blocks(mag), AX.X, ALU.max))
                            then(nc.vector.tensor_scalar(amax[:, 0:nb], amax[:, 0:nb], 1.0 / 6.0, 1e-12, ALU.mult, ALU.max))
                            then(nc.vector.reciprocal(inv[:, 0:nb], amax[:, 0:nb]))
                            then(nc.vector.tensor_tensor(blocks(mag), blocks(mag), of_block(inv), ALU.mult))
                            dve.wait_ge(side.sem, side.at(0, 2))
                            then(nc.vector.tensor_scalar(v, m, 5.0, 2.0, ALU.is_gt, ALU.mult))
                            then(nc.vector.scalar_tensor_tensor(v, m, 3.5, v, ALU.is_gt, ALU.add))
                            then(nc.vector.scalar_tensor_tensor(v, m, 2.5, v, ALU.is_gt, ALU.add))
                            then(nc.vector.tensor_scalar(v, v, 2.0, None, ALU.mult))
                            for mid in (1.75, 1.25, 0.75, 0.25):
                                then(nc.vector.scalar_tensor_tensor(v, m, mid, v, ALU.is_gt, ALU.add))
                            then(nc.vector.scalar_tensor_tensor(v, v, 0.5, sgn[:, 0:width], ALU.mult, ALU.mult))
                            v3 = v.rearrange("p (n k) -> p n k", k=FP4_BLOCK)
                            then(nc.vector.tensor_tensor(v3, v3, of_block(amax), ALU.mult))
                            assert done[0] == STEPS

                flat = lambda t: t.rearrange("p t d -> p (t d)")
                quantize(inputs[:, :], IN)

                chunks = [turn_chunk("act", tokens, 0, xnT), turn_chunk("dve", tokens, 4, xnT)]

                def turn_rows(g):
                    def f(o):
                        for j in range(FT):
                            last = nc.tensor.transpose(o[:, j * P:j * P + FP[j]], w_up[0:FP[j], g * FT + j, :],
                                                       ident[0:FP[j], 0:FP[j]])
                        return last
                    return Chunk(ENG[g], f, lambda o: copy(ENG[g], wT[:, g, :], o[:, 0:FP4_FFN]))
                chunks += [turn_rows(0), turn_rows(1)]

                def turn_down(j):
                    return Chunk("dve", lambda o: nc.tensor.transpose(o[0:FP[j], 0:D], w_down[:, j * P:j * P + FP[j]], ident[:, :]),
                                 lambda o: copy("dve", wdT[0:FP[j], j, :], o[0:FP[j], 0:D]))
                chunks += [turn_down(j) for j in range(FT)]
                chunk_block(chunks)
                gates, ups = [], []
                for t in range(NT):
                    for g in range(2):
                        mm = lambda o, t=t, g=g: nc.tensor.matmul(o[:, 0:FP4_FFN], xnT[:, t * P:(t + 1) * P], wT[:, g, :],
                                                                  start=True, stop=True)
                        if g == 0:
                            gates.append(Chunk("act", mm, lambda o, t=t: nc.scalar.activation(silu[:, t, :], o[:, 0:FP4_FFN], ACT.Silu)))
                        else:
                            ups.append(Chunk("dve", mm, lambda o, t=t: nc.vector.tensor_tensor(hid[:, t, :], o[:, 0:FP4_FFN], silu[:, t, :], ALU.mult)))
                chunks = ahead_of(gates, ups)
                chunk_block(chunks)
                quantize(flat(hid[:, :, :]), big)
                chunks = []
                for j in range(FT):
                    for t in (0, 4):
                        def turn(o, j=j, t=t):
                            for q in range(4):
                                last = nc.tensor.transpose(o[0:FP[j], q * P:(q + 1) * P], hid[:, t + q, j * P:j * P + FP[j]], ident[:, :])
                            return last
                        e = ENG[t // 4]
                        chunks.append(Chunk(e, turn, lambda o, e=e, j=j, t=t: copy(e, hidT[0:FP[j], j, t * P:(t + 4) * P], o[0:FP[j], :])))
                for t in (0, 4):
                    def downs(o, t=t):
                        for q in range(4):
                            for j in range(FT):
                                last = nc.tensor.matmul(o[:, q * D:(q + 1) * D], hidT[0:FP[j], j, (t + q) * P:(t + q + 1) * P],
                                                        wdT[0:FP[j], j, :], start=(j == 0), stop=(j == FT - 1))
                        return last
                    chunks.append(Chunk("dve", downs, add_to(x, t), after=tuple(range(2 * FT))))
                chunk_block(chunks)

        def l3_attn():
            DQ = 64
            wanted = ([(wq[:, 0:DQ], a["L3_attn_Wq"]), (wk[:, 0:DQ], a["L3_attn_Wk"]), (wv[:, :], a["L3_attn_Wv"])])
            norm(x, NT, D, z, xnT, loads=wanted)
            attention(self_units(lambda h, t: qT[0:DQ, 0, t * P:(t + 1) * P], lambda h, k0, w: kT[0:DQ, k0:k0 + w],
                                 lambda h, t, i: V[:, t, :], add_store, "causal", 1, D),
                      head=self_chunks(qs=float(DQ) ** -0.5, m=DQ))

        def l3_ffn():
            sub = ExitStack()
            with sub:
                def sbl(name, shape, dt=F32):
                    return sub.enter_context(nc.sbuf_tensor("net_" + name, shape, dt))
                p = lambda s: a["L3_ffn_" + s]
                INNER, HALVES = H * DH, H * DH // BANK
                GT = [P, P, GLU - 2 * P]
                NK = WINDOW + P
                raw = sbl("raw_qk", [P, NT, 2, INNER])
                vals = sbl("vals", [P, NT, INNER])
                w_qkv = sbl("w_qkv", [P, 3 * INNER])
                w_out = sbl("w_out", [P, PAIRS, D])
                w1 = sbl("w1", [P, 2 * GLU])
                w2 = sbl("w2", [P, 3, D])
                vec = sbl("layer_cols", [P, 8])
                qk_scale = sbl("qk_scale", [P, DEPTH * 2, DH])
                waves = sbl("waves", [P, QT, 2, 2, DH])
                tables = sbl("tables", [P, QT, 2, 2, DH])
                norms = sbl("qk_norms", [P, NT, 2, H])
                unit = sbl("unit_qk", [P, 4, 2, D])
                turned_cos = sbl("cos_qk", [P, NT, 2, D])
                turned_sin = sbl("sin_qk", [P, 4, 2, D])
                q_slots = sbl("q_slots", [P, 2, T])
                k_rows = sbl("k_rows", [P, T])
                probs0 = sbl("probs_first", [P, 2, 2, P])
                probs1 = sbl("probs_second", [P, 2, 2, 2 * P])
                flat_p = sbl("probs_turned", [P, 4, BANK])
                squares = flat_p
                maxima, sums, inverse = sbl("negmax", [P, NT, 2]), sbl("sums", [P, NT, 2]), sbl("inverse", [P, NT, 2])
                late = sbl("late", [P, 2, P])
                window, window16 = sbl("window", [P, NK]), sbl("window16", [P, NK], BF16)
                heads_T = vals[:, :, :].rearrange("p t d -> p (t d)").rearrange("p (c t) -> p c t", c=PAIRS)
                flat_raw = raw[:, :, :, :].rearrange("p t s d -> p (t s d)")
                acts = flat_raw[:, 0:3 * T].rearrange("p (j t) -> p j t", j=3)
                gelu = flat_raw[:, 3 * T:3 * T + 6 * BANK].rearrange("p (s n) -> p s n", s=6)
                by_batch = lambda v: v.rearrange("p (b n) -> p b n", b=B)
                qkv_in = signal("qkv_weights_in", 1, DEPTH + 1, 16)
                NLOADS = 9
                loaded = signal("layer_loads", NLOADS, DEPTH, 16)
                wanted = ([(waves[:, :, :, :, :], a["c_waves"].rearrange("p t (s w d) -> p t s w d", s=2, w=2)),
                      (late[:, :, :], a["c_late"]), (window[:, :], a["c_window"]),
                      (qk_scale[:, :, :], p("qk_scale").to_broadcast([P, DEPTH * 2 * DH]).rearrange("p (s d) -> p s d", d=DH))])
                norm(x, NT, D, xin, loads=wanted)
                made = signal("window_made", 3)
                with nc.Block() as block:
                    @block.sync
                    def _(sp):
                        sp.dma_start(w_qkv[:, :], p("Wqkv")[0]).then_inc(qkv_in.sem, 16)

                    @block.vector
                    def _(dve):
                        nc.vector.tensor_copy(window16[:, :], window[:, :]).then_inc(made.sem, 1)
                        nc.vector.memset(q_slots[:, :, :], 0.0).then_inc(made.sem, 1)
                        nc.vector.memset(probs1[:, :, :, 0:P - WINDOW], 0.0).then_inc(made.sem, 1)

                with nc.Fori(0, DEPTH) as l:
                    cleared = signal("shift_cleared", 1, DEPTH)
                    turned_in = signal("shift_turned", 2, DEPTH)
                    lower = signal("shift_lower", 2, DEPTH)
                    upper = signal("shift_upper", 2, DEPTH)
                    with ps("bank", [P, 2, BANK]) as bank, nc.Block() as block:
                        @block.tensor
                        def _(pe):
                            pe.wait_ge(qkv_in.sem, qkv_in.at(l, 1))
                            for j in range(2):
                                for q in range(4):
                                    last = nc.tensor.transpose(bank[:, j, q * P:(q + 1) * P], xin[:, 4 * j + q, :], ident[:, :])
                                last.then_inc(turned_in.sem, 1)

                        @block.scalar
                        def _(act):
                            for j in range(2):
                                act.wait_ge(turned_in.sem, turned_in.at(l, j + 1))
                                copy("act", xnT[0:D // 2, j * BANK:(j + 1) * BANK], bank[0:D // 2, j, :]).then_inc(lower.sem, 1)

                        @block.vector
                        def _(dve):
                            up = slice(D // 2, D)
                            nc.vector.memset(by_batch(xnT[up, :])[:, :, 0:1], 0.0).then_inc(cleared.sem, 1)
                            for j in range(2):
                                dve.wait_ge(turned_in.sem, turned_in.at(l, j + 1))
                                copy("dve", by_batch(xnT[up, :])[:, 2 * j:2 * j + 2, 1:N],
                                     bank[up, j, :].rearrange("p (b n) -> p b n", b=2)[:, :, 0:N - 1]).then_inc(upper.sem, 1)

                    project(l, p, raw, w_qkv, squares, norms, waves, tables, qk_scale, loaded, (vec, w1, w2, w_out, GT))
                    local_attention(l, p, loaded, NLOADS, raw, vals, w_qkv, norms, tables, unit, turned_cos, turned_sin, q_slots, k_rows,
                                    probs0, probs1, flat_p, maxima, sums, inverse, window16, qkv_in)

                    chunks = []
                    for c in range(PAIRS):
                        for t in (0, 4):
                            def turn(o, c=c, t=t):
                                for q in range(4):
                                    last = nc.tensor.transpose(o[:, q * P:(q + 1) * P], raw[:, t + q, 0, c * D:(c + 1) * D], ident[:, :])
                                return last
                            e = ENG[t // 4]
                            chunks.append(Chunk(e, turn, lambda o, e=e, c=c, t=t: copy(e, heads_T[:, c, t * P:(t + 4) * P], o)))
                    for t in (0, 4):
                        def outs(o, t=t):
                            for q in range(4):
                                for c in range(PAIRS):
                                    last = nc.tensor.matmul(o[:, q * D:(q + 1) * D], heads_T[:, c, (t + q) * P:(t + q + 1) * P],
                                                            w_out[:, c, :], start=(c == 0), stop=(c == PAIRS - 1))
                            return last
                        chunks.append(Chunk("dve", outs, add_to(xin, t), after=tuple(range(t // 4, 2 * PAIRS, 2))))
                    chunk_block(chunks, n=l, iters=DEPTH, tag="heads_")

                    shifted = signal("late_shifted", 2, DEPTH)
                    moved = signal("late_moved", 3, DEPTH)
                    rowed = signal("late_ones", 1, DEPTH)
                    with ps("bank", [P, 2, BANK]) as bank, nc.Block() as block:
                        @block.sync
                        def _(sp):
                            sp.dma_start(w_qkv[:, :], p("Wqkv")[bass.ds(l + 1, 1), :, :].rearrange("o p c -> p (o c)")).then_inc(qkv_in.sem, 16)

                        @block.gpsimd
                        def _(pool):
                            nc.gpsimd.memset(acts[D // 2:P, 2, :], 1.0).then_inc(rowed.sem, 1)

                        half = D // 2
                        tiles = lambda v, q: v[:, :, half:D].rearrange("p (b q) d -> p b q d", q=QT)[:, :, q, :]
                        late_bank = lambda q: bank[:, q, 0:B * half]

                        @block.tensor
                        def _(pe):
                            nc.tensor.matmul(late_bank(0), late[:, 0, :], tiles(xin, 0), start=True, stop=True).then_inc(shifted.sem, 1)
                            nc.tensor.matmul(late_bank(1), late[:, 0, :], tiles(xin, 1), start=True, stop=False)
                            nc.tensor.matmul(late_bank(1), late[:, 1, :], tiles(xin, 0), start=False, stop=True).then_inc(shifted.sem, 1)

                        @block.scalar
                        def _(act):
                            copy("act", z[:, :, 0:half], xin[:, :, 0:half]).then_inc(moved.sem, 1)

                        @block.vector
                        def _(dve):
                            for q in range(QT):
                                dve.wait_ge(shifted.sem, shifted.at(l, q + 1))
                                copy("dve", tiles(z, q), late_bank(q).rearrange("p (b d) -> p b d", b=B)).then_inc(moved.sem, 1)
                    norm(z, NT, D, z, xnT, gain=vec[:, 0:1], bias=vec[:, 1:2], n=l, iters=DEPTH)
                    gates, values = [], []
                    for j in range(3):
                        g = GT[j]
                        for c in range(2):
                            k, cc = 2 * j + c, slice(c * HALF, (c + 1) * HALF)
                            gates.append(Chunk("act", mm_T(w1[:, GLU + j * P:GLU + j * P + g], xnT, c * HALF, m=g),
                                               lambda o, g=g, j=j, k=k: nc.scalar.activation(gelu[0:g, k, :], o[0:g, :], ACT.Gelu,
                                                                                             bias=vec[0:g, 5 + j:6 + j])))
                            values.append(Chunk("dve", mm_T(w1[:, j * P:j * P + g], xnT, c * HALF, m=g),
                                                lambda o, g=g, j=j, k=k, cc=cc: nc.vector.scalar_tensor_tensor(
                                                    acts[0:g, j, cc], o[0:g, :], vec[0:g, 2 + j:3 + j], gelu[0:g, k, :], ALU.add, ALU.mult)))
                    chunks = ahead_of(gates, values)
                    for t in (0, 4):
                        def downs(o, t=t):
                            for q in range(4):
                                for j in range(3):
                                    k = GT[j] + (j == 2)
                                    last = nc.tensor.matmul(o[:, q * D:(q + 1) * D], acts[0:k, j, (t + q) * P:(t + q + 1) * P],
                                                            w2[0:k, j, :], start=(j == 0), stop=(j == 2))
                            return last
                        chunks.append(Chunk("dve", downs, add_to(xin, t), after=(11,)))
                    chunk_block(chunks, n=l, iters=DEPTH, tag="glu_")
                with nc.Block() as block:
                    @block.sync
                    def _(sp):
                        sp.wait_ge(qkv_in.sem, qkv_in.at(DEPTH, 1))
                add_all(x, xin)

        def project(l, p, raw, w_qkv, squares, norms, waves, tables, qk_scale, loaded, buffers):
            vec, w1, w2, w_out, GT = buffers
            INNER, HALVES = H * DH, H * DH // BANK
            HB = BANK // DH
            BANKS, SLOTS, LAG = 2 * NT, 8, 2
            total = DEPTH * HALVES
            filled = signal("qkv_filled", BANKS, total)
            copied = [signal(f"{nm}_copied", NT, total) for nm in "qk"]
            squared = [signal(f"{nm}_squared", NT, total) for nm in "qk"]
            added = signal("squares_added", 2 * NT, total)
            tabled = signal("tables_made", 6, DEPTH)
            with ps("bank", [P, SLOTS, BANK]) as bank, nc.Block() as block:
                @block.sync
                def _(sp):
                    one = lambda w: w[bass.ds(l, 1), :]
                    sp.dma_start(w_out[:, :, :], p("Wo")[bass.ds(l, 1), :, :].rearrange("o (c p) d -> p (o c) d", p=P)).then_inc(loaded.sem, 16)
                    sp.dma_start(vec[:, 0:1], one(p("ln_g")).rearrange("o d -> d o")).then_inc(loaded.sem, 16)
                    sp.dma_start(vec[:, 1:2], one(p("ln_b")).rearrange("o d -> d o")).then_inc(loaded.sem, 16)
                    sp.dma_start(vec[:, 2:8], p("b1c")[bass.ds(l, 1), :, :].rearrange("o p c -> p (o c)")).then_inc(loaded.sem, 16)
                    sp.dma_start(w2[GT[2]:GT[2] + 1, 2, :], one(p("b2"))).then_inc(loaded.sem, 16)
                    sp.dma_start(w1[:, :], p("W1")[bass.ds(l, 1), :, :].rearrange("o p c -> p (o c)")).then_inc(loaded.sem, 16)
                    for j in range(3):
                        sp.dma_start(w2[0:GT[j], j, :], p("W2")[bass.ds(l, 1), j * P:j * P + GT[j], :].rearrange("o p c -> (o p) c")).then_inc(loaded.sem, 16)

                @block.tensor
                def _(pe):
                    with pe.Fori(0, HALVES) as c:
                        n = l * HALVES + c
                        for j in range(BANKS):
                            pe.wait_ge(copied[j % 2].sem, copied[j % 2].at(n, (j - SLOTS) // 2 + 1))
                            nc.tensor.matmul(bank[:, j % SLOTS, :], xnT[:, j // 2 * P:(j // 2 + 1) * P],
                                             w_qkv[:, bass.ds(c * BANK + (j % 2) * INNER, BANK)],
                                             start=True, stop=True).then_inc(filled.sem, 1)

                def copy_raw(eng, e, kind, n, c, t):
                    eng.wait_ge(filled.sem, filled.at(n, 2 * t + kind + 1))
                    copy(e, raw[:, t, kind, bass.ds(c * BANK, BANK)], bank[:, (2 * t + kind) % SLOTS, :]).then_inc(copied[kind].sem, 1)

                @block.gpsimd
                def _(pool):
                    with pool.Fori(0, HALVES) as c:
                        n = l * HALVES + c
                        for t in range(NT):
                            pool.wait_ge(copied[1].sem, copied[1].at(n, t + 1))
                            pool.wait_ge(added.sem, added.at(n, 2 * t - 2))
                            own = raw[:, t, 1, bass.ds(c * BANK, BANK)]
                            nc.gpsimd.tensor_tensor(squares[:, (2 * t + 1) % 4, :], own, own, ALU.mult).then_inc(squared[1].sem, 1)

                @block.scalar
                def _(act):
                    with act.Fori(0, HALVES) as c:
                        n = l * HALVES + c
                        for t in range(NT):
                            copy_raw(act, "act", 1, n, c, t)
                            act.wait_ge(copied[0].sem, copied[0].at(n, t + 1))
                            act.wait_ge(added.sem, added.at(n, 2 * t - 3))
                            nc.scalar.activation(squares[:, 2 * t % 4, :], raw[:, t, 0, bass.ds(c * BANK, BANK)],
                                                 ACT.Square).then_inc(squared[0].sem, 1)

                @block.vector
                def _(dve):
                    for s in range(2):
                        scale = qk_scale[:, bass.ds(l * 2 + s, 1), :]
                        half = DH // 2
                        nc.vector.tensor_tensor(tables[:, :, s, 0, :], waves[:, :, s, 0, :], scale.to_broadcast([P, QT, DH]),
                                                ALU.mult).then_inc(tabled.sem, 1)
                        for h0, h1 in ((0, half), (half, 0)):
                            nc.vector.tensor_tensor(tables[:, :, s, 1, h0:h0 + half], waves[:, :, s, 1, h0:h0 + half],
                                                    scale[:, :, h1:h1 + half].to_broadcast([P, QT, half]),
                                                    ALU.mult).then_inc(tabled.sem, 1)
                    with dve.Fori(0, HALVES) as c:
                        n = l * HALVES + c
                        for u in range(2 * NT + LAG):
                            if u < 2 * NT and u % 2 == 0:
                                copy_raw(dve, "dve", 0, n, c, u // 2)
                            v = u - LAG
                            if v >= 0:
                                dve.wait_ge(squared[v % 2].sem, squared[v % 2].at(n, v // 2 + 1))
                                nc.vector.tensor_reduce(norms[:, v // 2, v % 2, bass.ds(c * HB, HB)],
                                                        squares[:, v % 4, :].rearrange("p (h d) -> p h d", d=DH), AX.X,
                                                        ALU.add).then_inc(added.sem, 1)

        def local_attention(l, p, loaded, nloads, raw, vals, w_qkv, norms, tables, unit, turned_cos, turned_sin, q_slots, k_rows,
                            probs0, probs1, flat_p, maxima, sums, inverse, window16, qkv_in):
            UNIT, WAVES, ROTATE, TURN, STORE = 9, 8, 7, 4, 4
            total = DEPTH * PAIRS
            HALVES = H * DH // BANK
            NV = NT * HALVES
            v_filled = signal("v_filled", NV, DEPTH)
            v_copied = signal("v_copied", NV, DEPTH)
            guarded = signal("squares_guarded", 1, DEPTH)
            rooted = signal("norms_rooted", 1, DEPTH)
            norms_in = signal("norms_inverted", 1, DEPTH)
            all_norms = norms[:, :, :, :].rearrange("p t s h -> p (t s h)")
            scaled = signal("unit_done", NT, total)
            cosed = signal("cos_done", NT, total)
            sined = signal("sin_done", NT, total)
            rotated = signal("rotated", NT, total)
            qk_turned = signal("qk_turned", B, total)
            qk_moved = signal("qk_moved", B, total)
            scored = signal("tile_scored", NT, total)
            maxed = signal("tile_maxed", NT, total)
            exped = signal("tile_exped", NT, total)
            flipped = signal("tile_flipped", NT, total)
            moved = [signal(f"{nm}_tile_moved", NT // QT, total) for nm in ("first", "second")]
            inverted = signal("tile_inverted", NT, total)
            summed = signal("tile_summed", NT, total)
            stored = signal("tile_stored", NT, total)
            FIRST = -UNIT
            with ExitStack() as inner:
                scores = inner.enter_context(ps("scores", [P, 2, BANK]))
                flip = inner.enter_context(ps("flip", [P, 2, BANK]))
                weighted = inner.enter_context(ps("weighted", [P, 2, BANK]))
                turn = inner.enter_context(ps("turn", [P, 2, BANK]))
                block = inner.enter_context(nc.Block())

                def v_bank(j):
                    return (flip, weighted)[j // 2 % 2][:, j % 2, :]

                def v_tile(j):
                    return j // HALVES, slice(j % HALVES * BANK, (j % HALVES + 1) * BANK)

                def keys_of(g):
                    return P if g % QT == 0 else P + WINDOW

                def score_bank(g):
                    return scores[:, g % 2, 0:2 * keys_of(g)].rearrange("p (h k) -> p h k", h=2)

                def probs_of(g):
                    return (probs0, probs1)[g % QT][:, g // QT % 2, :, :]

                def pair_cols(i, g, width=D, at=0):
                    return bass.ds((i + g // NT) * D + at, width)

                def through(eng, step):
                    for s in range(FIRST, STORE):
                        step(s, l * PAIRS, 0, lambda g: g >= 0)
                    with eng.Fori(0, PAIRS - 2) as i:
                        for s in range(STORE, NT + STORE):
                            step(s, l * PAIRS + i, i, lambda g: True)
                    for s in range(STORE, 2 * NT + STORE):
                        step(s, l * PAIRS + (PAIRS - 2), PAIRS - 2, lambda g: g < 2 * NT)

                def by_head(v, g, slots=4):
                    return v[:, g % slots, :, :].rearrange("p s (h d) -> p s h d", h=2)

                def make_unit(g, i):
                    heads = bass.ds((i + g // NT) * 2, 2)
                    factors = norms[:, g % NT, :, heads].rearrange("p s (h o) -> p s h o", o=1)
                    return nc.vector.tensor_tensor(by_head(unit, g), raw[:, g % NT, :, pair_cols(i, g)].rearrange("p s (h d) -> p s h d", h=2),
                                                   factors.to_broadcast([P, 2, 2, DH]), ALU.mult)

                def move_turned(eng, e, n, g):
                    eng.wait_ge(flipped.sem, flipped.at(n, g + 1))
                    eng.wait_ge(summed.sem, summed.at(n, g - 3))
                    w = (1 + g % QT) * 2 * P
                    copy(e, flat_p[:, g % 4, 0:w], flip[:, g % 2, 0:w]).then_inc(moved[g % QT].sem, 1)

                @block.gpsimd
                def _(pool):
                    def step(s, n, i, live):
                        g = s + ROTATE
                        if live(g):
                            pool.wait_ge(cosed.sem, cosed.at(n, g + 1))
                            pool.wait_ge(sined.sem, sined.at(n, g + 1))
                            both = lambda v, slot: v[:, slot, :, :].rearrange("p s d -> p (s d)")
                            qk = both(turned_cos, g % NT)
                            nc.gpsimd.tensor_tensor(qk, qk, both(turned_sin, g % 4), ALU.add).then_inc(rotated.sem, 1)
                        g = s + WAVES
                        if live(g):
                            pool.wait_ge(scaled.sem, scaled.at(n, g + 1))
                            pool.wait_ge(qk_turned.sem, qk_turned.at(n, (g - NT) // QT + 1))
                            nc.gpsimd.tensor_tensor(by_head(turned_cos, g, NT), by_head(unit, g),
                                                    tables[:, g % QT, :, 0:1, :].to_broadcast([P, 2, 2, DH]),
                                                    ALU.mult).then_inc(cosed.sem, 1)
                    through(pool, step)

                @block.tensor
                def _(pe):
                    for j in range(NV):
                        t, own = v_tile(j)
                        pe.wait_ge(v_copied.sem, v_copied.at(l, j - 3))
                        nc.tensor.matmul(v_bank(j), xnT[:, t * P:(t + 1) * P], w_qkv[:, 2 * H * DH + own.start:2 * H * DH + own.stop],
                                         start=True, stop=True).then_inc(v_filled.sem, 1)

                    def step(s, n, i, live):
                        g = s
                        if live(g):
                            t, nk = g % NT, keys_of(g)
                            pe.wait_ge(qk_moved.sem, qk_moved.at(n, g // QT + 1))
                            pe.wait_ge(exped.sem, exped.at(n, g - 1))
                            bank = score_bank(g)
                            mask = window16[:, (WINDOW + P) - nk:(WINDOW + P)].rearrange("p (o k) -> p o k", o=1).to_broadcast([P, 2, nk])
                            nc.tensor.matmul(bank, ident16[:, :], mask, start=True, stop=False)
                            k0 = (t + 1) * P - nk
                            for h in range(2):
                                last = nc.tensor.matmul(bank[:, h, :], q_slots[:, h, t * P:(t + 1) * P], k_rows[:, k0:k0 + nk],
                                                        start=False, stop=(h == 1))
                            last.then_inc(scored.sem, 1)
                        g = s - 2
                        if live(g):
                            if g == 0:
                                pe.wait_ge(v_copied.sem, v_copied.at(l, NV))
                            pe.wait_ge(exped.sem, exped.at(n, g + 1))
                            pe.wait_ge(moved[g % QT].sem, moved[g % QT].at(n, g // QT))
                            blocks = 1 + g % QT
                            for h in range(2):
                                for j in range(blocks):
                                    last = nc.tensor.transpose(flip[:, g % 2, (h * blocks + j) * P:(h * blocks + j + 1) * P],
                                                               probs_of(g)[:, h, j * P:(j + 1) * P], ident[:, :])
                            last.then_inc(flipped.sem, 1)
                        g = s - STORE
                        if live(g):
                            t, blocks = g % NT, 1 + g % QT
                            pe.wait_ge(moved[g % QT].sem, moved[g % QT].at(n, g // QT + 1))
                            pe.wait_ge(stored.sem, stored.at(n, g - 1))
                            for h in range(2):
                                for j in range(blocks):
                                    last = nc.tensor.matmul(weighted[:, g % 2, h * DH:(h + 1) * DH],
                                                            flat_p[:, g % 4, (h * blocks + j) * P:(h * blocks + j + 1) * P],
                                                            vals[:, t + 1 - blocks + j, pair_cols(i, g, DH, h * DH)],
                                                            start=(j == 0), stop=(j == blocks - 1))
                            last.then_inc(summed.sem, 1)
                        g = s + TURN
                        if g % QT == 0 and live(g):
                            m = g // QT
                            pe.wait_ge(rotated.sem, rotated.at(n, g + 2))
                            pe.wait_ge(qk_moved.sem, qk_moved.at(n, m - 1))
                            for k in range(2):
                                for q in range(QT):
                                    last = nc.tensor.transpose(turn[:, m % 2, (k * QT + q) * P:(k * QT + q + 1) * P],
                                                               turned_cos[:, (g + q) % NT, k, :], ident[:, :])
                            last.then_inc(qk_turned.sem, 1)
                    through(pe, step)

                @block.scalar
                def _(act):
                    def step(s, n, i, live):
                        g = s
                        if live(g):
                            nk = keys_of(g)
                            act.wait_ge(maxed.sem, maxed.at(n, g + 1))
                            act.wait_ge(flipped.sem, flipped.at(n, g - 3))
                            for h in range(2):
                                pr = probs_of(g)[:, h, :]
                                c0 = (1 + g % QT) * P - nk
                                last = nc.scalar.activation(pr[:, c0:c0 + nk], score_bank(g)[:, h, :], ACT.Exp,
                                                            bias=maxima[:, g % NT, h:h + 1], accum_out=sums[:, g % NT, h:h + 1])
                            last.then_inc(exped.sem, 1)
                        g = s + TURN - 1
                        if g % QT == 0 and live(g):
                            m, t = g // QT, g % NT
                            act.wait_ge(qk_turned.sem, qk_turned.at(n, m + 1))
                            cols_ = slice(t * P, (t + QT) * P)
                            for h in range(2):
                                copy("act", q_slots[h * DH:(h + 1) * DH, h, cols_], turn[h * DH:(h + 1) * DH, m % 2, 0:QT * P])
                            copy("act", k_rows[:, cols_], turn[:, m % 2, QT * P:2 * QT * P]).then_inc(qk_moved.sem, 1)
                        g = s - 2
                        if g % QT == 0 and live(g):
                            move_turned(act, "act", n, g)
                    act.wait_ge(guarded.sem, guarded.at(l, 1))
                    nc.scalar.activation(all_norms, all_norms, ACT.Sqrt).then_inc(rooted.sem, 1)
                    for j in range(NV):
                        t, own = v_tile(j)
                        act.wait_ge(v_filled.sem, v_filled.at(l, j + 1))
                        copy("act", vals[:, t, own], v_bank(j)).then_inc(v_copied.sem, 1)
                    through(act, step)

                @block.vector
                def _(dve):
                    def step(s, n, i, live):
                        g = s
                        if live(g):
                            dve.wait_ge(scored.sem, scored.at(n, g + 1))
                            nc.vector.tensor_reduce(maxima[:, g % NT, :], score_bank(g), AX.X, ALU.max,
                                                    negate=True).then_inc(maxed.sem, 1)
                        g = s + UNIT
                        if live(g):
                            dve.wait_ge(cosed.sem, cosed.at(n, g - 3))
                            make_unit(g, i).then_inc(scaled.sem, 1)
                        g = s + WAVES
                        if live(g):
                            dve.wait_ge(scaled.sem, scaled.at(n, g + 1))
                            dve.wait_ge(rotated.sem, rotated.at(n, g - 3))
                            half = DH // 2
                            for d, src in ((0, half), (half, 0)):
                                last = nc.vector.tensor_tensor(
                                    by_head(turned_sin, g)[:, :, :, d:d + half], by_head(unit, g)[:, :, :, src:src + half],
                                    tables[:, g % QT, :, 1:2, d:d + half].to_broadcast([P, 2, 2, half]), ALU.mult)
                            last.then_inc(sined.sem, 1)
                        g = s - 2
                        if live(g):
                            dve.wait_ge(exped.sem, exped.at(n, g + 1))
                            nc.vector.reciprocal(inverse[:, g % NT, :], sums[:, g % NT, :]).then_inc(inverted.sem, 1)
                            if g % QT == 1:
                                move_turned(dve, "dve", n, g)
                        g = s - STORE
                        if live(g):
                            dve.wait_ge(inverted.sem, inverted.at(n, g + 1))
                            dve.wait_ge(summed.sem, summed.at(n, g + 1))
                            nc.vector.tensor_tensor(
                                raw[:, g % NT, 0, pair_cols(i, g)].rearrange("p (h d) -> p h d", h=2),
                                weighted[:, g % 2, 0:D].rearrange("p (h d) -> p h d", h=2),
                                inverse[:, g % NT, :].rearrange("p (h o) -> p h o", o=1).to_broadcast([P, 2, DH]),
                                ALU.mult).then_inc(stored.sem, 1)
                    nc.vector.tensor_scalar(all_norms, all_norms, 1e-24, None, ALU.max).then_inc(guarded.sem, 1)
                    dve.wait_ge(rooted.sem, rooted.at(l, 1))
                    dve.wait_ge(loaded.sem, loaded.at(l, nloads))
                    nc.vector.reciprocal(all_norms, all_norms).then_inc(norms_in.sem, 1)
                    dve.wait_ge(norms_in.sem, norms_in.at(l, 1))
                    through(dve, step)

        def store():
            sent = signal("stored_out", 1, step=16)
            with nc.Block() as block:
                @block.sync
                def _(sp):
                    sp.dma_start(out.rearrange("b (t p) d -> p (b t) d", p=P), x[:, :, :]).then_inc(sent.sem, 16)
                    sp.wait_ge(sent.sem, sent.at(0, 1))

        stages = dict(l0_attn=l0_attn, l0_xattn=l0_xattn, l0_ffn=l0_ffn, l1_attn=l1_attn, l1_xattn=l1_xattn, l1_ffn=l1_ffn,
                      l2_attn=l2_attn, l2_xattn=l2_xattn, l2_ffn=l2_ffn, l3_attn=l3_attn, l3_xattn=l3_xattn, l3_ffn=l3_ffn)
        setup()
        for name in STAGES:
            if name == "l3_ffn":
                early.close()
            stages[name]()
        store()


STAGES = ("l0_attn", "l0_xattn", "l0_ffn", "l1_attn", "l1_xattn", "l1_ffn", "l2_attn", "l2_xattn", "l2_ffn", "l3_attn",
          "l3_xattn", "l3_ffn")


AHEAD = (
    "bank_filled", "bank_emptied_act", "bank_emptied_dve", "measured", "gathered", "eps_added", "rooted",
    "inverted", "normed", "norm_turned", "norm_moved_act", "norm_moved_dve", "scores_ready",
    "max_ready", "probs_ready", "probs_turned", "turned_moved_act", "turned_moved_dve",
    "values_ready", "rowinv_ready", "head_stored", "consts_made", "ipa_made", "rope_done", "added_all",
    "gate_step", "gate_exp", 
    "mixed", "squared", "mask_made", "qk_rooted", "qk_inverted", "qk_scaled", "head_squares", "norms_guarded", "fp4_cleared", "fp4_step",
    "heads_cleared", "window_made", "squares_guarded", "norms_rooted", "norms_inverted", "tables_made",
    "heads_bank_filled", "heads_bank_emptied_act", "heads_bank_emptied_dve", "late_shifted", "late_moved", "late_ones",
    "glu_bank_filled", "glu_bank_emptied_act", "glu_bank_emptied_dve", "shift_cleared", "shift_turned",
    "shift_lower", "shift_upper",
)

STEPS_AHEAD = 16
AHEAD_BY_STEPS = (
    "expert_up", "expert_silu", "expert_gated", "expert_down", "expert_added",
    "qkv_filled", "q_copied", "k_copied", "v_copied", "v_filled", "q_squared", "k_squared", "squares_added", "unit_done", "cos_done", "sin_done",
    "unit_scored", "unit_maxed", "unit_exped", "unit_rescaled", "unit_flipped", "unit_moved_act", "unit_moved_dve",
    "unit_inverted", "unit_summed", "unit_stored", "in_filled", "in_emptied_act", "in_emptied_dve", "out_filled",
    "out_emptied_act", "out_emptied_dve", "slots_copied", "halves_masked", "pair_mask_there",
    "rotated", "qk_turned", "qk_moved", "tile_scored", "tile_maxed", "tile_exped", "tile_flipped", "first_tile_moved", "second_tile_moved",
    "tile_inverted", "tile_summed", "tile_stored",
)


def constants():
    f = np.float32
    i, j = np.arange(P)[:, None], np.arange(P)[None, :]
    keep = np.stack([j <= i, j >= i], 1)
    reach = np.arange(WINDOW + P)[None, :] - WINDOW
    keep_window = (reach <= i) & (reach >= i - WINDOW)

    def rotation(width):
        r, half = np.zeros((P, P), f), width // 2
        for d in range(P):
            if d % width < half:
                r[d + half, d] = -1.0
            else:
                r[d - half, d] = 1.0
        return r

    def angles(width):
        inv = (f(1.0) / f(10000.0) ** (np.arange(0, width, 2, dtype=f) / f(width))).astype(f)
        ang = np.arange(N, dtype=f)[:, None] * inv[None, :]
        return np.concatenate([ang, ang], 1).astype(f)

    a8, a64 = angles(HS), angles(DH)
    half = np.arange(0, DH, 2, dtype=f)
    base = ((half + f(0.4 * DH)) / f(1.4 * DH)).astype(f)
    power = ((np.arange(N, dtype=f) - f(N // 2)) / f(WINDOW // 2)).astype(f)
    scale = (base[None, :] ** power[:, None]).astype(f)
    scale = np.concatenate([scale, scale], 1)
    tile = lambda t: np.ascontiguousarray(np.tile(t.T, (P // t.shape[1], 1))).astype(f)
    sign = np.where(np.arange(DH) < DH // 2, f(-1), f(1))
    waves = np.stack([np.stack([np.cos(a64) * c, np.sin(a64) * c * sign], 1) for c in (scale * f(QK_SCALE), f(1.0) / scale)], 1)
    waves = waves.astype(f).reshape(QT, P, 2 * 2 * DH).transpose(1, 0, 2)
    return {
        "c_ident": np.eye(P, dtype=f),
        "c_masks": np.where(keep, f(0), f(NEG)).astype(f),
        "c_late": np.stack([np.eye(P, k=1, dtype=f), np.eye(P, k=1 - P, dtype=f)], 1),
        "c_window": np.where(keep_window, f(0), f(NEG)).astype(f),
        "c_head_mask": (np.arange(P)[:, None] // HS == np.arange(H)[None, :]).astype(f),
        "c_rot8": rotation(HS),
        "c_cos8": tile(np.cos(a8)), "c_sin8": tile(np.sin(a8)),
        "c_waves": np.ascontiguousarray(waves),
    }


def laid_out(inp):
    g = {k: np.asarray(v) for k, v in inp.items()}
    t = lambda m: np.ascontiguousarray(m.T)
    o = dict(g)
    for nm in "qkvo":
        o[f"L0_xattn_{nm}_downT"] = t(o.pop(f"L0_xattn_{nm}_down"))
    wqkv = o.pop("L0_ffn_wqkv")
    kv = lambda r: t(np.repeat(wqkv[r:r + 32].reshape(4, 1, HS, D), 4, axis=1).reshape(D, D))
    o["L0_ffn_wqT"], o["L0_ffn_wkT"], o["L0_ffn_wvT"] = t(wqkv[0:D]), kv(D), kv(D + 32)
    o["L0_ffn_woT"], o["L0_ffn_gate_wT"] = t(o.pop("L0_ffn_wo")), t(o.pop("L0_ffn_gate_w"))
    o["L0_ffn_w13T"] = np.ascontiguousarray(o.pop("L0_ffn_w13").transpose(2, 0, 1).reshape(D, EXPERTS * 2 * FFN))
    w2 = o.pop("L0_ffn_w2")
    o["L0_ffn_w2T"] = np.ascontiguousarray(w2.transpose(2, 0, 1).reshape(2, P, EXPERTS, D).transpose(1, 2, 0, 3).reshape(P, EXPERTS * 2 * D))
    for nm in "rkv":
        o[f"L1_ffn_W_{nm}T"] = t(o.pop(f"L1_ffn_W_{nm}"))
    for nm in "QKV":
        o[f"L2_attn_{nm}T"] = t(o.pop(f"L2_attn_{nm}").reshape(H * DH, D))
    o["L2_attn_OT"] = t(o.pop("L2_attn_O"))
    wkv, wlkv = o.pop("L2_xattn_Wkv"), o.pop("L2_xattn_Wlkv")
    o["L2_xattn_WkT"], o["L2_xattn_WvT"] = t(wkv[0:D]), t(wkv[D:])
    o["L2_xattn_WlkT"], o["L2_xattn_WlvT"] = t(wlkv[0:D]), t(wlkv[D:])
    o["L2_xattn_WqT"], o["L2_xattn_WoT"] = t(o.pop("L2_xattn_Wq")), t(o.pop("L2_xattn_Wo"))
    wkv = o.pop("L3_xattn_w_kv")
    o["L3_xattn_w_k"], o["L3_xattn_w_v"] = wkv[:, 0:H * DH], wkv[:, H * DH:]
    b1 = o.pop("L3_ffn_b1")
    b1c = np.zeros((DEPTH, P, 6), b1.dtype)
    for h in range(2):
        for j in range(3):
            n = min(P, GLU - j * P)
            b1c[:, 0:n, 3 * h + j] = b1[:, h * GLU + j * P:h * GLU + j * P + n]
    o["L3_ffn_b1c"] = b1c
    o["L3_ffn_Wqkv"] = np.concatenate([o["L3_ffn_Wqkv"], o["L3_ffn_Wqkv"][0:1]])
    o["L3_ffn_qk_scale"] = np.stack([o.pop("L3_ffn_q_scale"), o.pop("L3_ffn_k_scale")], 1).reshape(1, DEPTH * 2 * DH)
    o["mask_BxS2_bk0"] = o["mask_BxS2_bk0"].reshape(1, B * M)
    return o


def kernel(**inputs):
    import concourse.bacc as bacc
    from concourse.bass_utils import run_bass_kernel_spmd

    nc = bacc.Bacc("TRN2", target_bir_lowering=False, num_devices=1)
    arrays, args = {}, {}
    for name, v in {**laid_out(inputs), **constants()}.items():
        v = np.ascontiguousarray(v)
        arrays[f"in_{name}"] = v
        args[name] = nc.dram_tensor(f"in_{name}", v.shape, mybir.dt.from_np(v.dtype), kind="ExternalInput").ap()
    y = nc.dram_tensor("out_0", (B, N, D), F32, kind="ExternalOutput").ap()
    decoder(nc, args, y)
    r = run_bass_kernel_spmd(nc, [arrays], core_ids=[0])
    return r.results[0]["out_0"]
```
